# Optimizing a Trainium2 kernel written in Bass

```python
import numpy as np
import jax
import jax.numpy as jnp

def _softmax(x, axis=-1):
    return jax.nn.softmax(x, axis=axis)

def _gelu(x):
    return jax.nn.gelu(x, approximate=True)

def _silu(x):
    return jax.nn.silu(x)

def _sigmoid(x):
    return jax.nn.sigmoid(x)

def _layernorm(x, axis=-1, eps=1e-05):
    m = jnp.mean(x, axis=axis, keepdims=True)
    v = jnp.var(x, axis=axis, keepdims=True)
    return (x - m) / jnp.sqrt(v + eps)

def _scatter_add(tgt, idx, src, axis=0):
    return tgt.at[idx].add(src)

def _segment_sum(src, seg, n):
    return jax.ops.segment_sum(src, seg, n)
kernel_name = 'mk_xattn_ffn_d2_seqx_r4_66c015'

def setup_inputs(seed: int=0):
    np.random.seed(seed)
    _w = jnp.asarray

    def _rec_inputs():
        import jax
        import jax.numpy as jnp
        _rk = jax.random.key(seed)
        x = 7.22e-05 + 1 * jax.random.normal(jax.random.fold_in(_rk, 1), (2, 1024, 256), jnp.float32)
        _lenS = 1024 - jax.random.randint(jax.random.fold_in(_rk, 7), (2,), 0, max(1, 1024 // 4) + 1, jnp.int32)
        _lenS2 = 77 - jax.random.randint(jax.random.fold_in(_rk, 8), (2,), 0, max(1, 77 // 4) + 1, jnp.int32)
        _ctx_768P = jax.random.normal(jax.random.fold_in(_rk, 11), (2, 16, 192), jnp.float32)
        _ctx_768c = jax.random.dirichlet(jax.random.fold_in(_rk, 511), 0.3 * jnp.ones((16,), jnp.float32), (2, 77))
        _ctx_768t = jnp.einsum('bsk,bkd->bsd', _ctx_768c, _ctx_768P)
        _ctx_768t = _ctx_768t * jax.lax.rsqrt(jnp.mean(jnp.square(_ctx_768t)) + 1e-12) * 0.953939
        ctx_768 = -0.000191848 + 0.999787 * (_ctx_768t + 0.3 * jax.random.normal(jax.random.fold_in(_rk, 611), (2, 77, 192), jnp.float32))
        _validS = jnp.arange(1024)[None, :] < _lenS[:, None]
        _validS2 = jnp.arange(77)[None, :] < _lenS2[:, None]
        _causal = jnp.tril(jnp.ones((1024, 1024), dtype=bool))
        mask_BxS_bf1 = jnp.ones((2, 1024), dtype=bool)
        mask_BxS2_bf1 = jnp.ones((2, 77), dtype=bool)
        return (x, ctx_768, mask_BxS_bf1, mask_BxS2_bf1)
    x, ctx_768, mask_BxS_bf1, mask_BxS2_bf1 = _rec_inputs()

    def _L0_xattn_setup():
        import jax, jax.numpy as jnp
        import numpy as np
        N_HEADS = 16
        key = jax.random.key(seed)
        ks = jax.random.split(key, 8)
        b, l, m = (8, 256, 256)
        d_embed, d_cross = (256, 192)
        s_q = 1.0 / np.sqrt(d_embed)
        s_kv = 1.0 / np.sqrt(d_cross)
        return {'x': jax.random.normal(ks[0], (b, l, d_embed), jnp.float32), 'y': jax.random.normal(ks[1], (b, m, d_cross), jnp.float32), 'Wq': jax.random.normal(ks[2], (d_embed, d_embed), jnp.float32) * s_q, 'bq': jax.random.normal(ks[3], (d_embed,), jnp.float32) * 0.01, 'Wkv': jax.random.normal(ks[4], (2 * d_embed, d_cross), jnp.float32) * s_kv, 'bkv': jax.random.normal(ks[5], (2 * d_embed,), jnp.float32) * 0.01, 'Wo': jax.random.normal(ks[6], (d_embed, d_embed), jnp.float32) * s_q, 'bo': jax.random.normal(ks[7], (d_embed,), jnp.float32) * 0.01}
    _L0_xattn_all = _L0_xattn_setup()
    _L0_xattn_in = {k: v for k, v in _L0_xattn_all.items() if k in ('Wq', 'bq', 'Wkv', 'bkv', 'Wo', 'bo')}
    del _L0_xattn_all

    def _L0_ffn_setup():
        import jax, jax.numpy as jnp
        import numpy as np
        TOP_K = 2
        EPS = 1e-09
        key = jax.random.key(seed)
        ks = jax.random.split(key, 6)
        B, T, D, H, E = (4, 512, 256, 512, 8)
        x = jax.random.normal(ks[0], (B, T, D), dtype=jnp.float32)
        Wg = jax.random.normal(ks[1], (E, D), dtype=jnp.float32) * 0.02
        W1 = jax.random.normal(ks[2], (E, 2 * H, D), dtype=jnp.float32) * 0.02
        b1 = jax.random.normal(ks[3], (E, 2 * H), dtype=jnp.float32) * 0.02
        Wo = jax.random.normal(ks[4], (D, H), dtype=jnp.float32) * 0.02
        bo = jax.random.normal(ks[5], (D,), dtype=jnp.float32) * 0.02
        return {'x': x, 'Wg': Wg, 'W1': W1, 'b1': b1, 'Wo': Wo, 'bo': bo}
    _L0_ffn_all = _L0_ffn_setup()
    _L0_ffn_in = {k: v for k, v in _L0_ffn_all.items() if k in ('Wg', 'W1', 'b1', 'Wo', 'bo')}
    del _L0_ffn_all

    def _L1_xattn_setup():
        import jax, jax.numpy as jnp
        import numpy as np
        B, T, DT, G, DV = (16, 128, 256, 144, 192)
        H, DH = (4, 32)
        INNER = H * DH
        HID = 4 * DT
        N_STATE = 64
        K_TOP = 32

        def layernorm(x, g, b, eps=1e-05):
            m = x.mean(-1, keepdims=True)
            v = x.var(-1, keepdims=True)
            return (x - m) * jax.lax.rsqrt(v + eps) * g + b

        def s4d(x, log_dt, A_re, A_im, C_re, C_im, D_skip):
            Bb, L, D = x.shape
            dt = jnp.exp(log_dt)
            A = A_re + 1j * A_im
            C = C_re + 1j * C_im
            dtA = dt[:, None] * A
            dC = C * (jnp.exp(dtA) - 1.0) / A
            powers = jnp.exp(dtA[:, :, None] * jnp.arange(L))
            K = 2.0 * jnp.einsum('dn,dnl->dl', dC, powers).real
            n = 2 * L
            Kf = jnp.fft.rfft(K, n=n, axis=-1)
            xf = jnp.fft.rfft(x, n=n, axis=1)
            y = jnp.fft.irfft(xf * Kf.T[None], n=n, axis=1)[:, :L]
            return y + x * D_skip
        key = jax.random.key(seed)
        ks = jax.random.split(key, 16)
        s = 0.02
        inp = {'x_text': jax.random.normal(ks[0], (B, T, DT), jnp.float32), 'x_vision': jax.random.normal(ks[1], (B, G, DV), jnp.float32), 'text_mask': jnp.ones((B, T), bool), 'vision_mask': jnp.ones((B, G), bool), 'Wq': jax.random.normal(ks[2], (DT, INNER), jnp.float32) * s, 'Wk': jax.random.normal(ks[3], (DV, INNER), jnp.float32) * s, 'Wv': jax.random.normal(ks[4], (DV, DT), jnp.float32) * s, 'W_film_in': jax.random.normal(ks[5], (DT, 2 * DT), jnp.float32) * s, 'b_film_in': jnp.zeros((2 * DT,), jnp.float32), 'W_film_out': jax.random.normal(ks[6], (DT, 2 * DT), jnp.float32) * s, 'b_film_out': jnp.zeros((2 * DT,), jnp.float32), 'g_norm_in': jnp.ones((DT,), jnp.float32), 'b_norm_in': jnp.zeros((DT,), jnp.float32), 'g_norm_out': jnp.ones((DT,), jnp.float32), 'b_norm_out': jnp.zeros((DT,), jnp.float32), 'g_ffn': jnp.ones((DT,), jnp.float32), 'b_ffn': jnp.zeros((DT,), jnp.float32), 'W1': jax.random.normal(ks[7], (DT, HID), jnp.float32) * s, 'b1': jnp.zeros((HID,), jnp.float32), 'W2': jax.random.normal(ks[8], (HID, DT), jnp.float32) * s, 'b2': jnp.zeros((DT,), jnp.float32), 'log_dt': jnp.log(0.001) + jax.random.uniform(ks[9], (DT,), jnp.float32) * (jnp.log(0.1) - jnp.log(0.001)), 'A_re': -0.5 * jnp.ones((DT, N_STATE), jnp.float32), 'A_im': jnp.tile(jnp.pi * jnp.arange(N_STATE, dtype=jnp.float32), (DT, 1)), 'C_re': jax.random.normal(ks[10], (DT, N_STATE), jnp.float32) * 0.5 ** 0.5, 'C_im': jax.random.normal(ks[11], (DT, N_STATE), jnp.float32) * 0.5 ** 0.5, 'D_skip': jax.random.normal(ks[12], (DT,), jnp.float32), 'mod_gate': jnp.array(0.5, jnp.float32)}
        return inp
    _L1_xattn_all = _L1_xattn_setup()
    _L1_xattn_in = {k: v for k, v in _L1_xattn_all.items() if k in ('Wq', 'Wk', 'Wv', 'W_film_in', 'b_film_in', 'W_film_out', 'b_film_out', 'g_norm_in', 'b_norm_in', 'g_norm_out', 'b_norm_out', 'g_ffn', 'b_ffn', 'W1', 'b1', 'W2', 'b2', 'log_dt', 'A_re', 'A_im', 'C_re', 'C_im', 'D_skip', 'mod_gate')}
    del _L1_xattn_all

    def _L1_ffn_setup():
        import jax, jax.numpy as jnp
        import numpy as np
        EXPERT_NUM = 8
        CAPACITY = 100
        key = jax.random.key(seed)
        k1, k2, k3 = jax.random.split(key, 3)
        B, S, H, E = (8, 512, 256, EXPERT_NUM)
        x = jax.random.normal(k1, (B, S, H), dtype=jnp.float32)
        w_gate = jax.random.normal(k2, (H, E), dtype=jnp.float32) * 0.02
        w_expert = jax.random.normal(k3, (H, H), dtype=jnp.float32) * 0.02
        b_expert = jnp.zeros((H,), dtype=jnp.float32)
        return {'x': x, 'w_gate': w_gate, 'w_expert': w_expert, 'b_expert': b_expert}
    _L1_ffn_all = _L1_ffn_setup()
    _L1_ffn_in = {k: v for k, v in _L1_ffn_all.items() if k in ('w_gate', 'w_expert', 'b_expert')}
    del _L1_ffn_all
    return {'x': x, 'ctx_768': ctx_768, 'mask_BxS_bf1': mask_BxS_bf1, 'mask_BxS2_bf1': mask_BxS2_bf1, 'L0_xattn_Wq': _L0_xattn_in['Wq'], 'L0_xattn_bq': _L0_xattn_in['bq'], 'L0_xattn_Wkv': _L0_xattn_in['Wkv'], 'L0_xattn_bkv': _L0_xattn_in['bkv'], 'L0_xattn_Wo': _L0_xattn_in['Wo'], 'L0_xattn_bo': _L0_xattn_in['bo'], 'L0_ffn_Wg': _L0_ffn_in['Wg'], 'L0_ffn_W1': _L0_ffn_in['W1'], 'L0_ffn_b1': _L0_ffn_in['b1'], 'L0_ffn_Wo': _L0_ffn_in['Wo'], 'L0_ffn_bo': _L0_ffn_in['bo'], 'L1_xattn_Wq': _L1_xattn_in['Wq'], 'L1_xattn_Wk': _L1_xattn_in['Wk'], 'L1_xattn_Wv': _L1_xattn_in['Wv'], 'L1_xattn_W_film_in': _L1_xattn_in['W_film_in'], 'L1_xattn_b_film_in': _L1_xattn_in['b_film_in'], 'L1_xattn_W_film_out': _L1_xattn_in['W_film_out'], 'L1_xattn_b_film_out': _L1_xattn_in['b_film_out'], 'L1_xattn_g_norm_in': _L1_xattn_in['g_norm_in'], 'L1_xattn_b_norm_in': _L1_xattn_in['b_norm_in'], 'L1_xattn_g_norm_out': _L1_xattn_in['g_norm_out'], 'L1_xattn_b_norm_out': _L1_xattn_in['b_norm_out'], 'L1_xattn_g_ffn': _L1_xattn_in['g_ffn'], 'L1_xattn_b_ffn': _L1_xattn_in['b_ffn'], 'L1_xattn_W1': _L1_xattn_in['W1'], 'L1_xattn_b1': _L1_xattn_in['b1'], 'L1_xattn_W2': _L1_xattn_in['W2'], 'L1_xattn_b2': _L1_xattn_in['b2'], 'L1_xattn_log_dt': _L1_xattn_in['log_dt'], 'L1_xattn_A_re': _L1_xattn_in['A_re'], 'L1_xattn_A_im': _L1_xattn_in['A_im'], 'L1_xattn_C_re': _L1_xattn_in['C_re'], 'L1_xattn_C_im': _L1_xattn_in['C_im'], 'L1_xattn_D_skip': _L1_xattn_in['D_skip'], 'L1_xattn_mod_gate': _L1_xattn_in['mod_gate'], 'L1_ffn_w_gate': _L1_ffn_in['w_gate'], 'L1_ffn_w_expert': _L1_ffn_in['w_expert'], 'L1_ffn_b_expert': _L1_ffn_in['b_expert']}

def reference(x, ctx_768, mask_BxS_bf1, mask_BxS2_bf1, L0_xattn_Wq, L0_xattn_bq, L0_xattn_Wkv, L0_xattn_bkv, L0_xattn_Wo, L0_xattn_bo, L0_ffn_Wg, L0_ffn_W1, L0_ffn_b1, L0_ffn_Wo, L0_ffn_bo, L1_xattn_Wq, L1_xattn_Wk, L1_xattn_Wv, L1_xattn_W_film_in, L1_xattn_b_film_in, L1_xattn_W_film_out, L1_xattn_b_film_out, L1_xattn_g_norm_in, L1_xattn_b_norm_in, L1_xattn_g_norm_out, L1_xattn_b_norm_out, L1_xattn_g_ffn, L1_xattn_b_ffn, L1_xattn_W1, L1_xattn_b1, L1_xattn_W2, L1_xattn_b2, L1_xattn_log_dt, L1_xattn_A_re, L1_xattn_A_im, L1_xattn_C_re, L1_xattn_C_im, L1_xattn_D_skip, L1_xattn_mod_gate, L1_ffn_w_gate, L1_ffn_w_expert, L1_ffn_b_expert):
    import jax
    import jax.numpy as jnp

    def _L0_xattn_ref(x, y, Wq, bq, Wkv, bkv, Wo, bo):
        import jax, jax.numpy as jnp
        import numpy as np
        N_HEADS = 16
        b, l, d = x.shape
        m = y.shape[1]
        h = N_HEADS
        dh = d // h
        q = (jnp.einsum('bld,ed->ble', x, Wq) + bq).reshape(b, l, h, dh)
        kv = (jnp.einsum('bmc,ec->bme', y, Wkv) + bkv).reshape(b, m, h, 2 * dh)
        k, v = (kv[..., :dh], kv[..., dh:])
        scale = 1.0 / jnp.sqrt(jnp.asarray(dh, x.dtype))
        att = jax.nn.softmax(jnp.einsum('blhd,bmhd->blmh', q, k) * scale, axis=2)
        out = jnp.einsum('blmh,bmhd->blhd', att, v).reshape(b, l, d)
        return jnp.einsum('bld,ed->ble', out, Wo) + bo

    def _L0_ffn_ref(x, Wg, W1, b1, Wo, bo):
        import jax, jax.numpy as jnp
        import numpy as np
        TOP_K = 2
        EPS = 1e-09
        E = Wg.shape[0]
        gate_logits = jnp.einsum('btd,ed->bte', x, Wg)
        gate_scores = jax.nn.softmax(gate_logits, axis=-1)
        topk_val, topk_idx = jax.lax.top_k(gate_scores, TOP_K)
        topk_val = topk_val / (topk_val.sum(axis=-1, keepdims=True) + EPS)
        comb = (jax.nn.one_hot(topk_idx, E, dtype=x.dtype) * topk_val[..., None]).sum(axis=-2)
        out = jnp.zeros_like(x)
        for e in range(E):
            h = jnp.einsum('btd,hd->bth', x, W1[e]) + b1[e]
            a, b = jnp.split(h, 2, axis=-1)
            g = a * jax.nn.sigmoid(b)
            eo = jnp.einsum('bth,dh->btd', g, Wo) + bo
            out = out + eo * comb[..., e:e + 1]
        return out

    def _L1_xattn_ref(x_text, x_vision, text_mask, vision_mask, Wq, Wk, Wv, W_film_in, b_film_in, W_film_out, b_film_out, g_norm_in, b_norm_in, g_norm_out, b_norm_out, g_ffn, b_ffn, W1, b1, W2, b2, log_dt, A_re, A_im, C_re, C_im, D_skip, mod_gate):
        import jax, jax.numpy as jnp
        import numpy as np
        B, T, DT, G, DV = (16, 128, 256, 144, 192)
        H, DH = (4, 32)
        INNER = H * DH
        HID = 4 * DT
        N_STATE = 64
        K_TOP = 32

        def layernorm(x, g, b, eps=1e-05):
            m = x.mean(-1, keepdims=True)
            v = x.var(-1, keepdims=True)
            return (x - m) * jax.lax.rsqrt(v + eps) * g + b

        def s4d(x, log_dt, A_re, A_im, C_re, C_im, D_skip):
            Bb, L, D = x.shape
            dt = jnp.exp(log_dt)
            A = A_re + 1j * A_im
            C = C_re + 1j * C_im
            dtA = dt[:, None] * A
            dC = C * (jnp.exp(dtA) - 1.0) / A
            powers = jnp.exp(dtA[:, :, None] * jnp.arange(L))
            K = 2.0 * jnp.einsum('dn,dnl->dl', dC, powers).real
            n = 2 * L
            Kf = jnp.fft.rfft(K, n=n, axis=-1)
            xf = jnp.fft.rfft(x, n=n, axis=1)
            y = jnp.fft.irfft(xf * Kf.T[None], n=n, axis=1)[:, :L]
            return y + x * D_skip
        Bb, Tt, D = x_text.shape
        Gg = x_vision.shape[1]
        Q = (x_text @ Wq).reshape(Bb, Tt, H, DH)
        K = (x_vision @ Wk).reshape(Bb, Gg, H, DH)
        scores = jnp.einsum('bthd,bghd->bhtg', Q, K) / np.sqrt(DH).astype(np.float32)
        scores = jnp.where(vision_mask[:, None, None, :], scores, -jnp.inf)
        topv, topi = jax.lax.top_k(scores, K_TOP)
        probs = jax.nn.softmax(topv, axis=-1)
        bi = jnp.arange(Bb)[:, None, None, None]
        hi = jnp.arange(H)[None, :, None, None]
        ti = jnp.arange(Tt)[None, None, :, None]
        attn = jnp.zeros_like(scores).at[bi, hi, ti, topi].set(probs)
        attn_mean = attn.mean(axis=1)
        V = x_vision @ Wv
        c_t = jnp.einsum('btg,bgd->btd', attn_mean, V)
        c_t = c_t * text_mask[..., None]
        x = layernorm(x_text, g_norm_in, b_norm_in)
        scale_in, shift_in = jnp.split(c_t @ W_film_in + b_film_in, 2, axis=-1)
        x = x * (1.0 + mod_gate * scale_in) + mod_gate * shift_in
        y = s4d(x, log_dt, A_re, A_im, C_re, C_im, D_skip)
        scale_out, shift_out = jnp.split(c_t @ W_film_out + b_film_out, 2, axis=-1)
        y = y * (1.0 + mod_gate * scale_out) + mod_gate * shift_out
        xt = x_text + y
        h = layernorm(xt, g_ffn, b_ffn)
        h = jax.nn.gelu(h @ W1 + b1, approximate=False) @ W2 + b2
        xt = xt + h
        return layernorm(xt, g_norm_out, b_norm_out)

    def _L1_ffn_ref(x, w_gate, w_expert, b_expert):
        import jax, jax.numpy as jnp
        import numpy as np
        EXPERT_NUM = 8
        CAPACITY = 100
        B, S, H = x.shape
        E, C = (EXPERT_NUM, CAPACITY)
        hs = x.reshape(-1, H)
        logits = hs @ w_gate
        probs = jax.nn.softmax(logits, axis=1)
        best = jnp.argmax(probs, axis=1)
        mask = jax.nn.one_hot(best, E, dtype=jnp.int32)
        gate = jnp.sum(probs * mask.astype(probs.dtype), axis=1)
        locations = jnp.cumsum(mask, axis=0) - 1
        mask = mask * (locations < C).astype(jnp.int32)
        loc_sum = jnp.sum(locations * mask, axis=1)
        new_gates = gate[:, None] * mask.astype(probs.dtype)
        loc_oh = jax.nn.one_hot(loc_sum, C, dtype=probs.dtype)
        combine = new_gates[:, :, None] * loc_oh[:, None, :]
        dispatch = (combine != 0).astype(hs.dtype)
        dispatched = jnp.einsum('tec,th->ech', dispatch, hs).reshape(E * C, H)
        expert_out = dispatched @ w_expert + b_expert
        combined = combine.reshape(-1, E * C) @ expert_out
        return combined.reshape(B, S, H)
    x = x + _L0_xattn_ref(_layernorm(x, axis=-1), ctx_768, L0_xattn_Wq, L0_xattn_bq, L0_xattn_Wkv, L0_xattn_bkv, L0_xattn_Wo, L0_xattn_bo)
    x = x + _L0_ffn_ref(_layernorm(x, axis=-1), L0_ffn_Wg, L0_ffn_W1, L0_ffn_b1, L0_ffn_Wo, L0_ffn_bo)
    x = x + _L1_xattn_ref(_layernorm(x, axis=-1), ctx_768, mask_BxS_bf1, mask_BxS2_bf1, L1_xattn_Wq, L1_xattn_Wk, L1_xattn_Wv, L1_xattn_W_film_in, L1_xattn_b_film_in, L1_xattn_W_film_out, L1_xattn_b_film_out, L1_xattn_g_norm_in, L1_xattn_b_norm_in, L1_xattn_g_norm_out, L1_xattn_b_norm_out, L1_xattn_g_ffn, L1_xattn_b_ffn, L1_xattn_W1, L1_xattn_b1, L1_xattn_W2, L1_xattn_b2, L1_xattn_log_dt, L1_xattn_A_re, L1_xattn_A_im, L1_xattn_C_re, L1_xattn_C_im, L1_xattn_D_skip, L1_xattn_mod_gate)
    x = x + _L1_ffn_ref(_layernorm(x, axis=-1), L1_ffn_w_gate, L1_ffn_w_expert, L1_ffn_b_expert)
    return x

_drawn_inputs = setup_inputs


def setup_inputs(seed=0):
    import zlib

    import numpy as np

    out = dict(_drawn_inputs(seed))
    spreads = {'L1_xattn_b_film_in': (0.0, 0.1),
     'L1_xattn_b_film_out': (0.0, 0.318),
     'L1_xattn_g_norm_in': (1.0, 0.2),
     'L1_xattn_b_norm_in': (0.0, 0.1),
     'L1_xattn_g_norm_out': (1.0, 0.2),
     'L1_xattn_b_norm_out': (0.0, 0.1),
     'L1_xattn_g_ffn': (1.0, 0.6),
     'L1_xattn_b_ffn': (0.0, 0.8),
     'L1_xattn_b1': (0.0, 0.8),
     'L1_xattn_b2': (0.0, 0.295),
     'L1_xattn_A_re': (-0.5, 0.2),
     'L1_ffn_b_expert': (0.0, 0.8)}
    factors = {'L0_xattn_bq': 8.0,
     'L0_xattn_bkv': 5.758,
     'L0_xattn_bo': 5.609,
     'L0_ffn_b1': 8.0,
     'L0_ffn_bo': 2.874,
     'L1_xattn_Wq': 8.0,
     'L1_xattn_Wk': 8.0,
     'L1_xattn_Wv': 2.778,
     'L1_xattn_W_film_in': 3.377,
     'L1_xattn_W_film_out': 4.671,
     'L1_ffn_w_gate': 3.789,
     'L1_ffn_w_expert': 2.883}
    for name, (base, spread) in spreads.items():
        noise = np.random.default_rng([zlib.crc32(name.encode()), seed]).standard_normal(out[name].shape)
        drawn = base * np.exp(spread * noise) if base else spread * noise
        out[name] = jnp.asarray(drawn.astype(out[name].dtype))
    for name, factor in factors.items():
        out[name] = (out[name] * factor).astype(out[name].dtype)
    return out
```

```python
import math
from contextlib import ExitStack

import concourse.bass as bass
from concourse import mybir

P = 128
NB, L, D = 2, 1024, 256
NT, TB = NB * L // P, L // P
KD = D // P
BLK = 512
NBLK = NB * L // BLK
S2, DC = 77, 192
CC = DC // 2
H0, DH0 = 16, 16
HG = 8
GW = HG * S2
BW = GW // 2
NCH = 5
NE, HID0 = 8, 512
H1, DH1, TOPK = 4, 32, 32
SW = H1 * S2
NS = 64
R = 32
HID1 = 1024
CAP = 100.0
BIAS_ROW = 96
UPE = NBLK * 4
HBUF = 4
CREDIT = 4
HUGE = 1.0e30
TAKEN = -3.0e38
ROUND = 1.5 * 2.0 ** 23
EPS = 1e-5

F32 = mybir.dt.float32
U8 = mybir.dt.uint8
ALU = mybir.AluOpType
ACT = mybir.ActivationFunctionType
AX = mybir.AxisListType.X
ENGINES = ("sync", "scalar", "vector", "gpsimd", "tensor")


class Steps:

    def __init__(self, eng, sem):
        self.eng, self.sem, self.n = eng, sem, 0

    def done(self, ins):
        self.n += 1
        ins.then_inc(self.sem, 1)

    def settle(self):
        self.eng.wait_ge(self.sem, self.n)


def build(nc, d, out, last="F"):
    ctx = ExitStack()
    with ctx:
        def sb(name, shape, dt=F32):
            return ctx.enter_context(nc.sbuf_tensor(name, shape, dt))

        def sem(name):
            return ctx.enter_context(nc.semaphore(name))

        stages = "ABKCDEF"[:"ABKCDEF".index(last) + 1]
        ps = ctx.enter_context(nc.psum_tensor("ps", [P, 8, BLK], F32))

        X = sb("X", [P, NT, D])
        ident = sb("ident", [P, P])
        ones = sb("ones", [P, P])
        tri = sb("tri", [P, P])
        neghalf = sb("neghalf", [P, 8])
        mask16, mask32 = sb("mask16", [P, HG]), sb("mask32", [P, H1])
        desc8 = sb("desc8", [P, 4, NE])
        ramps = sb("ramps", [P, 2, R])
        sgn = sb("sgn", [P, 1])
        halfpi = sb("halfpi", [P, 1])
        wq0, wo0 = sb("wq0", [P, KD, D]), sb("wo0", [P, KD, D])
        wk0, wv0 = sb("wk0", [CC, 2, D]), sb("wv0", [CC, 2, D])
        bias0 = sb("bias0", [P, 3, KD])
        ctxT = sb("ctxT", [CC, 2, NB * S2])
        wg0, wof = sb("wg0", [P, KD, NE]), sb("wof", [P, 4, D])
        wq1, wk1, wv1 = sb("wq1", [P, D]), sb("wk1", [CC, 2, P]), sb("wv1", [CC, 2, D])
        wfilm = sb("wfilm", [P, KD, 2, 2 * D])
        w1, w2 = sb("w1", [P, KD, HID1]), sb("w2", [P, HID1 // P, D])
        b1 = sb("b1", [P, HID1 // P])
        gb_ffn = sb("gb_ffn", [P, 2, KD])
        wx = sb("wx", [P, KD, D + NE])
        rows = sb("rows", [P, 9, D])
        BO0, BOF, GNI, BNI, GNO, BNO, B2, DSKIP, BEXP = range(9)
        mgate = sb("mgate", [P, 1])
        tmask8, vmask8 = sb("tmask8", [P, NT], U8), sb("vmask8", [P, NB, S2], U8)
        bstat = sb("bstat", [P, TB, 6])
        mv = sb("mv", [P, 2 * TB, 2])
        rstd = sb("rstd", [P, 2 * TB])
        arena = sb("arena", [P, 31300])

        class Region:
            def __init__(self, at=0):
                self.at = at

            def take(self, *dims):
                n = math.prod(dims)
                v = arena[:, self.at:self.at + n]
                self.at += n
                assert self.at <= 31300, self.at
                names = "abcd"[:len(dims)]
                if len(dims) > 1:
                    kw = {c: k for c, k in zip(names, dims)}
                    v = v.rearrange(f"p ({' '.join(names)}) -> p {' '.join(names)}", **kw)
                return v

        ra = Region()
        kblk, vblk = ra.take(2, NB, GW), ra.take(2, NB, GW)
        vwo = ra.take(NB, 2 * NCH, D)
        zA, zTA, qT = ra.take(TB, D), ra.take(KD, L), ra.take(2, L)
        Pb, PT = ra.take(4, GW), ra.take(2, NCH * P)
        kvT = ra.take(2, 2, NB * S2)
        mxA, smA = ra.take(4, HG), ra.take(4, HG)
        rb = Region()
        zB, zTB = rb.take(2, 4, D), rb.take(KD, NT * P)
        acc = rb.take(4, NT * P)
        combB = rb.take(2, NT * P)
        w1e = rb.take(2, KD, 2 * HID0)
        b1e = rb.take(2, 8)
        sig, gt, gc = rb.take(2, BLK), rb.take(2, BLK), rb.take(2, BLK)
        lgT = rb.take(BLK)
        combT_v = acc[:, 0, :]
        sm8 = rb.take(12, 4 * NE)
        comb_sum = rb.take(NT)
        rk = Region()
        KS0r, KS0i, KSCr, KSCi = (rk.take(4, D) for _ in range(4))
        KS0n, KSCn = rk.take(D), rk.take(D)
        DF = rk.take(4, L)
        keep_k = rk.at
        Pr, Pi, Qr, Qi = (rk.take(P, R) for _ in range(4))
        tk = [rk.take(R * 32) for _ in range(4)]
        kp = sb("kp", [P, 20, P])
        kl = Region(rk.at - 4 * 32 * R)
        KT, KL = kl.take(R, NS), kl.take(L // P, D)
        tmpD = kp[:].rearrange("p a b -> p (a b)").rearrange("p (a b) -> p a b", b=D)
        rc = Region(keep_k)
        U, XIN = rc.take(NT, D), rc.take(NT, D)
        AT, VW = rc.take(NT * P), rc.take(NB, 2, 2 * D)
        keep_c = rc.at
        uT = rc.take(KD, L)
        wqk = rc.take(KD, NB, SW)
        kb1 = rc.take(NB, SW)
        vT1 = rc.take(KD, NB * S2)
        k1T = rc.take(NB * S2)
        maskb = rc.take(NB, SW)
        tmask = rc.take(NT)
        Sc, Rk, Ex = rc.take(2, SW), rc.take(2, SW), rc.take(2, SW)
        top = rc.take(2, H1, TOPK)
        smC = rc.take(2, 3, H1)
        a77 = rc.take(2, S2)
        xn = rc.take(2, D)
        rd = Region(keep_c)
        DI = rd.take(8, BLK)
        YF = rd.take(4, 4, D)
        XS, pt_ = rd.take(4, D), rd.take(4, D)
        re_ = Region(keep_k + NT * D)
        xnE, xT = re_.take(4, D), re_.take(KD, BLK)
        hT = re_.take(HID1 // P, BLK)
        b1p = re_.take(HID1 // P)
        oE = re_.take(2, D)
        rf = Region()
        zF, zTF = rf.take(4, D), rf.take(KD, BLK)
        yF = rf.take(NT, D)
        lg, oh, fs = rf.take(NT, NE), rf.take(NT, NE), rf.take(8, NT, NE)
        r16 = rf.take(6, NT)

        scr_comb = nc.dram_tensor("scr_comb", [NE, NT * P], F32, kind="Internal").ap()
        scr_k = nc.dram_tensor("scr_k", [L, D], F32, kind="Internal").ap()

        names = """x_in consts_in wA_in wB_in wC_in wE_in rows_in kparam_in dft_in
            own_v own_p own_a stage_end acc_added
            lnA_stats lnA_rstd zA_ready zTA_ps zTA_sb qT_ps qT_sb kv_ps kv_sb kblk_ready vwo_ps vwo_sb
            scores_ready scores_read probs_exp probs_sum probs_norm pt_ps pt_sb oA_ps xA_done xbA
            lnB_stats lnB_rstd zB_ready zTB_ps zTB_sb lgT_ps lgT_sb lgB_ps lgB_exp0 lgB_exp comb_ready
            combT_ps combT_sb comb_out comb_in0 comb_in1 w1e_in0 w1e_in1 h_ps sig_ready h_read g_ready gc_ready
            acc_ready expert_read oB_ps xB_done sB_ready
            kp_exp kp_par kv_arg mag_ready k_trig k_sin k_used k_ps k_sb k_out k_in ks_ps ks_sb ks_done
            lnC_stats lnC_rstd u_ready uT_ps uT_sb lnU_stats lnU_rstd prepC_ps prepC_sb prepC_v sC_ps sC_read
            exC_in exC attn_ready AT_ps AT_sb film_ps xin_ready maskC vw_zero bfilm_in
            dfi_in xf_ps xf_sb xf_read pr_p pr_v yf_ready yd_ps xskip xt_ready
            lnE_stats lnE_rstd zE_ready xTE_ps xTE_sb b1p_ps b1p_sb w1s hE_ps hE_sb oE_ps oE_read
            lnO_stats lnO_rstd oE_ready xE_done
            lnF_stats lnF_rstd zF_ready zTF_ps zTF_sb yF_ps yF_sb lgF lgF_exp oh_ready cum_ps keep_ready
            xF_ready stored""".split()
        s = {n: sem(n) for n in names}

        def load(eng, dst, src, signal):
            eng.dma_start(dst, src).then_inc(s[signal], 16)

        def prow(name):
            return d[name].rearrange("(o d) -> o d", o=1).broadcast_to([P, D])

        def chunked(name, k):
            return d[name].rearrange("(k p) n -> p k n", k=k)

        block = ctx.enter_context(nc.Block())
        ends = {e: 0 for e in ENGINES}

        def stage_end(name, eng):
            ends[name] += 1
            eng.drain().then_inc(s["stage_end"], 1)
            eng.wait_ge(s["stage_end"], len(ENGINES) * ends[name])

        def ln_stats(v, own, src, n, at, signal):
            for j in range(n):
                own.done(v.bn_stats(bstat[:, j, :], src(j)))
            own.settle()
            for j in range(n):
                ins = v.bn_aggr(mv[:, at + j, :], bstat[:, j, :])
            ins.then_inc(s[signal], 1)

        def ln_rstd(p, own, n, at, stats, count, signal):
            p.wait_ge(s[stats], count)
            own.done(p.tensor_scalar(rstd[:, at:at + n], mv[:, at:at + n, 1], EPS, None, ALU.add))
            own.settle()
            p.tensor_tensor(rstd[:, at:at + n], rstd[:, at:at + n], neghalf[:, 0:n], ALU.pow).then_inc(s[signal], 1)

        def normalise(v, dst, src, k):
            return v.tensor_scalar(dst, src, mv[:, k, 0:1], rstd[:, k:k + 1], ALU.subtract, ALU.mult)

        def bank(i, n=BLK):
            return ps[:, i, 0:n]

        def load_expert(eng, e, par):
            load(eng, w1e[:, par, :, :], d["w1t"][bass.ds(e, 1)].rearrange("o (k p) n -> p (o k) n", p=P), f"w1e_in{par}")
            load(eng, b1e[:, par, :], d["b1t"][bass.ds(e, 1)].rearrange("o p n -> p (o n)"), f"w1e_in{par}")
            load(eng, combB[:, par, :], scr_comb[bass.ds(e, 1)].broadcast_to([P, NT * P]), f"w1e_in{par}")

        @block.sync
        def _(sp):
            load(sp, X[:], d["x"].rearrange("b (t p) n -> p (b t) n", p=P), "x_in")
            for dst, name in ((ident, "c_ident"), (tri, "c_tri"), (mask16, "c_mask16"), (mask32, "c_mask32"),
                              (sgn, "c_sgn")):
                load(sp, dst[:], d[name], "consts_in")
            load(sp, desc8[:], d["c_desc8"].rearrange("p (a b) -> p a b", a=4), "consts_in")
            load(sp, ramps[:], d["c_ramps"].rearrange("p (a b) -> p a b", a=2), "consts_in")
            load(sp, wk0[:], chunked("wk0", 2), "wA_in")
            load(sp, wv0[:], chunked("wv0", 2), "wA_in")
            load(sp, ctxT[:], chunked("ctxT", 2), "wA_in")
            load(sp, bias0[:], d["bias0"].rearrange("p (a k) -> p a k", a=3), "wA_in")
            load(sp, wq0[:], chunked("wq0", KD), "wA_in")
            load(sp, wo0[:], chunked("wo0", KD), "wA_in")
            for i, name in enumerate(("L0_xattn_bo", "L0_ffn_bo", "L1_xattn_g_norm_in", "L1_xattn_b_norm_in",
                                      "L1_xattn_g_norm_out", "L1_xattn_b_norm_out", "L1_xattn_b2",
                                      "L1_xattn_D_skip", "L1_ffn_b_expert")):
                load(sp, rows[:, i, :], prow(name), "rows_in")
            load(sp, wg0[:], chunked("wg0", KD), "wB_in")
            load(sp, wof[:], chunked("wof", 4), "wB_in")
            load(sp, wq1[:], d["wq1"], "wC_in")
            load(sp, wk1[:], chunked("L1_xattn_Wk", 2), "wC_in")
            load(sp, wv1[:], chunked("L1_xattn_Wv", 2), "wC_in")
            load(sp, wfilm[:, :, 0, :], chunked("L1_xattn_W_film_in", KD), "wC_in")
            load(sp, wfilm[:, :, 1, :], chunked("L1_xattn_W_film_out", KD), "wC_in")
            load(sp, mgate[:], d["mod_gate"].broadcast_to([P, 1]), "wC_in")
            load(sp, tmask8[:], d["text_mask"], "wC_in")
            load(sp, vmask8[:].rearrange("p b k -> p (b k)"),
                 d["vision_mask"].rearrange("b k -> (b k)").rearrange("(o n) -> o n", o=1).broadcast_to([P, NB * S2]),
                 "wC_in")
            load(sp, w1[:], chunked("L1_xattn_W1", KD), "wE_in")
            load(sp, w2[:], chunked("L1_xattn_W2", HID1 // P), "wE_in")
            load(sp, b1[:], d["b1"], "wE_in")
            load(sp, gb_ffn[:], d["gb_ffn"].rearrange("p (a k) -> p a k", a=2), "wE_in")
            load(sp, wx[:], chunked("wx", KD), "wE_in")
            for i, name in enumerate(("k_are", "k_aim", "k_cre", "k_cim")):
                load(sp, kp[:, i, :], d[name], "kparam_in")
            for h in range(2):
                load(sp, kp[h * NS:(h + 1) * NS, 4, :],
                     d["L1_xattn_log_dt"][h * P:(h + 1) * P].rearrange("(o d) -> o d", o=1).broadcast_to([NS, P]),
                     "kparam_in")
            stage_end("sync", sp)
            if "B" in stages:
                sp.wait_ge(s["combT_sb"], NBLK)
                sp.dma_start(scr_comb, combT_v[0:NE, :]).then_inc(s["comb_out"], 16)
                sp.wait_ge(s["comb_out"], 16)
                for e in range(2):
                    load_expert(sp, e, e)
                with sp.Fori(0, NE // 2 - 1, 1) as pair:
                    for par in range(2):
                        sp.wait_ge(s["gc_ready"], pair * (2 * UPE) + (par + 1) * UPE)
                        load_expert(sp, pair * 2 + (2 + par), par)
                stage_end("sync", sp)
            if "K" in stages:
                load(sp, DF, d["c_dftf"].rearrange("(k p) n -> p k n", p=P), "dft_in")
                sp.wait_ge(s["k_sb"], 8)
                for j in range(4):
                    sp.dma_start(scr_k.rearrange("(a b) n -> a b n", b=R)[:, :, j * NS:(j + 1) * NS],
                                 KT[32 * j:32 * j + 32, :, :]).then_inc(s["k_out"], 16)
                sp.wait_ge(s["k_out"], 64)
                load(sp, KL, scr_k.rearrange("(k p) n -> p k n", p=P), "k_in")
                stage_end("sync", sp)
            if "C" in stages:
                sp.wait_ge(s["vw_zero"], 1)
                for b in range(NB):
                    load(sp, VW[BIAS_ROW:BIAS_ROW + 1, b, :, :].rearrange("p a b -> p (a b)"), d["b_film"], "bfilm_in")
                stage_end("sync", sp)
            if "D" in stages:
                load(sp, DI, d["c_dfti"].rearrange("(k p) n -> p k n", p=P), "dfi_in")
                stage_end("sync", sp)
            if "E" in stages:
                stage_end("sync", sp)
            if "F" in stages:
                for t in range(NT):
                    sp.wait_ge(s["xF_ready"], t + 1)
                    sp.dma_start(out.rearrange("b (t p) n -> p (b t) n", p=P)[:, t, :], X[:, t, :]).then_inc(s["stored"], 16)
                sp.wait_ge(s["stored"], 16 * NT)
            else:
                sp.dma_start(out.rearrange("b (t p) n -> p (b t) n", p=P), X[:]).then_inc(s["stored"], 16)
                sp.wait_ge(s["stored"], 16)

        @block.tensor
        def _(pe):
            def mm(o, l, r, first, final):
                return pe.matmul(o, l, r, start=first, stop=final)

            pe.wait_ge(s["consts_in"], 16 * 7)
            pe.wait_ge(s["wA_in"], 16 * 6)
            for i in range(4):
                w, g = (wk0, wv0)[i // 2], i % 2
                for c in range(2):
                    ins = mm(bank(i, NB * S2), w[:, c, g * P:(g + 1) * P], ctxT[:, c, :], c == 0, c == 1)
                ins.then_inc(s["kv_ps"], 1)
            pe.wait_ge(s["kblk_ready"], 8)
            for b in range(NB):
                for g in range(2):
                    for c in range(NCH):
                        n = (b * 2 + g) * NCH + c
                        m = min(P, GW - c * P)
                        if n >= 4:
                            pe.wait_ge(s["vwo_sb"], n - 3)
                        mm(ps[0:m, 4 + n % 4, 0:D], vblk[:, g, b, c * P:c * P + m], wo0[:, g, :], True, True)\
                            .then_inc(s["vwo_ps"], 1)
            pe.wait_ge(s["vwo_sb"], 4 * NCH)
            for b in range(NB):
                for t in range(TB):
                    n = b * TB + t
                    pe.wait_ge(s["zA_ready"], n + 1)
                    if n >= 2:
                        pe.wait_ge(s["zTA_sb"], n - 1)
                    for k in range(KD):
                        ins = pe.transpose(ps[:, 6 + n % 2, k * P:(k + 1) * P], zA[:, t, k * P:(k + 1) * P], ident[:])
                    ins.then_inc(s["zTA_ps"], 1)
                pe.wait_ge(s["zTA_sb"], (b + 1) * TB)
                for h in range(2):
                    for g in range(2):
                        n = (b * 2 + h) * 2 + g
                        if n % 4 >= 2:
                            pe.wait_ge(s["qT_sb"], n - 1)
                        for k in range(KD):
                            ins = mm(bank(6 + n % 2), wq0[:, k, g * P:(g + 1) * P], zTA[:, k, h * BLK:(h + 1) * BLK],
                                     k == 0, k == KD - 1)
                        ins.then_inc(s["qT_ps"], 1)
                pe.wait_ge(s["qT_sb"], (b + 1) * 4)
                NU = 2 * TB
                for step in range(NU + 3):
                    if step < NU:
                        u, t, g = b * NU + step, step // 2, step % 2
                        if u >= 2:
                            pe.wait_ge(s["scores_read"], u - 1)
                        for c in range(2):
                            ins = mm(ps[:, 2 * (u % 2) + c, 0:BW], qT[:, g, t * P:(t + 1) * P],
                                     kblk[:, g, b, c * BW:(c + 1) * BW], True, True)
                        ins.then_inc(s["scores_ready"], 1)
                    if 0 <= step - 2 < NU:
                        u = b * NU + step - 2
                        pe.wait_ge(s["probs_norm"], u + 1)
                        if u >= 1:
                            pe.wait_ge(s["pt_sb"], u)
                        for c in range(NCH):
                            m = min(P, GW - c * P)
                            ins = pe.transpose(ps[0:m, 4 + c // 4, (c % 4) * P:(c % 4) * P + P],
                                               Pb[:, u % 4, c * P:c * P + m], ident[:])
                        ins.then_inc(s["pt_ps"], 1)
                    if 0 <= step - 3 < NU:
                        u = b * NU + step - 3
                        g, T = (step - 3) % 2, u // 2
                        pe.wait_ge(s["pt_sb"], u + 1)
                        if g == 0 and T >= 2:
                            pe.wait_ge(s["xA_done"], T - 1)
                        for c in range(NCH):
                            m = min(P, GW - c * P)
                            ins = mm(ps[:, 6 + T % 2, 0:D], PT[0:m, u % 2, c * P:(c + 1) * P], vwo[0:m, b, g * NCH + c, :],
                                     g == 0 and c == 0, g == 1 and c == NCH - 1)
                        ins.then_inc(s["oA_ps"], 1)
            stage_end("tensor", pe)
            if "B" in stages:
                pe.wait_ge(s["wB_in"], 32)
                for i in range(NBLK):
                    for t in range(4):
                        n = i * 4 + t
                        pe.wait_ge(s["zB_ready"], n + 1)
                        if n >= 2:
                            pe.wait_ge(s["zTB_sb"], n - 1)
                        for k in range(KD):
                            ins = pe.transpose(ps[:, n % 2, k * P:(k + 1) * P], zB[:, i % 2, t, k * P:(k + 1) * P], ident[:])
                        ins.then_inc(s["zTB_ps"], 1)
                    pe.wait_ge(s["zTB_sb"], 4 * i + 4)
                    if i:
                        pe.wait_ge(s["lgB_exp0"], i)
                    for t in range(4):
                        for k in range(KD):
                            ins = mm(ps[:, 2, t * NE:(t + 1) * NE], zTB[:, k, (i * 4 + t) * P:(i * 4 + t + 1) * P], wg0[:, k, :],
                                     k == 0, k == KD - 1)
                    ins.then_inc(s["lgB_ps"], 1)
                    pe.wait_ge(s["comb_ready"], i + 1)
                    if i:
                        pe.wait_ge(s["combT_sb"], i)
                    for t in range(4):
                        ins = pe.transpose(ps[0:NE, 3, t * P:(t + 1) * P], sm8[:, 11, t * NE:(t + 1) * NE], ident[:])
                    ins.then_inc(s["combT_ps"], 1)
                pe.wait_ge(s["combT_sb"], NBLK)
                with pe.Fori(0, NE // 2, 1) as pair:
                    for par in range(2):
                        pe.wait_ge(s[f"w1e_in{par}"], pair * 48 + 48)
                        for n in range(UPE):
                            w, i, f = par * UPE + n, n // 4, n % 4
                            pe.wait_ge(s["g_ready"], pair * (2 * UPE) + (w + 1 + CREDIT - HBUF))
                            for half in range(2):
                                for k in range(KD):
                                    ins = mm(bank(2 * (w % HBUF) + half),
                                             w1e[:, par, k, half * HID0 + f * P:half * HID0 + (f + 1) * P],
                                             zTB[:, k, i * BLK:(i + 1) * BLK], k == 0, k == KD - 1)
                            ins.then_inc(s["h_ps"], 1)
                pe.wait_ge(s["acc_ready"], 1)
                for T in range(NT):
                    if T >= 2:
                        pe.wait_ge(s["xB_done"], T - 1)
                    for f in range(4):
                        ins = mm(ps[:, 6 + T % 2, 0:D], acc[:, f, T * P:(T + 1) * P], wof[:, f, :], f == 0, f == 3)
                    ins.then_inc(s["oB_ps"], 1)
                stage_end("tensor", pe)
            if "K" in stages:
                pe.wait_ge(s["k_used"], 8)
                for q in range(4):
                    for h in range(2):
                        for c16 in range(16):
                            for jj in range(2):
                                j, sl = 2 * h + jj, q * 16 + c16
                                chan = jj * NS + sl
                                o = ps[32 * j:32 * j + 32, 4 * h + q, c16 * R:(c16 + 1) * R]
                                rowsl = slice(64 * h, 64 * h + 64)
                                mm(o, Pr[rowsl, chan, :], Qr[rowsl, chan, :], True, False)
                                ins = mm(o, Pi[rowsl, chan, :], Qi[rowsl, chan, :], False, True)
                        ins.then_inc(s["k_ps"], 1)
                pe.wait_ge(s["k_in"], 16)
                pe.wait_ge(s["dft_in"], 16)
                for m in range(8):
                    if m >= 4:
                        pe.wait_ge(s["ks_done"], m - 3)
                    for k in range(4):
                        ins = mm(bank(m % 4), DF[:, k, m * P:(m + 1) * P],
                                 KL.rearrange("p (j k) n -> p j k n", j=2)[:, :, k, :], k == 0, k == 3)
                    ins.then_inc(s["ks_ps"], 1)
                stage_end("tensor", pe)
            if "C" in stages:
                pe.wait_ge(s["wC_in"], 16 * 8)
                for c in range(2):
                    ins = mm(bank(0, NB * S2), wk1[:, c, :], ctxT[:, c, :], c == 0, c == 1)
                ins.then_inc(s["prepC_ps"], 1)
                for g in range(2):
                    for c in range(2):
                        ins = mm(bank(1 + g, NB * S2), wv1[:, c, g * P:(g + 1) * P], ctxT[:, c, :], c == 0, c == 1)
                    ins.then_inc(s["prepC_ps"], 1)
                pe.wait_ge(s["prepC_v"], 2)
                for b in range(NB):
                    for g in range(2):
                        mm(bank(4 + 2 * b + g, SW), wq1[:, g * P:(g + 1) * P], kb1[:, b, :], True, True)\
                            .then_inc(s["prepC_ps"], 1)
                pe.wait_ge(s["prepC_sb"], 7)
                for b in range(NB):
                    for io in range(2):
                        for g in range(2):
                            ins = mm(ps[0:S2, 2 * b + io, :], vT1[:, g, b * S2:(b + 1) * S2], wfilm[:, g, io, :], g == 0, g == 1)
                        ins.then_inc(s["prepC_ps"], 1)
                pe.wait_ge(s["prepC_v"], 6)
                for b in range(NB):
                    for t in range(TB):
                        n = b * TB + t
                        pe.wait_ge(s["u_ready"], n + 1)
                        if n >= 2:
                            pe.wait_ge(s["uT_sb"], n - 1)
                        for k in range(KD):
                            ins = pe.transpose(ps[:, n % 2, k * P:(k + 1) * P], U[:, n, k * P:(k + 1) * P], ident[:])
                        ins.then_inc(s["uT_ps"], 1)
                    for step in range(TB + 1):
                        if step < TB:
                            n, t = b * TB + step, step
                            pe.wait_ge(s["uT_sb"], n + 1)
                            if n >= 2:
                                pe.wait_ge(s["sC_read"], n - 1)
                            for k in range(KD):
                                ins = mm(bank(2 + n % 2, SW), uT[:, k, t * P:(t + 1) * P], wqk[:, k, b, :], k == 0, k == KD - 1)
                            ins.then_inc(s["sC_ps"], 1)
                        if step >= 1:
                            n = b * TB + step - 1
                            pe.wait_ge(s["attn_ready"], n + 1)
                            if n:
                                pe.wait_ge(s["AT_sb"], n)
                            pe.transpose(ps[0:S2, 4, 0:P], a77[:, n % 2, :], ident[:]).then_inc(s["AT_ps"], 1)
                            pe.wait_ge(s["AT_sb"], n + 1)
                            if n >= 2:
                                pe.wait_ge(s["xin_ready"], n - 1)
                            mm(bank(6 + n % 2), AT[0:BIAS_ROW + 1, n * P:(n + 1) * P], VW[0:BIAS_ROW + 1, b, 0, :], True, True)\
                                .then_inc(s["film_ps"], 1)
                stage_end("tensor", pe)
            if "D" in stages:
                for b in range(NB):
                    for m in range(4):
                        n = b * 4 + m
                        if n:
                            pe.wait_ge(s["xf_sb"], n)
                        for j in range(2):
                            for ri in range(2):
                                for k in range(4):
                                    ins = mm(ps[:, 2 * j + ri, 0:D], DF[:, k, (4 * ri + m) * P:(4 * ri + m + 1) * P],
                                             XIN[:, b * TB + 4 * j + k, :], k == 0, k == 3)
                        ins.then_inc(s["xf_ps"], 1)
                    pe.wait_ge(s["yf_ready"], 4 * (b + 1))
                    pe.wait_ge(s["dfi_in"], 16)
                    for t in range(TB):
                        n, j, k = b * TB + t, t // 4, t % 4
                        if n >= 2:
                            pe.wait_ge(s["xt_ready"], n - 1)
                        for m in range(8):
                            mm(ps[:, 4 + n % 2, 0:D], DI[:, m, k * P:(k + 1) * P], YF[:, m % 4, 2 * j + m // 4, :], m == 0, m == 7)
                        mm(bank(6 + n % 2), AT[0:BIAS_ROW + 1, n * P:(n + 1) * P], VW[0:BIAS_ROW + 1, b, 1, :], True, True)\
                            .then_inc(s["yd_ps"], 1)
                stage_end("tensor", pe)
            if "E" in stages:
                pe.wait_ge(s["wE_in"], 16 * 5)
                for f in range(HID1 // P):
                    for k in range(KD):
                        ins = mm(ps[:, 7, f:f + 1], w1[:, k, f * P:(f + 1) * P], gb_ffn[:, 1, k:k + 1], k == 0, k == 1)
                ins.then_inc(s["b1p_ps"], 1)
                pe.wait_ge(s["w1s"], 1)
                for i in range(NBLK):
                    for t in range(4):
                        n = i * 4 + t
                        pe.wait_ge(s["zE_ready"], n + 1)
                        if n >= 2:
                            pe.wait_ge(s["xTE_sb"], n - 1)
                        for k in range(KD):
                            ins = pe.transpose(ps[:, n % 2, k * P:(k + 1) * P], xnE[:, t, k * P:(k + 1) * P], ident[:])
                        ins.then_inc(s["xTE_ps"], 1)
                    pe.wait_ge(s["xTE_sb"], 4 * i + 4)
                    for f in range(HID1 // P):
                        n = i * 8 + f
                        if n >= 2:
                            pe.wait_ge(s["hE_sb"], n - 1)
                        for k in range(KD):
                            ins = mm(bank(2 + n % 2), w1[:, k, f * P:(f + 1) * P], xT[:, k, :], k == 0, k == KD - 1)
                        ins.then_inc(s["hE_ps"], 1)
                    pe.wait_ge(s["hE_sb"], 8 * i + 8)
                    for t in range(4):
                        n = i * 4 + t
                        if n >= 2:
                            pe.wait_ge(s["oE_read"], n - 1)
                        for f in range(HID1 // P):
                            ins = mm(ps[:, 4 + n % 2, 0:D], hT[:, f, t * P:(t + 1) * P], w2[:, f, :], f == 0, f == 7)
                        ins.then_inc(s["oE_ps"], 1)
                stage_end("tensor", pe)
            if "F" in stages:
                for i in range(NBLK):
                    for t in range(4):
                        n = i * 4 + t
                        pe.wait_ge(s["zF_ready"], n + 1)
                        if n >= 2:
                            pe.wait_ge(s["zTF_sb"], n - 1)
                        for k in range(KD):
                            ins = pe.transpose(ps[:, n % 2, k * P:(k + 1) * P], zF[:, t, k * P:(k + 1) * P], ident[:])
                        ins.then_inc(s["zTF_ps"], 1)
                    for t in range(4):
                        n = i * 4 + t
                        pe.wait_ge(s["zTF_sb"], n + 1)
                        if n >= 2:
                            pe.wait_ge(s["yF_sb"], n - 1)
                        for k in range(KD):
                            ins = mm(ps[:, 2 + n % 2, 0:D + NE], zTF[:, k, t * P:(t + 1) * P], wx[:, k, :], k == 0, k == KD - 1)
                        ins.then_inc(s["yF_ps"], 1)
                pe.wait_ge(s["oh_ready"], 1)
                ohf = oh.rearrange("p t e -> p (t e)")
                mm(bank(4, NT * NE), tri[:], ohf, True, True)
                mm(bank(5, NT * NE), ones[:], ohf, True, True).then_inc(s["cum_ps"], 1)

        @block.scalar
        def _(a):
            own = Steps(a, s["own_a"])

            def copy(o, i):
                return a.activation(o, i, ACT.Copy)

            for i in range(4):
                a.wait_ge(s["kv_ps"], i + 1)
                if i == 0:
                    a.wait_ge(s["wA_in"], 16 * 6)
                a.activation(kvT[:, i // 2, i % 2, :], bank(i, NB * S2), ACT.Identity,
                             bias=bias0[:, 1 + i // 2, i % 2:i % 2 + 1]).then_inc(s["kv_sb"], 1)
            for b in range(NB):
                for g in range(2):
                    for c in range(NCH):
                        n, m = (b * 2 + g) * NCH + c, min(P, GW - c * P)
                        a.wait_ge(s["vwo_ps"], n + 1)
                        copy(vwo[0:m, b, g * NCH + c, :], ps[0:m, 4 + n % 4, 0:D]).then_inc(s["vwo_sb"], 1)
            for b in range(NB):
                for t in range(TB):
                    n = b * TB + t
                    a.wait_ge(s["zTA_ps"], n + 1)
                    copy(zTA[:, :, t * P:(t + 1) * P], ps[:, 6 + n % 2, 0:D].rearrange("p (k c) -> p k c", k=KD))\
                        .then_inc(s["zTA_sb"], 1)
                for h in range(2):
                    for g in range(2):
                        n = (b * 2 + h) * 2 + g
                        a.wait_ge(s["qT_ps"], n + 1)
                        a.activation(qT[:, g, h * BLK:(h + 1) * BLK], bank(6 + n % 2), ACT.Identity,
                                     bias=bias0[:, 0, g:g + 1]).then_inc(s["qT_sb"], 1)
                NU = 2 * TB
                for step in range(NU + 2):
                    if step < NU:
                        u = b * NU + step
                        a.wait_ge(s["scores_read"], u + 1)
                        a.activation(Pb[:, u % 4, :], Pb[:, u % 4, :], ACT.Exp, scale=1.0 / math.sqrt(DH0))\
                            .then_inc(s["probs_exp"], 1)
                    if step >= 2:
                        u = b * NU + step - 2
                        a.wait_ge(s["pt_ps"], u + 1)
                        if u >= 2:
                            a.wait_ge(s["oA_ps"], u - 1)
                        last_rows = GW - 4 * P
                        own.done(copy(PT[:, u % 2, 0:4 * P], bank(4)))
                        copy(PT[0:last_rows, u % 2, 4 * P:5 * P], ps[0:last_rows, 5, 0:P]).then_inc(s["pt_sb"], 1)
            stage_end("scalar", a)
            if "B" in stages:
                for i in range(NBLK):
                    for t in range(4):
                        n = i * 4 + t
                        a.wait_ge(s["zTB_ps"], n + 1)
                        copy(zTB[:, :, n * P:(n + 1) * P], ps[:, n % 2, 0:D].rearrange("p (k c) -> p k c", k=KD))\
                            .then_inc(s["zTB_sb"], 1)
                    a.wait_ge(s["lgB_exp0"], i + 1)
                    a.activation(sm8[:, 1, :], sm8[:, 0, :], ACT.Exp).then_inc(s["lgB_exp"], 1)
                    a.wait_ge(s["combT_ps"], i + 1)
                    copy(combT_v[0:NE, i * BLK:(i + 1) * BLK], ps[0:NE, 3, :]).then_inc(s["combT_sb"], 1)
                with a.Fori(0, NE // 2, 1) as pair:
                    for par in range(2):
                        a.wait_ge(s[f"w1e_in{par}"], pair * 48 + 48)
                        for n in range(UPE):
                            w = par * UPE + n
                            a.wait_ge(s["h_ps"], pair * (2 * UPE) + (w + 1))
                            a.wait_ge(s["g_ready"], pair * (2 * UPE) + (w + 1 + CREDIT - 2))
                            a.activation(sig[:, w % 2, :], bank(2 * (w % HBUF) + 1), ACT.Sigmoid,
                                         bias=b1e[:, par, 4 + n % 4:5 + n % 4]).then_inc(s["sig_ready"], 1)
                stage_end("scalar", a)
            if "K" in stages:
                a.wait_ge(s["kparam_in"], 16 * 6)
                a.activation(kp[:, 5, :], kp[:, 4, :], ACT.Exp).then_inc(s["kp_exp"], 1)
                a.wait_ge(s["kp_par"], 1)
                a.activation(kp[:, 8, :], kp[:, 6, :], ACT.Tanh, scale=0.5).then_inc(s["kp_exp"], 1)
                for n in range(8):
                    dst = (Pr, Qr)[n // 4][:, (n % 4) * 32:(n % 4) * 32 + 32, :]
                    a.wait_ge(s["kv_arg"], n + 1)
                    a.activation(dst, dst, ACT.Exp).then_inc(s["mag_ready"], 1)
                a.wait_ge(s["kp_par"], 2)
                two_pi = 2 * math.pi
                own.done(a.activation(kp[:, 10, :], kp[:, 7, :], ACT.Sin, scale=two_pi))
                own.done(a.activation(kp[:, 11, :], kp[:, 9, :], ACT.Sin, scale=-two_pi, bias=halfpi[:]))
                a.activation(kp[:, 12, :], kp[:, 7, :], ACT.Sin, scale=math.pi).then_inc(s["kp_exp"], 1)
                for n in range(8):
                    a.wait_ge(s["k_trig"], n + 1)
                    if n:
                        a.wait_ge(s["k_used"], n)
                    own.done(a.activation(tk[2], tk[0], ACT.Sin, scale=two_pi))
                    a.activation(tk[3], tk[1], ACT.Sin, scale=-two_pi, bias=halfpi[:]).then_inc(s["k_sin"], 1)
                for q in range(4):
                    for h in range(2):
                        a.wait_ge(s["k_ps"], 2 * q + h + 1)
                        copy(KT[64 * h:64 * h + 64, :, q * 16:(q + 1) * 16].rearrange("p b c -> p c b"),
                             ps[64 * h:64 * h + 64, 4 * h + q, :].rearrange("p (c b) -> p c b", b=R)).then_inc(s["k_sb"], 1)
                for m in range(8):
                    a.wait_ge(s["ks_ps"], m + 1)
                    copy((KS0r, KS0i)[m // 4][:, m % 4, :], ps[:, m % 4, 0:D]).then_inc(s["ks_sb"], 1)
                stage_end("scalar", a)
            if "C" in stages:
                a.wait_ge(s["prepC_ps"], 1)
                copy(k1T[:, :], bank(0, NB * S2)).then_inc(s["prepC_sb"], 1)
                for g in range(2):
                    a.wait_ge(s["prepC_ps"], 2 + g)
                    copy(vT1[:, g, :], bank(1 + g, NB * S2)).then_inc(s["prepC_sb"], 1)
                for b in range(NB):
                    for g in range(2):
                        a.wait_ge(s["prepC_ps"], 4 + 2 * b + g)
                        copy(wqk[:, g, b, :], bank(4 + 2 * b + g, SW)).then_inc(s["prepC_sb"], 1)
                for b in range(NB):
                    for t in range(TB):
                        n = b * TB + t
                        a.wait_ge(s["uT_ps"], n + 1)
                        if b and t == 0:
                            a.wait_ge(s["sC_ps"], TB)
                        copy(uT[:, :, t * P:(t + 1) * P], ps[:, n % 2, 0:D].rearrange("p (k c) -> p k c", k=KD))\
                            .then_inc(s["uT_sb"], 1)
                    for t in range(TB):
                        n = b * TB + t
                        a.wait_ge(s["exC_in"], n + 1)
                        a.activation(Ex[:, n % 2, :], Ex[:, n % 2, :], ACT.Exp).then_inc(s["exC"], 1)
                        a.wait_ge(s["AT_ps"], n + 1)
                        if n == 0:
                            a.wait_ge(s["maskC"], 1)
                        copy(AT[0:S2, n * P:(n + 1) * P], ps[0:S2, 4, 0:P]).then_inc(s["AT_sb"], 1)
                stage_end("scalar", a)
            if "D" in stages:
                for n in range(NB * 4):
                    a.wait_ge(s["xf_ps"], n + 1)
                    if n:
                        a.wait_ge(s["yf_ready"], n)
                    copy(XS, ps[:, 0:4, 0:D]).then_inc(s["xf_sb"], 1)
                stage_end("scalar", a)
            if "E" in stages:
                for i in range(NBLK):
                    for t in range(4):
                        n = i * 4 + t
                        a.wait_ge(s["xTE_ps"], n + 1)
                        if t == 0 and i:
                            a.wait_ge(s["hE_ps"], 8 * i)
                        copy(xT[:, :, t * P:(t + 1) * P], ps[:, n % 2, 0:D].rearrange("p (k c) -> p k c", k=KD))\
                            .then_inc(s["xTE_sb"], 1)
                    for f in range(HID1 // P):
                        n = i * 8 + f
                        a.wait_ge(s["hE_ps"], n + 1)
                        if n == 0:
                            a.wait_ge(s["b1p_sb"], 1)
                        if f == 0 and i:
                            a.wait_ge(s["oE_ps"], 4 * i)
                        a.activation(hT[:, f, :], bank(2 + n % 2), ACT.Gelu, bias=b1p[:, f:f + 1]).then_inc(s["hE_sb"], 1)
                stage_end("scalar", a)
            if "F" in stages:
                for i in range(NBLK):
                    for t in range(4):
                        n = i * 4 + t
                        a.wait_ge(s["zTF_ps"], n + 1)
                        if t == 0 and i:
                            a.wait_ge(s["yF_ps"], 4 * i)
                        copy(zTF[:, :, t * P:(t + 1) * P], ps[:, n % 2, 0:D].rearrange("p (k c) -> p k c", k=KD))\
                            .then_inc(s["zTF_sb"], 1)
                a.wait_ge(s["lgF"], 1)
                a.activation(fs[:, 1], fs[:, 0], ACT.Exp).then_inc(s["lgF_exp"], 1)

        @block.gpsimd
        def _(p):
            own = Steps(p, s["own_p"])
            own.done(p.memset(neghalf[:], -0.5))
            own.done(p.memset(ones[:], 1.0))
            own.done(p.memset(halfpi[:], math.pi / 2))
            own.settle()
            p.wait_ge(s["rows_in"], 16 * 9)
            for b in range(NB):
                ln_rstd(p, own, TB, 0, "lnA_stats", b + 1, "lnA_rstd")
                p.wait_ge(s["zA_ready"], (b + 1) * TB)
                for t in range(TB):
                    T = b * TB + t
                    p.tensor_tensor(X[:, T, :], X[:, T, :], rows[:, BO0, :], ALU.add).then_inc(s["xbA"], 1)
                for st in range(2 * TB):
                    u = b * 2 * TB + st
                    p.wait_ge(s["probs_sum"], u + 1)
                    pv = Pb[:, u % 4, :].rearrange("p (h k) -> p h k", h=HG)
                    p.tensor_tensor(pv, pv, smA[:, u % 4, :].unsqueeze(2).broadcast_to([P, HG, S2]), ALU.mult)\
                        .then_inc(s["probs_norm"], 1)
            stage_end("gpsimd", p)
            if "B" in stages:
                for i in range(NBLK):
                    ln_rstd(p, own, 4, 4 * (i % 2), "lnB_stats", i + 1, "lnB_rstd")
                own.done(p.memset(acc[:, 1:4, :], 0.0))
                p.wait_ge(s["comb_out"], 16)
                own.done(p.memset(acc[:, 0, :], 0.0))
                own.settle()
                with p.Fori(0, NE // 2, 1) as pair:
                    for par in range(2):
                        for n in range(UPE):
                            w, i, f = par * UPE + n, n // 4, n % 4
                            p.wait_ge(s["gc_ready"], pair * (2 * UPE) + (w + 1))
                            dst = acc[:, f, i * BLK:(i + 1) * BLK]
                            p.tensor_tensor(dst, dst, gc[:, w % 2, :], ALU.add).then_inc(s["acc_added"], 1)
                p.wait_ge(s["acc_added"], NE * UPE + CREDIT)
                p.nop().then_inc(s["acc_ready"], 1)
                stage_end("gpsimd", p)
            if "K" in stages:
                p.wait_ge(s["kp_par"], 1)
                for n in range(8):
                    c = slice((n % 4) * 32, (n % 4) * 32 + 32)
                    p.tensor_tensor((Pr, Qr)[n // 4][:, c, :], kp[:, 6, c].unsqueeze(2).broadcast_to([P, 32, R]),
                                    ramps[:, n // 4, :].unsqueeze(1).broadcast_to([P, 32, R]), ALU.mult)\
                        .then_inc(s["kv_arg"], 1)
                stage_end("gpsimd", p)
            if "C" in stages:
                own.done(p.memset(AT[:, :], 0.0))
                own.settle()
                p.memset(AT[BIAS_ROW:BIAS_ROW + 1, :], 1.0).then_inc(s["maskC"], 1)
                p.wait_ge(s["maskC"], 1)
                for b in range(NB):
                    ln_rstd(p, own, TB, 0, "lnC_stats", b + 1, "lnC_rstd")
                    ln_rstd(p, own, TB, TB, "lnU_stats", b + 1, "lnU_rstd")
                stage_end("gpsimd", p)
            if "D" in stages:
                for b in range(NB):
                    for m in range(4):
                        n = b * 4 + m
                        p.wait_ge(s["xf_sb"], n + 1)
                        if n:
                            p.wait_ge(s["yf_ready"], n)
                        kn = KS0n if m == 0 else KS0r[:, m, :]
                        p.tensor_tensor(pt_[:, 0, :], XS[:, 2, :], KS0r[:, m, :], ALU.mult).then_inc(s["pr_p"], 1)
                        p.tensor_tensor(pt_[:, 1, :], XS[:, 3, :], KS0i[:, m, :], ALU.mult).then_inc(s["pr_p"], 1)
                        p.tensor_tensor(pt_[:, 2, :], XS[:, 2, :], KS0i[:, m, :], ALU.mult).then_inc(s["pr_p"], 1)
                        p.tensor_tensor(pt_[:, 3, :], XS[:, 3, :], kn, ALU.mult).then_inc(s["pr_p"], 1)
                    p.wait_ge(s["xf_ps"], 4 * b + 4)
                    for t in range(TB):
                        T = b * TB + t
                        p.tensor_tensor(XIN[:, T, :], XIN[:, T, :], rows[:, DSKIP, :], ALU.mult).then_inc(s["xskip"], 1)
                stage_end("gpsimd", p)
            if "E" in stages:
                for i in range(NBLK):
                    ln_rstd(p, own, 4, 0, "lnE_stats", i + 1, "lnE_rstd")
                    for t in range(4):
                        n = i * 4 + t
                        ln_rstd(p, own, 1, 8 + n % 2, "lnO_stats", n + 1, "lnO_rstd")
                        p.wait_ge(s["oE_ready"], n + 1)
                        own.done(p.tensor_tensor(oE[:, n % 2, :], oE[:, n % 2, :], rows[:, GNO, :], ALU.mult))
                        own.settle()
                        own.done(p.tensor_tensor(oE[:, n % 2, :], oE[:, n % 2, :], rows[:, BNO, :], ALU.add))
                        own.settle()
                        p.tensor_tensor(X[:, n, :], X[:, n, :], oE[:, n % 2, :], ALU.add).then_inc(s["xE_done"], 1)
                stage_end("gpsimd", p)
            if "F" in stages:
                for i in range(NBLK):
                    ln_rstd(p, own, 4, 0, "lnF_stats", i + 1, "lnF_rstd")

        @block.vector
        def _(v):
            own = Steps(v, s["own_v"])

            def tt(o, x, y, op):
                own.done(v.tensor_tensor(o, x, y, op))

            def ts(o, x, c1, c2, op0, op1=ALU.bypass):
                own.done(v.tensor_scalar(o, x, c1, c2, op0, op1) if c2 is not None else v.tensor_scalar(o, x, c1, None, op0))

            def stt(o, x, c, y, op0, op1):
                return v.scalar_tensor_tensor(out=o, in0=x, scalar=c, in1=y, op0=op0, op1=op1)

            def bc(x, n):
                return x.unsqueeze(2).broadcast_to([x.shape[0], x.shape[1], n])

            v.wait_ge(s["consts_in"], 16 * 7)
            for i in range(2):
                for g in range(2):
                    v.wait_ge(s["kv_sb"], 2 * i + g + 1)
                    for b in range(NB):
                        v.tensor_tensor((kblk, vblk)[i][:, g, b, :].rearrange("p (h k) -> p h k", h=HG),
                                        kvT[:, i, g, b * S2:(b + 1) * S2].unsqueeze(1).broadcast_to([P, HG, S2]),
                                        bc(mask16[:], S2), ALU.mult).then_inc(s["kblk_ready"], 1)
            v.wait_ge(s["x_in"], 16)
            for b in range(NB):
                ln_stats(v, own, lambda j: X[:, b * TB + j, :], TB, 0, "lnA_stats")
                v.wait_ge(s["lnA_rstd"], b + 1)
                if b:
                    v.wait_ge(s["zTA_ps"], TB)
                for t in range(TB):
                    normalise(v, zA[:, t, :], X[:, b * TB + t, :], t).then_inc(s["zA_ready"], 1)
                NU = 2 * TB
                for step in range(NU + 4):
                    if step < NU:
                        u = b * NU + step
                        sv = ps[:, 2 * (u % 2):2 * (u % 2) + 2, 0:BW].rearrange("p c (h k) -> p c h k", k=S2)
                        v.wait_ge(s["scores_ready"], u + 1)
                        own.done(v.tensor_reduce(mxA[:, u % 4, :].rearrange("p (c h) -> p c h", c=2), sv, AX, ALU.max))
                        own.settle()
                        if u >= 4:
                            v.wait_ge(s["pt_ps"], u - 3)
                        v.tensor_tensor(Pb[:, u % 4, :].rearrange("p (c h k) -> p c h k", c=2, h=4), sv,
                                        mxA[:, u % 4, :].rearrange("p (c h) -> p c h", c=2).unsqueeze(3)
                                        .broadcast_to([P, 2, 4, S2]), ALU.subtract).then_inc(s["scores_read"], 1)
                    if 1 <= step <= NU:
                        u = b * NU + step - 1
                        v.wait_ge(s["probs_exp"], u + 1)
                        own.done(v.tensor_reduce(smA[:, u % 4, :], Pb[:, u % 4, :].rearrange("p (h k) -> p h k", h=HG), AX, ALU.add))
                        own.settle()
                        v.reciprocal(smA[:, u % 4, :], smA[:, u % 4, :]).then_inc(s["probs_sum"], 1)
                    if step >= 4 and step % 2 == 1:
                        T = b * TB + (step - 5) // 2
                        v.wait_ge(s["oA_ps"], 2 * T + 2)
                        v.wait_ge(s["xbA"], T + 1)
                        v.tensor_tensor(X[:, T, :], X[:, T, :], ps[:, 6 + T % 2, 0:D], ALU.add).then_inc(s["xA_done"], 1)
            stage_end("vector", v)
            if "B" in stages:
                for i in range(NBLK):
                    ln_stats(v, own, lambda j: X[:, 4 * i + j, :], 4, 4 * (i % 2), "lnB_stats")
                    v.wait_ge(s["lnB_rstd"], i + 1)
                    if i >= 2:
                        v.wait_ge(s["zTB_ps"], 4 * (i - 1))
                    for t in range(4):
                        normalise(v, zB[:, i % 2, t, :], X[:, 4 * i + t, :], 4 * (i % 2) + t).then_inc(s["zB_ready"], 1)
                    E8 = [sm8[:, r, :].rearrange("p (t e) -> p t e", t=4) for r in range(12)]
                    small = [sm8[:, 10, 4 * r:4 * r + 4] for r in range(8)]
                    v.wait_ge(s["lgB_ps"], i + 1)
                    own.done(v.tensor_reduce(small[0], ps[:, 2, 0:4 * NE].rearrange("p (t e) -> p t e", t=4), AX, ALU.max))
                    own.settle()
                    v.tensor_tensor(E8[0], ps[:, 2, 0:4 * NE].rearrange("p (t e) -> p t e", t=4), bc(small[0], NE),
                                    ALU.subtract).then_inc(s["lgB_exp0"], 1)
                    v.wait_ge(s["lgB_exp"], i + 1)
                    own.done(v.tensor_reduce(small[1], E8[1], AX, ALU.add))
                    own.settle()
                    own.done(v.reciprocal(small[2], small[1]))
                    own.settle()
                    tt(E8[2], E8[1], bc(small[2], NE), ALU.mult)
                    own.settle()
                    src = 2
                    for r in range(2):
                        own.done(v.tensor_reduce(small[3 + r], E8[src], AX, ALU.max))
                        own.settle()
                        tt(E8[3], E8[src], bc(small[3 + r], NE), ALU.is_equal)
                        own.settle()
                        tt(E8[3], E8[3], desc8[:], ALU.mult)
                        own.settle()
                        own.done(v.tensor_reduce(small[5], E8[3], AX, ALU.max))
                        own.settle()
                        tt(E8[4 + r], E8[3], bc(small[5], NE), ALU.is_equal)
                        own.settle()
                        if r == 0:
                            own.done(stt(E8[6], E8[4], -2.0, E8[2], ALU.mult, ALU.add))
                            own.settle()
                            src = 6
                    tt(E8[4], E8[4], E8[5], ALU.add)
                    tt(small[6], small[3], small[4], ALU.add)
                    own.settle()
                    ts(small[6], small[6], 1e-9, None, ALU.add)
                    tt(E8[4], E8[4], E8[2], ALU.mult)
                    own.settle()
                    own.done(v.reciprocal(small[7], small[6]))
                    own.settle()
                    if i:
                        v.wait_ge(s["combT_ps"], i)
                    v.tensor_tensor(E8[11], E8[4], bc(small[7], NE), ALU.mult).then_inc(s["comb_ready"], 1)
                    v.wait_ge(s["comb_ready"], i + 1)
                    own.done(v.tensor_reduce(comb_sum[:, 4 * i:4 * i + 4], E8[11], AX, ALU.add))
                own.settle()
                v.nop().then_inc(s["g_ready"], CREDIT)
                v.nop().then_inc(s["acc_added"], CREDIT)
                with v.Fori(0, NE // 2, 1) as pair:
                    for par in range(2):
                        v.wait_ge(s[f"w1e_in{par}"], pair * 48 + 48)
                        for n in range(UPE):
                            w, i, f = par * UPE + n, n // 4, n % 4
                            v.wait_ge(s["sig_ready"], pair * (2 * UPE) + (w + 1))
                            stt(gt[:, w % 2, :], bank(2 * (w % HBUF)), b1e[:, par, f:f + 1], sig[:, w % 2, :], ALU.add, ALU.mult)\
                                .then_inc(s["g_ready"], 1)
                            v.wait_ge(s["g_ready"], pair * (2 * UPE) + (w + 1 + CREDIT))
                            v.wait_ge(s["acc_added"], pair * (2 * UPE) + (w + 1 + CREDIT - 2))
                            v.tensor_tensor(gc[:, w % 2, :], gt[:, w % 2, :], combB[:, par, i * BLK:(i + 1) * BLK], ALU.mult)\
                                .then_inc(s["gc_ready"], 1)
                for T in range(NT):
                    own.done(stt(X[:, T, :], rows[:, BOF, :], comb_sum[:, T:T + 1], X[:, T, :], ALU.mult, ALU.add))
                own.settle()
                for T in range(NT):
                    v.wait_ge(s["oB_ps"], T + 1)
                    v.tensor_tensor(X[:, T, :], X[:, T, :], ps[:, 6 + T % 2, 0:D], ALU.add).then_inc(s["xB_done"], 1)
                stage_end("vector", v)

            if "K" in stages:
                ARE, AIM, CRE, CIM, LOGDT, DT, AR, TURN, TH, ABS, SIN, COS, SINH = range(13)
                q = lambda i: kp[:, i, :]

                def op(o, x, y, kind):
                    tt(q(o), q(x), q(y), kind)
                    own.settle()

                def turns(o, r, x):
                    ts(r, x, ROUND, -ROUND, ALU.add, ALU.add)
                    own.settle()
                    tt(o, x, r, ALU.subtract)
                    own.settle()

                v.wait_ge(s["kparam_in"], 16 * 6)
                v.wait_ge(s["kp_exp"], 1)
                v.tensor_tensor(q(AR), q(DT), q(ARE), ALU.mult).then_inc(s["kp_par"], 1)
                op(13, DT, AIM, ALU.mult)
                ts(q(13), q(13), 1 / (2 * math.pi), None, ALU.mult)
                own.settle()
                turns(q(TURN), q(14), q(13))
                stt(q(ABS), q(TURN), -1.0, q(TURN), ALU.mult, ALU.max).then_inc(s["kp_par"], 1)
                v.wait_ge(s["kp_exp"], 2)
                ts(q(13), q(TH), -1.0, 1.0, ALU.mult, ALU.add)
                own.settle()
                own.done(v.reciprocal(q(14), q(13)))
                own.settle()
                own.done(stt(q(14), q(TH), 2.0, q(14), ALU.mult, ALU.mult))
                own.settle()
                ts(q(15), q(14), 1.0, None, ALU.add)
                v.wait_ge(s["kp_exp"], 3)
                own.done(stt(q(16), q(SINH), -2.0, q(SINH), ALU.mult, ALU.mult))
                op(17, 14, COS, ALU.mult)
                op(16, 16, 17, ALU.add)
                op(17, 15, SIN, ALU.mult)
                op(13, ARE, ARE, ALU.mult)
                op(18, AIM, AIM, ALU.mult)
                op(13, 13, 18, ALU.add)
                own.done(v.reciprocal(q(13), q(13)))
                op(14, 16, ARE, ALU.mult)
                op(15, 17, AIM, ALU.mult)
                op(18, 17, ARE, ALU.mult)
                op(19, 16, AIM, ALU.mult)
                op(14, 14, 15, ALU.add)
                op(18, 18, 19, ALU.subtract)
                op(14, 14, 13, ALU.mult)
                op(18, 18, 13, ALU.mult)
                op(16, CRE, 14, ALU.mult)
                op(15, CIM, 18, ALU.mult)
                op(17, CRE, 18, ALU.mult)
                op(19, CIM, 14, ALU.mult)
                op(16, 16, 15, ALU.subtract)
                op(17, 17, 19, ALU.add)
                ts(q(16), q(16), 2.0, None, ALU.mult)
                ts(q(17), q(17), 2.0, None, ALU.mult)
                own.settle()
                for n in range(8):
                    c = slice((n % 4) * 32, (n % 4) * 32 + 32)
                    wr, wi = ((Pr, Pi), (Qr, Qi))[n // 4]
                    wr, wi = wr[:, c, :], wi[:, c, :]
                    f4 = [t.rearrange("p (c k) -> p c k", k=R) for t in tk]
                    if n:
                        v.wait_ge(s["k_sin"], n)
                    tt(f4[0], bc(kp[:, TURN, c], R), ramps[:, n // 4, :].unsqueeze(1).broadcast_to([P, 32, R]), ALU.mult)
                    own.settle()
                    turns(tk[0], tk[1], tk[0])
                    stt(tk[1], tk[0], -1.0, tk[0], ALU.mult, ALU.max).then_inc(s["k_trig"], 1)
                    v.wait_ge(s["k_sin"], n + 1)
                    v.wait_ge(s["mag_ready"], n + 1)
                    if n < 4:
                        dr, di = bc(kp[:, 16, c], R), bc(kp[:, 17, c], R)
                        tt(wi, wr, f4[2], ALU.mult)
                        own.settle()
                        tt(wr, wr, f4[3], ALU.mult)
                        own.settle()
                        tt(f4[2], wi, di, ALU.mult)
                        tt(f4[3], wr, di, ALU.mult)
                        own.settle()
                        tt(wr, wr, dr, ALU.mult)
                        tt(wi, wi, dr, ALU.mult)
                        own.settle()
                        tt(wr, wr, f4[2], ALU.subtract)
                        v.tensor_tensor(wi, wi, f4[3], ALU.add).then_inc(s["k_used"], 1)
                    else:
                        own.done(stt(wi, wr, -1.0, f4[2], ALU.mult, ALU.mult))
                        own.settle()
                        v.tensor_tensor(wr, wr, f4[3], ALU.mult).then_inc(s["k_used"], 1)
                for m in range(8):
                    v.wait_ge(s["ks_sb"], m + 1)
                    stt((KSCr, KSCi)[m // 4][:, m % 4, :], (KS0r, KS0i)[m // 4][:, m % 4, :], sgn[:, 0:1],
                        ps[:, m % 4, D:2 * D], ALU.mult, ALU.add).then_inc(s["ks_done"], 1)
                v.wait_ge(s["ks_done"], 8)
                for re, im, ny in ((KS0r, KS0i, KS0n), (KSCr, KSCi, KSCn)):
                    own.done(v.tensor_copy(ny, re[:, 0, :]))
                    own.settle()
                    own.done(v.tensor_copy(ny[0:1, :], im[0:1, 0, :]))
                    own.settle()
                    own.done(v.memset(im[0:1, 0, :], 0.0))
                stage_end("vector", v)
            if "C" in stages:
                v.wait_ge(s["wC_in"], 16 * 8)
                v.memset(VW[:], 0.0).then_inc(s["vw_zero"], 1)
                for b in range(NB):
                    ts(maskb[:, b, :].rearrange("p (h k) -> p h k", h=H1),
                       vmask8[:, b, :].unsqueeze(1).broadcast_to([P, H1, S2]), HUGE, -HUGE, ALU.mult, ALU.add)
                ts(tmask, tmask8[:], 1.0 / H1, None, ALU.mult)
                v.wait_ge(s["prepC_sb"], 1)
                for b in range(NB):
                    v.tensor_tensor(kb1[:, b, :].rearrange("p (h k) -> p h k", h=H1),
                                    k1T[:, b * S2:(b + 1) * S2].unsqueeze(1).broadcast_to([P, H1, S2]),
                                    bc(mask32[:], S2), ALU.mult).then_inc(s["prepC_v"], 1)
                v.wait_ge(s["bfilm_in"], 16 * NB)
                for b in range(NB):
                    for io in range(2):
                        v.wait_ge(s["prepC_ps"], 7 + 2 * b + io + 1)
                        ts(VW[0:S2, b, io, :], ps[0:S2, 2 * b + io, :], mgate[0:S2, 0:1], None, ALU.mult)
                        one = VW[BIAS_ROW:BIAS_ROW + 1, b, io, :]
                        ts(one, one, mgate[BIAS_ROW:BIAS_ROW + 1, 0:1], None, ALU.mult)
                        own.settle()
                        ts(one[:, 0:D], one[:, 0:D], 1.0, None, ALU.add)
                        own.settle()
                        if io == 0:
                            r97 = slice(0, BIAS_ROW + 1)
                            sc, sh = VW[r97, b, 0, 0:D], VW[r97, b, 0, D:2 * D]
                            tt(xn[r97, 0, :], sc, rows[r97, BNI, :], ALU.mult)
                            own.settle()
                            tt(sh, sh, xn[r97, 0, :], ALU.add)
                            tt(sc, sc, rows[r97, GNI, :], ALU.mult)
                            own.settle()
                        v.nop().then_inc(s["prepC_v"], 1)
                for b in range(NB):
                    ln_stats(v, own, lambda j: X[:, b * TB + j, :], TB, 0, "lnC_stats")
                    v.wait_ge(s["lnC_rstd"], b + 1)
                    for t in range(TB):
                        normalise(v, U[:, b * TB + t, :], X[:, b * TB + t, :], t).then_inc(s["u_ready"], 1)
                    v.wait_ge(s["u_ready"], (b + 1) * TB)
                    ln_stats(v, own, lambda j: U[:, b * TB + j, :], TB, TB, "lnU_stats")
                    v.wait_ge(s["lnU_rstd"], b + 1)
                    for step in range(TB + 1):
                        if step < TB:
                            n, par = b * TB + step, step % 2
                            S, Rr, E = Sc[:, par, :], Rk[:, par, :], Ex[:, par, :]
                            hv = lambda x: x.rearrange("p (h k) -> p h k", h=H1)
                            v.wait_ge(s["sC_ps"], n + 1)
                            stt(S, bank(2 + n % 2, SW), 1.0 / math.sqrt(DH1), maskb[:, b, :], ALU.mult, ALU.add)\
                                .then_inc(s["sC_read"], 1)
                            v.wait_ge(s["sC_read"], n + 1)
                            for r in range(TOPK // 8):
                                cur = S if r == 0 else Rr
                                for h in range(H1):
                                    own.done(v.max(top[:, par, h, 8 * r:8 * r + 8], hv(cur)[:, h, :]))
                                own.settle()
                                if r == 0:
                                    v.tensor_tensor(hv(E), hv(S), bc(top[:, par, :, 0], S2), ALU.subtract)\
                                        .then_inc(s["exC_in"], 1)
                                for h in range(H1):
                                    own.done(v.match_replace(hv(Rr)[:, h, :], top[:, par, h, 8 * r:8 * r + 8],
                                                             hv(cur)[:, h, :], TAKEN))
                                own.settle()
                            v.wait_ge(s["exC"], n + 1)
                            own.done(stt(E, Rr, TAKEN / 1.5, E, ALU.is_le, ALU.mult))
                            own.settle()
                            own.done(v.tensor_reduce(smC[:, par, 0, :], hv(E), AX, ALU.add))
                            own.settle()
                            own.done(v.reciprocal(smC[:, par, 1, :], smC[:, par, 0, :]))
                            own.settle()
                            ts(smC[:, par, 2, :], smC[:, par, 1, :], tmask[:, n:n + 1], None, ALU.mult)
                            own.settle()
                            tt(hv(E), hv(E), bc(smC[:, par, 2, :], S2), ALU.mult)
                            own.settle()
                            if n >= 2:
                                v.wait_ge(s["AT_ps"], n - 1)
                            v.tensor_reduce(a77[:, par, :], E.rearrange("p (h k) -> p k h", h=H1), AX, ALU.add)\
                                .then_inc(s["attn_ready"], 1)
                        if step >= 1:
                            n = b * TB + step - 1
                            par = n % 2
                            own.done(normalise(v, xn[:, par, :], U[:, n, :], TB + step - 1))
                            own.settle()
                            v.wait_ge(s["film_ps"], n + 1)
                            tt(xn[:, par, :], xn[:, par, :], ps[:, 6 + n % 2, 0:D], ALU.mult)
                            own.settle()
                            v.tensor_tensor(XIN[:, n, :], xn[:, par, :], ps[:, 6 + n % 2, D:2 * D], ALU.add)\
                                .then_inc(s["xin_ready"], 1)
                stage_end("vector", v)
            if "D" in stages:
                for b in range(NB):
                    for m in range(4):
                        n = b * 4 + m
                        v.wait_ge(s["xf_sb"], n + 1)
                        x0r, x0i = XS[:, 0, :], XS[:, 1, :]
                        k0n, kcn = (KS0n, KSCn) if m == 0 else (KS0r[:, m, :], KSCr[:, m, :])
                        Y, T = (lambda r: YF[:, m, r, :]), (lambda r: tmpD[:, r, :])
                        for r, (kr, ki) in enumerate(((KS0r[:, m, :], KS0i[:, m, :]), (KS0i[:, m, :], k0n),
                                                      (KSCr[:, m, :], KSCi[:, m, :]), (KSCi[:, m, :], kcn))):
                            tt(Y(r), x0r, kr, ALU.mult)
                            tt(T(r), x0i, ki, ALU.mult)
                        own.settle()
                        for r in range(4):
                            tt(Y(r), Y(r), T(r), (ALU.subtract, ALU.add)[r % 2])
                        own.settle()
                        v.wait_ge(s["pr_p"], 4 * (n + 1))
                        tt(Y(2), Y(2), pt_[:, 0, :], ALU.add)
                        tt(Y(3), Y(3), pt_[:, 2, :], ALU.add)
                        own.settle()
                        tt(Y(2), Y(2), pt_[:, 1, :], ALU.subtract)
                        v.tensor_tensor(Y(3), Y(3), pt_[:, 3, :], ALU.add).then_inc(s["yf_ready"], 1)
                    for t in range(TB):
                        n = b * TB + t
                        T = tmpD[:, 4 + n % 2, :]
                        v.wait_ge(s["yd_ps"], n + 1)
                        v.wait_ge(s["xskip"], n + 1)
                        tt(T, XIN[:, n, :], ps[:, 4 + n % 2, 0:D], ALU.add)
                        own.settle()
                        tt(T, T, ps[:, 6 + n % 2, 0:D], ALU.mult)
                        own.settle()
                        v.tensor_tensor(T, T, ps[:, 6 + n % 2, D:2 * D], ALU.add).then_inc(s["xt_ready"], 1)
                        v.wait_ge(s["xt_ready"], n + 1)
                        tt(U[:, n, :], U[:, n, :], T, ALU.add)
                stage_end("vector", v)
            if "E" in stages:
                v.wait_ge(s["b1p_ps"], 1)
                v.tensor_tensor(b1p, ps[:, 7, 0:HID1 // P], b1[:], ALU.add).then_inc(s["b1p_sb"], 1)
                ts(w1[:, 0, :], w1[:, 0, :], gb_ffn[:, 0, 0:1], None, ALU.mult)
                v.tensor_scalar(w1[:, 1, :], w1[:, 1, :], gb_ffn[:, 0, 1:2], None, ALU.mult).then_inc(s["w1s"], 1)
                for i in range(NBLK):
                    ln_stats(v, own, lambda j: U[:, 4 * i + j, :], 4, 0, "lnE_stats")
                    v.wait_ge(s["lnE_rstd"], i + 1)
                    if i:
                        v.wait_ge(s["xTE_ps"], 4 * i)
                    for t in range(4):
                        normalise(v, xnE[:, t, :], U[:, 4 * i + t, :], t).then_inc(s["zE_ready"], 1)
                    for t in range(4):
                        own.done(v.tensor_tensor(U[:, 4 * i + t, :], U[:, 4 * i + t, :], rows[:, B2, :], ALU.add))
                    own.settle()
                    for t in range(4):
                        n = 4 * i + t
                        v.wait_ge(s["oE_ps"], n + 1)
                        v.tensor_tensor(U[:, n, :], U[:, n, :], ps[:, 4 + n % 2, 0:D], ALU.add).then_inc(s["oE_read"], 1)
                        v.wait_ge(s["oE_read"], n + 1)
                        ln_stats(v, own, lambda j: U[:, n, :], 1, 8 + n % 2, "lnO_stats")
                        v.wait_ge(s["lnO_rstd"], n + 1)
                        if n >= 2:
                            v.wait_ge(s["xE_done"], n - 1)
                        normalise(v, oE[:, n % 2, :], U[:, n, :], 8 + n % 2).then_inc(s["oE_ready"], 1)
                stage_end("vector", v)
            if "F" in stages:
                for i in range(NBLK):
                    ln_stats(v, own, lambda j: X[:, 4 * i + j, :], 4, 0, "lnF_stats")
                    v.wait_ge(s["lnF_rstd"], i + 1)
                    if i:
                        v.wait_ge(s["zTF_ps"], 4 * i)
                    for t in range(4):
                        normalise(v, zF[:, t, :], X[:, 4 * i + t, :], t).then_inc(s["zF_ready"], 1)
                    for t in range(4):
                        n = 4 * i + t
                        v.wait_ge(s["yF_ps"], n + 1)
                        tt(yF[:, n, :], ps[:, 2 + n % 2, 0:D], rows[:, BEXP, :], ALU.add)
                        v.tensor_copy(lg[:, n, :], ps[:, 2 + n % 2, D:D + NE]).then_inc(s["yF_sb"], 1)
                v.wait_ge(s["yF_sb"], NT)
                own.done(v.tensor_reduce(r16[:, 0, :], lg, AX, ALU.max))
                own.settle()
                v.tensor_tensor(fs[:, 0], lg, bc(r16[:, 0, :], NE), ALU.subtract).then_inc(s["lgF"], 1)
                tt(oh, lg, bc(r16[:, 0, :], NE), ALU.is_equal)
                own.settle()
                tt(oh, oh, desc8[:, 0, :].unsqueeze(1).broadcast_to([P, NT, NE]), ALU.mult)
                own.settle()
                own.done(v.tensor_reduce(r16[:, 1, :], oh, AX, ALU.max))
                own.settle()
                v.tensor_tensor(oh, oh, bc(r16[:, 1, :], NE), ALU.is_equal).then_inc(s["oh_ready"], 1)
                v.wait_ge(s["lgF_exp"], 1)
                own.done(v.tensor_reduce(r16[:, 2, :], fs[:, 1], AX, ALU.add))
                own.settle()
                own.done(v.reciprocal(r16[:, 3, :], r16[:, 2, :]))
                v.wait_ge(s["cum_ps"], 1)
                own.done(v.memset(fs[:, 2], 0.0))
                own.settle()
                own.done(v.tensor_copy(fs[:, 2, 1:NT, :], bank(5, NT * NE).rearrange("p (t e) -> p t e", e=NE)[:, 0:NT - 1, :]))
                own.settle()
                a, c = 2, 3
                shift = 1
                while shift < NT:
                    own.done(v.tensor_copy(fs[:, c, 0:shift, :], fs[:, a, 0:shift, :]))
                    tt(fs[:, c, shift:NT, :], fs[:, a, shift:NT, :], fs[:, a, 0:NT - shift, :], ALU.add)
                    own.settle()
                    a, c, shift = c, a, 2 * shift
                tt(fs[:, 4], fs[:, a], bank(4, NT * NE).rearrange("p (t e) -> p t e", e=NE), ALU.add)
                own.settle()
                own.done(stt(fs[:, 5], fs[:, 4], CAP, oh, ALU.is_le, ALU.mult))
                own.settle()
                own.done(v.tensor_reduce(r16[:, 4, :], fs[:, 5], AX, ALU.add))
                own.settle()
                tt(r16[:, 5, :], r16[:, 4, :], r16[:, 3, :], ALU.mult)
                own.settle()
                for T in range(NT):
                    stt(X[:, T, :], yF[:, T, :], r16[:, 5, T:T + 1], X[:, T, :], ALU.mult, ALU.add).then_inc(s["xF_ready"], 1)




def host_inputs(inp):
    import numpy as np

    A = {k: np.ascontiguousarray(np.asarray(x)) for k, x in inp.items()}
    o = {}
    o["x"] = A["x"]
    p = np.arange(P)
    o["c_ident"] = np.eye(P, dtype=np.float32)
    o["c_tri"] = (p[:, None] <= p[None, :]).astype(np.float32)
    o["c_mask16"] = (p[:, None] // DH0 == np.arange(HG)[None, :]).astype(np.float32)
    o["c_mask32"] = (p[:, None] // DH1 == np.arange(H1)[None, :]).astype(np.float32)
    o["c_sgn"] = (1.0 - 2.0 * (p[:, None] % 2)).astype(np.float32)
    o["c_desc8"] = np.tile(np.arange(NE, 0, -1, dtype=np.float32), (P, 4))
    o["c_ramps"] = np.tile(np.concatenate([R * np.arange(R), np.arange(R)]).astype(np.float32), (P, 1))
    N = L
    t, f = np.arange(N // 2)[:, None].astype(np.int64), np.arange(N // 2)[None, :].astype(np.int64)
    ang = 2 * np.pi * ((t * f) % N) / N
    fwd = np.concatenate([np.cos(ang), -np.sin(ang)], 1)
    fwd[:, N // 2] = 1.0 - 2.0 * (np.arange(N // 2) % 2)
    inv = fwd.T * 2.0 / N
    inv[0] /= 2
    inv[N // 2] /= 2
    o["c_dftf"], o["c_dfti"] = fwd.astype(np.float32), inv.astype(np.float32)
    wkv = A["L0_xattn_Wkv"].reshape(H0, 2, DH0, DC)
    bkv = A["L0_xattn_bkv"].reshape(H0, 2, DH0)
    o["wk0"], o["wv0"] = (wkv[:, i].reshape(D, DC).T for i in range(2))
    def columns(*v):
        return np.concatenate([x.reshape(-1, P) for x in v]).T

    o["bias0"] = columns(A["L0_xattn_bq"], bkv[:, 0].reshape(D), bkv[:, 1].reshape(D))
    o["ctxT"] = A["ctx_768"].reshape(NB * S2, DC).T
    o["wq0"], o["wo0"] = A["L0_xattn_Wq"].T, A["L0_xattn_Wo"].T
    o["wg0"], o["wof"] = A["L0_ffn_Wg"].T, A["L0_ffn_Wo"].T
    o["w1t"] = A["L0_ffn_W1"].transpose(0, 2, 1)
    o["b1t"] = A["L0_ffn_b1"].reshape(NE, 8, P).transpose(0, 2, 1)
    o["wq1"] = A["L1_xattn_Wq"].T
    for n in ("Wk", "Wv", "W_film_in", "W_film_out", "W1", "W2", "b2", "D_skip", "g_norm_in", "b_norm_in",
              "g_norm_out", "b_norm_out", "log_dt"):
        o["L1_xattn_" + n] = A["L1_xattn_" + n]
    o["b_film"] = np.concatenate([A["L1_xattn_b_film_in"], A["L1_xattn_b_film_out"]])[None]
    o["L0_xattn_bo"], o["L0_ffn_bo"], o["L1_ffn_b_expert"] = A["L0_xattn_bo"], A["L0_ffn_bo"], A["L1_ffn_b_expert"]
    o["gb_ffn"] = columns(A["L1_xattn_g_ffn"], A["L1_xattn_b_ffn"])
    o["b1"] = columns(A["L1_xattn_b1"])
    o["wx"] = np.concatenate([A["L1_ffn_w_expert"], A["L1_ffn_w_gate"]], 1)
    for n, k in (("k_are", "A_re"), ("k_aim", "A_im"), ("k_cre", "C_re"), ("k_cim", "C_im")):
        o[n] = A["L1_xattn_" + k].reshape(2, P, NS).transpose(0, 2, 1).reshape(P, P)
    o["mod_gate"] = A["L1_xattn_mod_gate"].reshape(1, 1)
    o["text_mask"] = A["mask_BxS_bf1"].view(np.uint8).reshape(NT, P).T
    o["vision_mask"] = A["mask_BxS2_bf1"].view(np.uint8)
    return {k: np.ascontiguousarray(x) for k, x in o.items()}


def kernel(**inputs):
    import concourse.bacc as bacc
    from concourse.bass_utils import run_bass_kernel_spmd

    nc = bacc.Bacc("TRN2", target_bir_lowering=False, num_devices=1)
    arrays = host_inputs(inputs)
    d = {k: nc.dram_tensor(f"in_{k}", a.shape, mybir.dt.from_np(a.dtype), kind="ExternalInput").ap()
         for k, a in arrays.items()}
    out = nc.dram_tensor("out", (NB, L, D), F32, kind="ExternalOutput").ap()
    build(nc, d, out)
    r = run_bass_kernel_spmd(nc, [{f"in_{k}": a for k, a in arrays.items()}], core_ids=[0])
    return r.results[0]["out"]
```

```python
import math
from contextlib import ExitStack

import concourse.bass as bass
from concourse import mybir

P = 128
NB, L, D = 2, 1024, 256
NT, TB = NB * L // P, L // P
KD = D // P
BLK = 512
NBLK = NB * L // BLK
S2, DC = 77, 192
CC = DC // 2
H0, DH0 = 16, 16
HG = 8
GW = HG * S2
BW = GW // 2
NCH = 5
NE, HID0 = 8, 512
H1, DH1, TOPK = 4, 32, 32
SW = H1 * S2
NS = 64
R = 32
HID1 = 1024
CAP = 100.0
BIAS_ROW = 96
NSEL = 2
ST = (NSEL * NB * L + NE * (P - 1)) // P
FLOOR = -0.5 + 1.0 / 512
KCH, KPARTS = 4, 9
KW = 32
ARENA = 37384
BROWS = 2 * 32 + NE
HUGE = 1.0e30
TAKEN = -3.0e38
ROUND = 1.5 * 2.0 ** 23
EPS = 1e-5

F32 = mybir.dt.float32
BF16 = mybir.dt.bfloat16
I32, U32 = mybir.dt.int32, mybir.dt.uint32
U8 = mybir.dt.uint8
ALU = mybir.AluOpType
ACT = mybir.ActivationFunctionType
AX = mybir.AxisListType.X
ENGINES = ("sync", "scalar", "vector", "gpsimd", "tensor")


class Steps:

    def __init__(self, eng, sem):
        self.eng, self.sem, self.n = eng, sem, 0

    def done(self, ins):
        self.n += 1
        ins.then_inc(self.sem, 1)

    def settle(self):
        self.eng.wait_ge(self.sem, self.n)


def build(nc, d, out, last="F"):
    ctx = ExitStack()
    with ctx:
        def sb(name, shape, dt=F32):
            return ctx.enter_context(nc.sbuf_tensor(name, shape, dt))

        def sem(name):
            return ctx.enter_context(nc.semaphore(name))

        stages = "ABCDEF"[:"ABCDEF".index(last) + 1]
        ps = ctx.enter_context(nc.psum_tensor("ps", [P, 8, BLK], F32))

        X = sb("X", [P, NT, D])
        ident = sb("ident", [P, P])
        ones = sb("ones", [P, P])
        tri = sb("tri", [P, P])
        neghalf = sb("neghalf", [P, 8])
        mask16, mask32 = sb("mask16", [P, HG]), sb("mask32", [P, H1])
        desc8 = sb("desc8", [P, 4, NE])
        ramps = sb("ramps", [P, 2, R])
        sgn = sb("sgn", [P, 1])
        halfpi = sb("halfpi", [P, 1])
        wq0, wo0 = sb("wq0", [P, KD, D]), sb("wo0", [P, KD, D])
        wk0, wv0 = sb("wk0", [CC, 2, D]), sb("wv0", [CC, 2, D])
        bias0 = sb("bias0", [P, 3, KD])
        ctxT = sb("ctxT", [CC, 2, NB * S2])
        wg0, wof = sb("wg0", [P, KD, NE]), sb("wof", [P, 4, D])
        wq1, wk1, wv1 = sb("wq1", [P, D]), sb("wk1", [CC, 2, P]), sb("wv1", [CC, 2, D])
        b1 = sb("b1", [P, HID1 // P])
        gb_ffn = sb("gb_ffn", [P, 2, KD])
        wx = sb("wx", [P, KD, D + NE])
        rows = sb("rows", [P, 9, D])
        BO0, BOF, GNI, BNI, GNO, BNO, B2, DSKIP, BEXP = range(9)
        mgate = sb("mgate", [P, 1])
        tmask8, vmask8 = sb("tmask8", [P, NT], U8), sb("vmask8", [P, NB, S2], U8)
        bstat = sb("bstat", [P, TB, 6])
        mv = sb("mv", [P, 2 * TB, 2])
        rstd = sb("rstd", [P, 2 * TB])
        arena = sb("arena", [P, ARENA])

        class Region:
            def __init__(self, at=0):
                self.at = at

            def take(self, *dims):
                n = math.prod(dims)
                v = arena[:, self.at:self.at + n]
                self.at += n
                assert self.at <= ARENA, self.at
                names = "abcd"[:len(dims)]
                if len(dims) > 1:
                    kw = {c: k for c, k in zip(names, dims)}
                    v = v.rearrange(f"p ({' '.join(names)}) -> p {' '.join(names)}", **kw)
                return v

        ra = Region()
        kblk, vblk = ra.take(2, NB, GW), ra.take(2, NB, GW)
        vwo = ra.take(NB, 2 * NCH, D)
        zA, zTA, qT = ra.take(TB, D), ra.take(KD, L), ra.take(2, L)
        Pb, PT = ra.take(4, GW), ra.take(2, NCH * P)
        kvT = ra.take(2, 2, NB * S2)
        mxA, smA = ra.take(4, HG), ra.take(4, HG)
        w1all = Region(ARENA - KD * NE * 2 * HID0).take(KD, NE, 2 * HID0)
        assert ra.at <= ARENA - KD * NE * 2 * HID0
        rb = Region()
        zB = rb.take(NT, D)
        rb.take(4 * KW * R)
        rkern = Region()
        Pr, Pi, Qr, Qi = (rkern.take(KW, R) for _ in range(4))
        tk = [rkern.take(KW * R) for _ in range(4)]
        assert rkern.at == rb.at
        KT = rb.take(R, NS)
        zTB = rb.take(2, KD, P)
        xg, xTg = rb.take(2, D), rb.take(2, KD, P)
        sig, gt, gT, yb = rb.take(2, HID0), rb.take(2, HID0), rb.take(2, 4, P), rb.take(2, D)
        yg = rb.take(2, NSEL, D)
        rt = [rb.take(NT, NE) for _ in range(12)]
        r1 = [rb.take(NT) for _ in range(8)]
        r8 = [rb.take(NE) for _ in range(6)]
        cw, pos = rb.take(NSEL, NT), rb.take(NSEL, NT)
        phi, plo = rb.take(NSEL, NT), rb.take(NSEL, NT)
        ends8, te = rb.take(ST, NE), rb.take(ST)
        idlo = rb.take(ST)
        b1s = [x.rearrange("p a b -> p (a b)") for x in (sig, gt)]
        assert rb.at <= ARENA - KD * NE * 2 * HID0
        posU, idsU = sb("posU", [P, NSEL, NT], U32), sb("idsU", [P, ST], U32)
        teI = sb("teI", [P, ST], I32)
        lowhot, hihot = sb("lowhot", [P, 4, P], BF16), sb("hihot", [P, 4, 2, ST], BF16)
        b1r = sb("b1r", [BROWS, 2 * HID0], BF16)
        picked = sb("picked", [BROWS, ST], BF16)
        erow = sb("erow", [BROWS, 1])
        iota, pcol = sb("iota", [P, P]), sb("pcol", [P, 1])
        rk = Region()
        KS0r, KS0i, KSCr, KSCi = (rk.take(4, D) for _ in range(4))
        KS0n, KSCn = rk.take(D), rk.take(D)
        DF = rk.take(4, L)
        keep_k = rk.at
        kp = sb("kp", [P, 20, P])
        tmpD = kp[:].rearrange("p a b -> p (a b)").rearrange("p (a b) -> p a b", b=D)
        rw = Region(ARENA - 3 * 2048)
        w1, w2, wfilm = rw.take(KD, HID1), rw.take(HID1 // P, D), rw.take(KD, 2, 2 * D)
        rc = Region(keep_k)
        U, XIN = rc.take(NT, D), rc.take(NT, D)
        AT, VW = rc.take(NT * P), rc.take(NB, 2, 2 * D)
        keep_c = rc.at
        uT = rc.take(KD, L)
        wqk = rc.take(KD, NB, SW)
        kb1 = rc.take(NB, SW)
        vT1 = rc.take(KD, NB * S2)
        k1T = rc.take(NB * S2)
        maskb = rc.take(NB, SW)
        tmask = rc.take(NT)
        Sc, Rk, Ex = rc.take(2, SW), rc.take(2, SW), rc.take(2, SW)
        top = rc.take(2, H1, TOPK)
        smC = rc.take(2, 3, H1)
        a77 = rc.take(2, S2)
        xn = rc.take(2, D)
        KL = rc.take(L // P, D)
        rd = Region(keep_c)
        DI = rd.take(8, BLK)
        YF = rd.take(4, 4, D)
        XS, pt_ = rd.take(4, D), rd.take(4, D)
        re_ = Region(keep_k + NT * D)
        xnE, xT = re_.take(4, D), re_.take(KD, BLK)
        hT = re_.take(HID1 // P, BLK)
        b1p = re_.take(HID1 // P)
        oE = re_.take(2, D)
        rf = Region()
        zF, zTF = rf.take(4, D), rf.take(KD, BLK)
        yF = rf.take(NT, D)
        lg, oh, fs = rf.take(NT, NE), rf.take(NT, NE), rf.take(8, NT, NE)
        r16 = rf.take(6, NT)

        scr_z = nc.dram_tensor("scr_z", [NT * P, D], F32, kind="Internal").ap()
        scr_y = nc.dram_tensor("scr_y", [ST * P, D], F32, kind="Internal").ap()
        scr_k = nc.dram_tensor("scr_k", [L, D], F32, kind="Internal").ap()

        names = """x_in consts_in wA_in wB_in wC_in wE_in rows_in kparam_in dft_in
            own_v own_p own_a stage_end acc_added
            lnA_stats lnA_rstd zA_ready zTA_ps zTA_sb qT_ps qT_sb kv_ps kv_sb kblk_ready vwo_ps vwo_sb
            scores_ready scores_read probs_exp probs_sum probs_norm pt_ps pt_sb oA_ps xA_done xbA
            lnB_stats lnB_rstd zB_ready zTB_ps zTB_sb lgB_ps lgB_exp0 lgB_exp ohB_ready cntB_ps
            hot_ready table_ps route_ready w1all_in b1_zero b1_in b1r_ready z_out
            gx0 gx1 xTg_ps xTg_sb h_ps sig_ready g_ready gT_ps gT_sb yB_ps yB_ready ys0 ys1 gy0 gy1 xB_done
            kp_exp kp_par kv_arg mag_ready k_trig k_sin k_used k_ps k_sb k_out k_in w2_in wfilm_in ks_ps ks_sb ks_done
            lnC_stats lnC_rstd u_ready uT_ps uT_sb lnU_stats lnU_rstd prepC_ps prepC_sb prepC_v sC_ps sC_read
            exC_in exC attn_ready AT_ps AT_sb film_ps xin_ready maskC vw_zero bfilm_in
            dfi_in xf_ps xf_sb xf_read pr_p pr_v yf_ready yd_ps xskip xt_ready
            lnE_stats lnE_rstd zE_ready xTE_ps xTE_sb b1p_ps b1p_sb w1s hE_ps hE_sb oE_ps oE_read
            lnO_stats lnO_rstd oE_ready xE_done
            lnF_stats lnF_rstd zF_ready zTF_ps zTF_sb yF_ps yF_sb lgF lgF_exp oh_ready cum_ps keep_ready
            xF_ready stored""".split()
        s = {n: sem(n) for n in names}

        def load(eng, dst, src, signal):
            eng.dma_start(dst, src).then_inc(s[signal], 16)

        def prow(name):
            return d[name].rearrange("(o d) -> o d", o=1).broadcast_to([P, D])

        def chunked(name, k):
            return d[name].rearrange("(k p) n -> p k n", k=k)

        block = ctx.enter_context(nc.Block())
        ends = {e: 0 for e in ENGINES}

        def stage_end(name, eng):
            ends[name] += 1
            eng.drain().then_inc(s["stage_end"], 1)
            eng.wait_ge(s["stage_end"], len(ENGINES) * ends[name])

        def ln_stats(v, own, src, n, at, signal):
            for j in range(n):
                own.done(v.bn_stats(bstat[:, j, :], src(j)))
            own.settle()
            for j in range(n):
                ins = v.bn_aggr(mv[:, at + j, :], bstat[:, j, :])
            ins.then_inc(s[signal], 1)

        def ln_rstd(p, own, n, at, stats, count, signal):
            p.wait_ge(s[stats], count)
            own.done(p.tensor_scalar(rstd[:, at:at + n], mv[:, at:at + n, 1], EPS, None, ALU.add))
            own.settle()
            p.tensor_tensor(rstd[:, at:at + n], rstd[:, at:at + n], neghalf[:, 0:n], ALU.pow).then_inc(s[signal], 1)

        def normalise(v, dst, src, k):
            return v.tensor_scalar(dst, src, mv[:, k, 0:1], rstd[:, k:k + 1], ALU.subtract, ALU.mult)

        def chan(i, c):
            v = kp[:, i, :].rearrange("p (j c) -> p j c", j=2)[:, :, c * 16:(c + 1) * 16]
            return v.unsqueeze(3).broadcast_to([P, 2, 16, R])

        def bank(i, n=BLK):
            return ps[:, i, 0:n]

        @block.sync
        def _(sp):
            load(sp, X[:], d["x"].rearrange("b (t p) n -> p (b t) n", p=P), "x_in")
            for dst, name in ((ident, "c_ident"), (tri, "c_tri"), (mask16, "c_mask16"), (mask32, "c_mask32"),
                              (sgn, "c_sgn"), (iota, "c_iota"), (pcol, "c_pcol")):
                load(sp, dst[:], d[name], "consts_in")
            load(sp, desc8[:], d["c_desc8"].rearrange("p (a b) -> p a b", a=4), "consts_in")
            load(sp, ramps[:], d["c_ramps"].rearrange("p (a b) -> p a b", a=2), "consts_in")
            load(sp, wk0[:], chunked("wk0", 2), "wA_in")
            load(sp, wv0[:], chunked("wv0", 2), "wA_in")
            load(sp, ctxT[:], chunked("ctxT", 2), "wA_in")
            load(sp, bias0[:], d["bias0"].rearrange("p (a k) -> p a k", a=3), "wA_in")
            load(sp, wq0[:], chunked("wq0", KD), "wA_in")
            load(sp, wo0[:], chunked("wo0", KD), "wA_in")
            for i, name in enumerate(("L0_xattn_bo", "L0_ffn_bo", "L1_xattn_g_norm_in", "L1_xattn_b_norm_in",
                                      "L1_xattn_g_norm_out", "L1_xattn_b_norm_out", "L1_xattn_b2",
                                      "L1_xattn_D_skip", "L1_ffn_b_expert")):
                load(sp, rows[:, i, :], prow(name), "rows_in")
            load(sp, wg0[:], chunked("wg0", KD), "wB_in")
            load(sp, wof[:], chunked("wof", 4), "wB_in")
            load(sp, erow[:], d["c_erow"], "wB_in")
            for e in range(NE):
                load(sp, w1all[:, :, e, :], d["w1t"][e].rearrange("(k p) n -> p k n", p=P), "w1all_in")
            load(sp, wq1[:], d["wq1"], "wC_in")
            load(sp, wk1[:], chunked("L1_xattn_Wk", 2), "wC_in")
            load(sp, wv1[:], chunked("L1_xattn_Wv", 2), "wC_in")
            load(sp, mgate[:], d["mod_gate"].broadcast_to([P, 1]), "wC_in")
            load(sp, tmask8[:], d["text_mask"], "wC_in")
            load(sp, vmask8[:].rearrange("p b k -> p (b k)"),
                 d["vision_mask"].rearrange("b k -> (b k)").rearrange("(o n) -> o n", o=1).broadcast_to([P, NB * S2]),
                 "wC_in")
            load(sp, b1[:], d["b1"], "wE_in")
            load(sp, gb_ffn[:], d["gb_ffn"].rearrange("p (a k) -> p a k", a=2), "wE_in")
            load(sp, wx[:], chunked("wx", KD), "wE_in")
            for i, name in enumerate(("k_are", "k_aim", "k_cre", "k_cim")):
                load(sp, kp[:, i, :], d[name], "kparam_in")
            for h in range(2):
                load(sp, kp[h * NS:(h + 1) * NS, 4, :],
                     d["L1_xattn_log_dt"][h * P:(h + 1) * P].rearrange("(o d) -> o d", o=1).broadcast_to([NS, P]),
                     "kparam_in")
            stage_end("sync", sp)
            if "B" in stages:
                sp.wait_ge(s["b1_zero"], 1)
                for i in range(3):
                    load(sp, b1s[0][32 * i:32 * i + NE, :], d["b1e"], "b1_in")
                for i in range(NBLK):
                    sp.wait_ge(s["zB_ready"], 4 * i + 4)
                    sp.dma_start(scr_z.rearrange("(t p) n -> p t n", p=P)[:, 4 * i:4 * i + 4, :], zB[:, 4 * i:4 * i + 4, :])\
                        .then_inc(s["z_out"], 16)
                for u in range(ST):
                    sp.wait_ge(s["yB_ready"], u + 1)
                    sp.dma_start(scr_y[u * P:(u + 1) * P, :], yb[:, u % 2, :]).then_inc(s[f"ys{u % 2}"], 16)
                sp.wait_ge(s["k_sb"], 2 * KCH)
                for j in range(4):
                    sp.dma_start(scr_k.rearrange("(a b) n -> a b n", b=R)[:, :, j * NS:(j + 1) * NS],
                                 KT[32 * j:32 * j + 32, :, :]).then_inc(s["k_out"], 16)
                sp.wait_ge(s["k_out"], 64)
                stage_end("sync", sp)
            if "C" in stages:
                load(sp, wfilm[:, :, 0, :], chunked("L1_xattn_W_film_in", KD), "wfilm_in")
                load(sp, wfilm[:, :, 1, :], chunked("L1_xattn_W_film_out", KD), "wfilm_in")
                load(sp, KL, scr_k.rearrange("(k p) n -> p k n", p=P), "k_in")
                load(sp, DF, d["c_dftf"].rearrange("(k p) n -> p k n", p=P), "dft_in")
                load(sp, w1, chunked("L1_xattn_W1", KD), "w2_in")
                load(sp, w2, chunked("L1_xattn_W2", HID1 // P), "w2_in")
                sp.wait_ge(s["vw_zero"], 1)
                for b in range(NB):
                    load(sp, VW[BIAS_ROW:BIAS_ROW + 1, b, :, :].rearrange("p a b -> p (a b)"), d["b_film"], "bfilm_in")
                stage_end("sync", sp)
            if "D" in stages:
                load(sp, DI, d["c_dfti"].rearrange("(k p) n -> p k n", p=P), "dfi_in")
                stage_end("sync", sp)
            if "E" in stages:
                stage_end("sync", sp)
            if "F" in stages:
                for t in range(NT):
                    sp.wait_ge(s["xF_ready"], t + 1)
                    sp.dma_start(out.rearrange("b (t p) n -> p (b t) n", p=P)[:, t, :], X[:, t, :]).then_inc(s["stored"], 16)
                sp.wait_ge(s["stored"], 16 * NT)
            else:
                sp.dma_start(out.rearrange("b (t p) n -> p (b t) n", p=P), X[:]).then_inc(s["stored"], 16)
                sp.wait_ge(s["stored"], 16)

        @block.tensor
        def _(pe):
            def mm(o, l, r, first, final):
                return pe.matmul(o, l, r, start=first, stop=final)

            pe.wait_ge(s["consts_in"], 16 * 9)
            pe.wait_ge(s["wA_in"], 16 * 6)
            for i in range(4):
                w, g = (wk0, wv0)[i // 2], i % 2
                for c in range(2):
                    ins = mm(bank(i, NB * S2), w[:, c, g * P:(g + 1) * P], ctxT[:, c, :], c == 0, c == 1)
                ins.then_inc(s["kv_ps"], 1)
            pe.wait_ge(s["kblk_ready"], 8)
            for b in range(NB):
                for g in range(2):
                    for c in range(NCH):
                        n = (b * 2 + g) * NCH + c
                        m = min(P, GW - c * P)
                        if n >= 4:
                            pe.wait_ge(s["vwo_sb"], n - 3)
                        mm(ps[0:m, 4 + n % 4, 0:D], vblk[:, g, b, c * P:c * P + m], wo0[:, g, :], True, True)\
                            .then_inc(s["vwo_ps"], 1)
            pe.wait_ge(s["vwo_sb"], 4 * NCH)
            for b in range(NB):
                for t in range(TB):
                    n = b * TB + t
                    pe.wait_ge(s["zA_ready"], n + 1)
                    if n >= 2:
                        pe.wait_ge(s["zTA_sb"], n - 1)
                    for k in range(KD):
                        ins = pe.transpose(ps[:, 6 + n % 2, k * P:(k + 1) * P], zA[:, t, k * P:(k + 1) * P], ident[:])
                    ins.then_inc(s["zTA_ps"], 1)
                pe.wait_ge(s["zTA_sb"], (b + 1) * TB)
                for h in range(2):
                    for g in range(2):
                        n = (b * 2 + h) * 2 + g
                        if n % 4 >= 2:
                            pe.wait_ge(s["qT_sb"], n - 1)
                        for k in range(KD):
                            ins = mm(bank(6 + n % 2), wq0[:, k, g * P:(g + 1) * P], zTA[:, k, h * BLK:(h + 1) * BLK],
                                     k == 0, k == KD - 1)
                        ins.then_inc(s["qT_ps"], 1)
                pe.wait_ge(s["qT_sb"], (b + 1) * 4)
                NU = 2 * TB
                for step in range(NU + 3):
                    if step < NU:
                        u, t, g = b * NU + step, step // 2, step % 2
                        if u >= 2:
                            pe.wait_ge(s["scores_read"], u - 1)
                        for c in range(2):
                            ins = mm(ps[:, 2 * (u % 2) + c, 0:BW], qT[:, g, t * P:(t + 1) * P],
                                     kblk[:, g, b, c * BW:(c + 1) * BW], True, True)
                        ins.then_inc(s["scores_ready"], 1)
                    if 0 <= step - 2 < NU:
                        u = b * NU + step - 2
                        pe.wait_ge(s["probs_norm"], u + 1)
                        if u >= 1:
                            pe.wait_ge(s["pt_sb"], u)
                        for c in range(NCH):
                            m = min(P, GW - c * P)
                            ins = pe.transpose(ps[0:m, 4 + c // 4, (c % 4) * P:(c % 4) * P + P],
                                               Pb[:, u % 4, c * P:c * P + m], ident[:])
                        ins.then_inc(s["pt_ps"], 1)
                    if 0 <= step - 3 < NU:
                        u = b * NU + step - 3
                        g, T = (step - 3) % 2, u // 2
                        pe.wait_ge(s["pt_sb"], u + 1)
                        if g == 0 and T >= 2:
                            pe.wait_ge(s["xA_done"], T - 1)
                        for c in range(NCH):
                            m = min(P, GW - c * P)
                            ins = mm(ps[:, 6 + T % 2, 0:D], PT[0:m, u % 2, c * P:(c + 1) * P], vwo[0:m, b, g * NCH + c, :],
                                     g == 0 and c == 0, g == 1 and c == NCH - 1)
                        ins.then_inc(s["oA_ps"], 1)
            stage_end("tensor", pe)
            if "B" in stages:
                pe.wait_ge(s["wB_in"], 48)
                for n in range(NT + 1):
                    if n < NT:
                        pe.wait_ge(s["zB_ready"], n + 1)
                        if n >= 2:
                            pe.wait_ge(s["zTB_sb"], n - 1)
                        for k in range(KD):
                            ins = pe.transpose(ps[:, n % 2, k * P:(k + 1) * P], zB[:, n, k * P:(k + 1) * P], ident[:])
                        ins.then_inc(s["zTB_ps"], 1)
                    if n >= 1:
                        pe.wait_ge(s["zTB_sb"], n)
                        for k in range(KD):
                            ins = mm(ps[:, 2, (n - 1) * NE:n * NE], zTB[:, (n - 1) % 2, k, :], wg0[:, k, :], k == 0, k == KD - 1)
                        ins.then_inc(s["lgB_ps"], 1)
                pe.wait_ge(s["ohB_ready"], 1)
                ohf = rt[7].rearrange("p t e -> p (t e)")
                mm(bank(4, NT * NE), tri[:], ohf, True, True)
                mm(bank(5, NT * NE), ones[:], ohf, True, True).then_inc(s["cntB_ps"], 1)
                for n in range(NSEL * NT):
                    pe.wait_ge(s["hot_ready"], n + 1)
                    mm(bank(6, 2 * ST), lowhot[:, n % 4, :], hihot[:, n % 4, :, :].rearrange("p a b -> p (a b)"),
                       n == 0, n == NSEL * NT - 1).then_inc(s["table_ps"], 1)
                pe.wait_ge(s["route_ready"], 1)
                pe.wait_ge(s["w1all_in"], 16 * NE)
                pe.wait_ge(s["b1r_ready"], 3)

                def turn_x(u):
                    pe.wait_ge(s[f"gx{u % 2}"], 16 * (u // 2 + 1))
                    if u:
                        pe.wait_ge(s["xTg_sb"], u)
                    for k in range(KD):
                        ins = pe.transpose(ps[:, 6, k * P:(k + 1) * P],
                                           xg[:, u % 2, k * P:(k + 1) * P], ident[:])
                    ins.then_inc(s["xTg_ps"], 1)

                turn_x(0)
                for st in range(ST + 2):
                    if st < ST:
                        u = st
                        e = pe.value_load(teI[0:1, u:u + 1], min_val=0, max_val=NE - 1)
                        pe.wait_ge(s["xTg_sb"], u + 1)
                        if u >= 2:
                            pe.wait_ge(s["g_ready"], u - 1)
                        for half in range(2):
                            cols = slice(half * HID0, (half + 1) * HID0)
                            o = bank(2 * (u % 2) + half)
                            mm(o, picked[:, u:u + 1].broadcast_to([BROWS, P]), b1r[:, cols], True, False)
                            for k in range(KD):
                                ins = mm(o, xTg[:, u % 2, k, :],
                                         w1all[:, k, bass.ds(e, 1), cols].rearrange("p o n -> p (o n)"), False, k == KD - 1)
                        ins.then_inc(s["h_ps"], 1)
                        if u + 1 < ST:
                            turn_x(u + 1)
                    if 0 <= st - 1 < ST:
                        u = st - 1
                        pe.wait_ge(s["g_ready"], u + 1)
                        if u >= 1:
                            pe.wait_ge(s["gT_sb"], u)
                        for f in range(4):
                            ins = pe.transpose(ps[:, 4, f * P:(f + 1) * P], gt[:, u % 2, f * P:(f + 1) * P], ident[:])
                        ins.then_inc(s["gT_ps"], 1)
                    if 0 <= st - 2 < ST:
                        u = st - 2
                        pe.wait_ge(s["gT_sb"], u + 1)
                        if u:
                            pe.wait_ge(s["yB_ready"], u)
                        for f in range(4):
                            ins = mm(ps[:, 5, 0:D], gT[:, u % 2, f, :], wof[:, f, :], f == 0, f == 3)
                        ins.then_inc(s["yB_ps"], 1)
                    c, h = st // KPARTS - 1, st % KPARTS
                    if 0 <= c < KCH and h < 2:
                        pe.wait_ge(s["k_used"], 2 * (c + 1))
                        if 2 * c + h:
                            pe.wait_ge(s["k_sb"], 2 * c + h)
                        half_rows = slice(64 * h, 64 * h + 64)
                        for c16 in range(16):
                            for jj in range(2):
                                j, w = 2 * h + jj, jj * 16 + c16
                                o = ps[32 * j:32 * j + 32, 7, c16 * R:(c16 + 1) * R]
                                mm(o, Pr[half_rows, w, :], Qr[half_rows, w, :], True, False)
                                ins = mm(o, Pi[half_rows, w, :], Qi[half_rows, w, :], False, True)
                        ins.then_inc(s["k_ps"], 1)
                stage_end("tensor", pe)
            if "C" in stages:
                pe.wait_ge(s["wC_in"], 16 * 6)
                for c in range(2):
                    ins = mm(bank(0, NB * S2), wk1[:, c, :], ctxT[:, c, :], c == 0, c == 1)
                ins.then_inc(s["prepC_ps"], 1)
                for g in range(2):
                    for c in range(2):
                        ins = mm(bank(1 + g, NB * S2), wv1[:, c, g * P:(g + 1) * P], ctxT[:, c, :], c == 0, c == 1)
                    ins.then_inc(s["prepC_ps"], 1)
                pe.wait_ge(s["prepC_v"], 2)
                for b in range(NB):
                    for g in range(2):
                        mm(bank(4 + 2 * b + g, SW), wq1[:, g * P:(g + 1) * P], kb1[:, b, :], True, True)\
                            .then_inc(s["prepC_ps"], 1)
                pe.wait_ge(s["prepC_sb"], 7)
                pe.wait_ge(s["wfilm_in"], 32)
                for b in range(NB):
                    for io in range(2):
                        for g in range(2):
                            ins = mm(ps[0:S2, 2 * b + io, :], vT1[:, g, b * S2:(b + 1) * S2], wfilm[:, g, io, :], g == 0, g == 1)
                        ins.then_inc(s["prepC_ps"], 1)
                pe.wait_ge(s["prepC_v"], 6)
                for b in range(NB):
                    for t in range(TB):
                        n = b * TB + t
                        pe.wait_ge(s["u_ready"], n + 1)
                        if n >= 2:
                            pe.wait_ge(s["uT_sb"], n - 1)
                        for k in range(KD):
                            ins = pe.transpose(ps[:, n % 2, k * P:(k + 1) * P], U[:, n, k * P:(k + 1) * P], ident[:])
                        ins.then_inc(s["uT_ps"], 1)
                    for step in range(TB + 1):
                        if step < TB:
                            n, t = b * TB + step, step
                            pe.wait_ge(s["uT_sb"], n + 1)
                            if n >= 2:
                                pe.wait_ge(s["sC_read"], n - 1)
                            for k in range(KD):
                                ins = mm(bank(2 + n % 2, SW), uT[:, k, t * P:(t + 1) * P], wqk[:, k, b, :], k == 0, k == KD - 1)
                            ins.then_inc(s["sC_ps"], 1)
                        if step >= 1:
                            n = b * TB + step - 1
                            pe.wait_ge(s["attn_ready"], n + 1)
                            if n:
                                pe.wait_ge(s["AT_sb"], n)
                            pe.transpose(ps[0:S2, 4, 0:P], a77[:, n % 2, :], ident[:]).then_inc(s["AT_ps"], 1)
                            pe.wait_ge(s["AT_sb"], n + 1)
                            if n >= 2:
                                pe.wait_ge(s["xin_ready"], n - 1)
                            mm(bank(6 + n % 2), AT[0:BIAS_ROW + 1, n * P:(n + 1) * P], VW[0:BIAS_ROW + 1, b, 0, :], True, True)\
                                .then_inc(s["film_ps"], 1)
                            if b == 0:
                                m = step - 1
                                if m == 0:
                                    pe.wait_ge(s["k_in"], 16)
                                    pe.wait_ge(s["dft_in"], 16)
                                else:
                                    pe.wait_ge(s["ks_done"], m)
                                for k in range(4):
                                    ins = mm(bank(5), DF[:, k, m * P:(m + 1) * P],
                                             KL.rearrange("p (j k) n -> p j k n", j=2)[:, :, k, :], k == 0, k == 3)
                                ins.then_inc(s["ks_ps"], 1)
                stage_end("tensor", pe)
            if "D" in stages:
                for b in range(NB):
                    for m in range(4):
                        n = b * 4 + m
                        if n:
                            pe.wait_ge(s["xf_sb"], n)
                        for j in range(2):
                            for ri in range(2):
                                for k in range(4):
                                    ins = mm(ps[:, 2 * j + ri, 0:D], DF[:, k, (4 * ri + m) * P:(4 * ri + m + 1) * P],
                                             XIN[:, b * TB + 4 * j + k, :], k == 0, k == 3)
                        ins.then_inc(s["xf_ps"], 1)
                    pe.wait_ge(s["yf_ready"], 4 * (b + 1))
                    pe.wait_ge(s["dfi_in"], 16)
                    for t in range(TB):
                        n, j, k = b * TB + t, t // 4, t % 4
                        if n >= 2:
                            pe.wait_ge(s["xt_ready"], n - 1)
                        for m in range(8):
                            mm(ps[:, 4 + n % 2, 0:D], DI[:, m, k * P:(k + 1) * P], YF[:, m % 4, 2 * j + m // 4, :], m == 0, m == 7)
                        mm(bank(6 + n % 2), AT[0:BIAS_ROW + 1, n * P:(n + 1) * P], VW[0:BIAS_ROW + 1, b, 1, :], True, True)\
                            .then_inc(s["yd_ps"], 1)
                stage_end("tensor", pe)
            if "E" in stages:
                pe.wait_ge(s["wE_in"], 16 * 3)
                pe.wait_ge(s["w2_in"], 32)
                for f in range(HID1 // P):
                    for k in range(KD):
                        ins = mm(ps[:, 7, f:f + 1], w1[:, k, f * P:(f + 1) * P], gb_ffn[:, 1, k:k + 1], k == 0, k == 1)
                ins.then_inc(s["b1p_ps"], 1)
                pe.wait_ge(s["w1s"], 1)
                for i in range(NBLK):
                    for t in range(4):
                        n = i * 4 + t
                        pe.wait_ge(s["zE_ready"], n + 1)
                        if n >= 2:
                            pe.wait_ge(s["xTE_sb"], n - 1)
                        for k in range(KD):
                            ins = pe.transpose(ps[:, n % 2, k * P:(k + 1) * P], xnE[:, t, k * P:(k + 1) * P], ident[:])
                        ins.then_inc(s["xTE_ps"], 1)
                    pe.wait_ge(s["xTE_sb"], 4 * i + 4)
                    for f in range(HID1 // P):
                        n = i * 8 + f
                        if n >= 2:
                            pe.wait_ge(s["hE_sb"], n - 1)
                        for k in range(KD):
                            ins = mm(bank(2 + n % 2), w1[:, k, f * P:(f + 1) * P], xT[:, k, :], k == 0, k == KD - 1)
                        ins.then_inc(s["hE_ps"], 1)
                    pe.wait_ge(s["hE_sb"], 8 * i + 8)
                    for t in range(4):
                        n = i * 4 + t
                        if n >= 2:
                            pe.wait_ge(s["oE_read"], n - 1)
                        for f in range(HID1 // P):
                            ins = mm(ps[:, 4 + n % 2, 0:D], hT[:, f, t * P:(t + 1) * P], w2[:, f, :], f == 0, f == 7)
                        ins.then_inc(s["oE_ps"], 1)
                stage_end("tensor", pe)
            if "F" in stages:
                for i in range(NBLK):
                    for t in range(4):
                        n = i * 4 + t
                        pe.wait_ge(s["zF_ready"], n + 1)
                        if n >= 2:
                            pe.wait_ge(s["zTF_sb"], n - 1)
                        for k in range(KD):
                            ins = pe.transpose(ps[:, n % 2, k * P:(k + 1) * P], zF[:, t, k * P:(k + 1) * P], ident[:])
                        ins.then_inc(s["zTF_ps"], 1)
                    for t in range(4):
                        n = i * 4 + t
                        pe.wait_ge(s["zTF_sb"], n + 1)
                        if n >= 2:
                            pe.wait_ge(s["yF_sb"], n - 1)
                        for k in range(KD):
                            ins = mm(ps[:, 2 + n % 2, 0:D + NE], zTF[:, k, t * P:(t + 1) * P], wx[:, k, :], k == 0, k == KD - 1)
                        ins.then_inc(s["yF_ps"], 1)
                pe.wait_ge(s["oh_ready"], 1)
                ohf = oh.rearrange("p t e -> p (t e)")
                mm(bank(4, NT * NE), tri[:], ohf, True, True)
                mm(bank(5, NT * NE), ones[:], ohf, True, True).then_inc(s["cum_ps"], 1)

        @block.scalar
        def _(a):
            own = Steps(a, s["own_a"])

            def copy(o, i):
                return a.activation(o, i, ACT.Copy)

            for i in range(4):
                a.wait_ge(s["kv_ps"], i + 1)
                if i == 0:
                    a.wait_ge(s["wA_in"], 16 * 6)
                a.activation(kvT[:, i // 2, i % 2, :], bank(i, NB * S2), ACT.Identity,
                             bias=bias0[:, 1 + i // 2, i % 2:i % 2 + 1]).then_inc(s["kv_sb"], 1)
            for b in range(NB):
                for g in range(2):
                    for c in range(NCH):
                        n, m = (b * 2 + g) * NCH + c, min(P, GW - c * P)
                        a.wait_ge(s["vwo_ps"], n + 1)
                        copy(vwo[0:m, b, g * NCH + c, :], ps[0:m, 4 + n % 4, 0:D]).then_inc(s["vwo_sb"], 1)
            for b in range(NB):
                for t in range(TB):
                    n = b * TB + t
                    a.wait_ge(s["zTA_ps"], n + 1)
                    copy(zTA[:, :, t * P:(t + 1) * P], ps[:, 6 + n % 2, 0:D].rearrange("p (k c) -> p k c", k=KD))\
                        .then_inc(s["zTA_sb"], 1)
                for h in range(2):
                    for g in range(2):
                        n = (b * 2 + h) * 2 + g
                        a.wait_ge(s["qT_ps"], n + 1)
                        a.activation(qT[:, g, h * BLK:(h + 1) * BLK], bank(6 + n % 2), ACT.Identity,
                                     bias=bias0[:, 0, g:g + 1]).then_inc(s["qT_sb"], 1)
                NU = 2 * TB
                for step in range(NU + 2):
                    if step < NU:
                        u = b * NU + step
                        a.wait_ge(s["scores_read"], u + 1)
                        a.activation(Pb[:, u % 4, :], Pb[:, u % 4, :], ACT.Exp, scale=1.0 / math.sqrt(DH0))\
                            .then_inc(s["probs_exp"], 1)
                    if step >= 2:
                        u = b * NU + step - 2
                        a.wait_ge(s["pt_ps"], u + 1)
                        if u >= 2:
                            a.wait_ge(s["oA_ps"], u - 1)
                        last_rows = GW - 4 * P
                        own.done(copy(PT[:, u % 2, 0:4 * P], bank(4)))
                        copy(PT[0:last_rows, u % 2, 4 * P:5 * P], ps[0:last_rows, 5, 0:P]).then_inc(s["pt_sb"], 1)
            stage_end("scalar", a)
            if "B" in stages:
                for n in range(NT):
                    a.wait_ge(s["zTB_ps"], n + 1)
                    if n >= 2:
                        a.wait_ge(s["lgB_ps"], n - 1)
                    copy(zTB[:, n % 2, :, :], ps[:, n % 2, 0:D].rearrange("p (k c) -> p k c", k=KD)).then_inc(s["zTB_sb"], 1)
                    if n == 4:
                        a.wait_ge(s["kparam_in"], 16 * 6)
                        a.activation(kp[:, 5, :], kp[:, 4, :], ACT.Exp).then_inc(s["kp_exp"], 1)
                a.wait_ge(s["kp_par"], 1)
                a.activation(kp[:, 8, :], kp[:, 6, :], ACT.Tanh, scale=0.5).then_inc(s["kp_exp"], 1)
                a.wait_ge(s["kp_par"], 2)
                two_pi = 2 * math.pi
                own.done(a.activation(kp[:, 10, :], kp[:, 7, :], ACT.Sin, scale=two_pi))
                own.done(a.activation(kp[:, 11, :], kp[:, 9, :], ACT.Sin, scale=-two_pi, bias=halfpi[:]))
                a.activation(kp[:, 12, :], kp[:, 7, :], ACT.Sin, scale=math.pi).then_inc(s["kp_exp"], 1)
                a.wait_ge(s["lgB_exp0"], 1)
                a.activation(rt[1], rt[0], ACT.Exp).then_inc(s["lgB_exp"], 1)

                def put_x(u):
                    a.wait_ge(s["xTg_ps"], u + 1)
                    if u >= 2:
                        a.wait_ge(s["h_ps"], u - 1)
                    copy(xTg[:, u % 2, :, :].rearrange("p k c -> p (k c)"), ps[:, 6, 0:D])\
                        .then_inc(s["xTg_sb"], 1)

                put_x(0)
                for st in range(ST + 2):
                    if st < ST:
                        u = st
                        a.wait_ge(s["h_ps"], u + 1)
                        if u >= 2:
                            a.wait_ge(s["g_ready"], u - 1)
                        a.activation(sig[:, u % 2, :], bank(2 * (u % 2) + 1), ACT.Sigmoid).then_inc(s["sig_ready"], 1)
                        if u + 1 < ST:
                            put_x(u + 1)
                    if 0 <= st - 1 < ST:
                        u = st - 1
                        a.wait_ge(s["gT_ps"], u + 1)
                        if u >= 2:
                            a.wait_ge(s["yB_ps"], u - 1)
                        copy(gT[:, u % 2, :, :].rearrange("p f c -> p (f c)"), bank(4)).then_inc(s["gT_sb"], 1)
                    c, part = st // KPARTS, st % KPARTS
                    if 1 <= c <= KCH and part < 2:
                        a.wait_ge(s["k_ps"], 2 * (c - 1) + part + 1)
                        rowsk = slice(64 * part, 64 * part + 64)
                        copy(KT[rowsk, :, (c - 1) * 16:c * 16].rearrange("p b c -> p c b"),
                             ps[rowsk, 7, :].rearrange("p (c b) -> p c b", b=R)).then_inc(s["k_sb"], 1)
                    if c < KCH and part == 2:
                        a.wait_ge(s["k_trig"], 2 * c + 2)
                        for i in range(2):
                            own.done(a.activation(tk[2 * i], tk[2 * i], ACT.Sin, scale=two_pi))
                            ins = a.activation(tk[2 * i + 1], tk[2 * i + 1], ACT.Sin, scale=-two_pi, bias=halfpi[:])
                            ins.then_inc(s["k_sin"], 1)
                    if c < KCH and part == 3:
                        a.wait_ge(s["kv_arg"], 2 * c + 2)
                        for mag in (Pr, Qr):
                            a.activation(mag, mag, ACT.Exp).then_inc(s["mag_ready"], 1)
                stage_end("scalar", a)
            if "C" in stages:
                a.wait_ge(s["prepC_ps"], 1)
                copy(k1T[:, :], bank(0, NB * S2)).then_inc(s["prepC_sb"], 1)
                for g in range(2):
                    a.wait_ge(s["prepC_ps"], 2 + g)
                    copy(vT1[:, g, :], bank(1 + g, NB * S2)).then_inc(s["prepC_sb"], 1)
                for b in range(NB):
                    for g in range(2):
                        a.wait_ge(s["prepC_ps"], 4 + 2 * b + g)
                        copy(wqk[:, g, b, :], bank(4 + 2 * b + g, SW)).then_inc(s["prepC_sb"], 1)
                for b in range(NB):
                    for t in range(TB):
                        n = b * TB + t
                        a.wait_ge(s["uT_ps"], n + 1)
                        if b and t == 0:
                            a.wait_ge(s["sC_ps"], TB)
                        copy(uT[:, :, t * P:(t + 1) * P], ps[:, n % 2, 0:D].rearrange("p (k c) -> p k c", k=KD))\
                            .then_inc(s["uT_sb"], 1)
                    for t in range(TB):
                        n = b * TB + t
                        a.wait_ge(s["exC_in"], n + 1)
                        a.activation(Ex[:, n % 2, :], Ex[:, n % 2, :], ACT.Exp).then_inc(s["exC"], 1)
                        a.wait_ge(s["AT_ps"], n + 1)
                        if n == 0:
                            a.wait_ge(s["maskC"], 1)
                        copy(AT[0:S2, n * P:(n + 1) * P], ps[0:S2, 4, 0:P]).then_inc(s["AT_sb"], 1)
                        if b == 0:
                            a.wait_ge(s["ks_ps"], t + 1)
                            copy((KS0r, KS0i)[t // 4][:, t % 4, :], ps[:, 5, 0:D]).then_inc(s["ks_sb"], 1)
                stage_end("scalar", a)
            if "D" in stages:
                for n in range(NB * 4):
                    a.wait_ge(s["xf_ps"], n + 1)
                    if n:
                        a.wait_ge(s["yf_ready"], n)
                    copy(XS, ps[:, 0:4, 0:D]).then_inc(s["xf_sb"], 1)
                stage_end("scalar", a)
            if "E" in stages:
                for i in range(NBLK):
                    for t in range(4):
                        n = i * 4 + t
                        a.wait_ge(s["xTE_ps"], n + 1)
                        if t == 0 and i:
                            a.wait_ge(s["hE_ps"], 8 * i)
                        copy(xT[:, :, t * P:(t + 1) * P], ps[:, n % 2, 0:D].rearrange("p (k c) -> p k c", k=KD))\
                            .then_inc(s["xTE_sb"], 1)
                    for f in range(HID1 // P):
                        n = i * 8 + f
                        a.wait_ge(s["hE_ps"], n + 1)
                        if n == 0:
                            a.wait_ge(s["b1p_sb"], 1)
                        if f == 0 and i:
                            a.wait_ge(s["oE_ps"], 4 * i)
                        a.activation(hT[:, f, :], bank(2 + n % 2), ACT.Gelu, bias=b1p[:, f:f + 1]).then_inc(s["hE_sb"], 1)
                stage_end("scalar", a)
            if "F" in stages:
                for i in range(NBLK):
                    for t in range(4):
                        n = i * 4 + t
                        a.wait_ge(s["zTF_ps"], n + 1)
                        if t == 0 and i:
                            a.wait_ge(s["yF_ps"], 4 * i)
                        copy(zTF[:, :, t * P:(t + 1) * P], ps[:, n % 2, 0:D].rearrange("p (k c) -> p k c", k=KD))\
                            .then_inc(s["zTF_sb"], 1)
                a.wait_ge(s["lgF"], 1)
                a.activation(fs[:, 1], fs[:, 0], ACT.Exp).then_inc(s["lgF_exp"], 1)

        @block.gpsimd
        def _(p):
            own = Steps(p, s["own_p"])
            own.done(p.memset(neghalf[:], -0.5))
            own.done(p.memset(ones[:], 1.0))
            own.done(p.memset(halfpi[:], math.pi / 2))
            own.settle()
            p.wait_ge(s["rows_in"], 16 * 9)
            for b in range(NB):
                ln_rstd(p, own, TB, 0, "lnA_stats", b + 1, "lnA_rstd")
                p.wait_ge(s["zA_ready"], (b + 1) * TB)
                for t in range(TB):
                    T = b * TB + t
                    p.tensor_tensor(X[:, T, :], X[:, T, :], rows[:, BO0, :], ALU.add).then_inc(s["xbA"], 1)
                for st in range(2 * TB):
                    u = b * 2 * TB + st
                    p.wait_ge(s["probs_sum"], u + 1)
                    pv = Pb[:, u % 4, :].rearrange("p (h k) -> p h k", h=HG)
                    p.tensor_tensor(pv, pv, smA[:, u % 4, :].unsqueeze(2).broadcast_to([P, HG, S2]), ALU.mult)\
                        .then_inc(s["probs_norm"], 1)
            stage_end("gpsimd", p)
            if "B" in stages:
                for i in range(2):
                    ln_rstd(p, own, TB, TB * i, "lnB_stats", i + 1, "lnB_rstd")
                p.wait_ge(s["route_ready"], 1)
                p.wait_ge(s["z_out"], 16 * NBLK)
                for st in range(ST):
                    if st >= 2:
                        p.wait_ge(s["xTg_ps"], st - 1)
                    p.indirect_dma_start(xg[:, st % 2, :], None, scr_z,
                                         bass.IndirectOffsetOnAxis(ap=idsU[:, st:st + 1], axis=0)).then_inc(s[f"gx{st % 2}"], 16)
                    c, part = st // KPARTS, st % KPARTS
                    if c < KCH and part == 2:
                        if c:
                            p.wait_ge(s["k_ps"], 2 * c)
                        for i, dst in enumerate((Pr, Qr)):
                            p.tensor_tensor(dst.rearrange("p (j c) r -> p j c r", j=2), chan(6, c),
                                            ramps[:, i, :].unsqueeze(1).unsqueeze(1).broadcast_to([P, 2, 16, R]), ALU.mult)\
                                .then_inc(s["kv_arg"], 1)
                for i in range(2):
                    p.wait_ge(s[f"ys{i}"], 16 * ((ST + 1 - i) // 2))
                for T in range(NT):
                    if T >= 2:
                        p.wait_ge(s["xB_done"], T - 1)
                    for k in range(NSEL):
                        p.indirect_dma_start(yg[:, T % 2, k, :], None, scr_y,
                                             bass.IndirectOffsetOnAxis(ap=posU[:, k, T:T + 1], axis=0))\
                            .then_inc(s[f"gy{T % 2}"], 16)
                stage_end("gpsimd", p)
            if "C" in stages:
                own.done(p.memset(AT[:, :], 0.0))
                own.settle()
                p.memset(AT[BIAS_ROW:BIAS_ROW + 1, :], 1.0).then_inc(s["maskC"], 1)
                p.wait_ge(s["maskC"], 1)
                for b in range(NB):
                    ln_rstd(p, own, TB, 0, "lnC_stats", b + 1, "lnC_rstd")
                    ln_rstd(p, own, TB, TB, "lnU_stats", b + 1, "lnU_rstd")
                stage_end("gpsimd", p)
            if "D" in stages:
                for b in range(NB):
                    for m in range(4):
                        n = b * 4 + m
                        p.wait_ge(s["xf_sb"], n + 1)
                        if n:
                            p.wait_ge(s["yf_ready"], n)
                        kn = KS0n if m == 0 else KS0r[:, m, :]
                        p.tensor_tensor(pt_[:, 0, :], XS[:, 2, :], KS0r[:, m, :], ALU.mult).then_inc(s["pr_p"], 1)
                        p.tensor_tensor(pt_[:, 1, :], XS[:, 3, :], KS0i[:, m, :], ALU.mult).then_inc(s["pr_p"], 1)
                        p.tensor_tensor(pt_[:, 2, :], XS[:, 2, :], KS0i[:, m, :], ALU.mult).then_inc(s["pr_p"], 1)
                        p.tensor_tensor(pt_[:, 3, :], XS[:, 3, :], kn, ALU.mult).then_inc(s["pr_p"], 1)
                    p.wait_ge(s["xf_ps"], 4 * b + 4)
                    for t in range(TB):
                        T = b * TB + t
                        p.tensor_tensor(XIN[:, T, :], XIN[:, T, :], rows[:, DSKIP, :], ALU.mult).then_inc(s["xskip"], 1)
                stage_end("gpsimd", p)
            if "E" in stages:
                for i in range(NBLK):
                    ln_rstd(p, own, 4, 0, "lnE_stats", i + 1, "lnE_rstd")
                    for t in range(4):
                        n = i * 4 + t
                        ln_rstd(p, own, 1, 8 + n % 2, "lnO_stats", n + 1, "lnO_rstd")
                        p.wait_ge(s["oE_ready"], n + 1)
                        own.done(p.tensor_tensor(oE[:, n % 2, :], oE[:, n % 2, :], rows[:, GNO, :], ALU.mult))
                        own.settle()
                        own.done(p.tensor_tensor(oE[:, n % 2, :], oE[:, n % 2, :], rows[:, BNO, :], ALU.add))
                        own.settle()
                        p.tensor_tensor(X[:, n, :], X[:, n, :], oE[:, n % 2, :], ALU.add).then_inc(s["xE_done"], 1)
                stage_end("gpsimd", p)
            if "F" in stages:
                for i in range(NBLK):
                    ln_rstd(p, own, 4, 0, "lnF_stats", i + 1, "lnF_rstd")

        @block.vector
        def _(v):
            own = Steps(v, s["own_v"])

            def tt(o, x, y, op):
                own.done(v.tensor_tensor(o, x, y, op))

            def ts(o, x, c1, c2, op0, op1=ALU.bypass):
                own.done(v.tensor_scalar(o, x, c1, c2, op0, op1) if c2 is not None else v.tensor_scalar(o, x, c1, None, op0))

            def stt(o, x, c, y, op0, op1):
                return v.scalar_tensor_tensor(out=o, in0=x, scalar=c, in1=y, op0=op0, op1=op1)

            def bc(x, n):
                return x.unsqueeze(2).broadcast_to([x.shape[0], x.shape[1], n])

            def earlier_tiles(a, b, totals):
                own.done(v.memset(a, 0.0))
                own.settle()
                own.done(v.tensor_copy(a[:, 1:NT, :], totals[:, 0:NT - 1, :]))
                own.settle()
                shift = 1
                while shift < NT:
                    own.done(v.tensor_copy(b[:, 0:shift, :], a[:, 0:shift, :]))
                    tt(b[:, shift:NT, :], a[:, shift:NT, :], a[:, 0:NT - shift, :], ALU.add)
                    own.settle()
                    a, b, shift = b, a, 2 * shift
                return a

            v.wait_ge(s["consts_in"], 16 * 9)
            for i in range(2):
                for g in range(2):
                    v.wait_ge(s["kv_sb"], 2 * i + g + 1)
                    for b in range(NB):
                        v.tensor_tensor((kblk, vblk)[i][:, g, b, :].rearrange("p (h k) -> p h k", h=HG),
                                        kvT[:, i, g, b * S2:(b + 1) * S2].unsqueeze(1).broadcast_to([P, HG, S2]),
                                        bc(mask16[:], S2), ALU.mult).then_inc(s["kblk_ready"], 1)
            v.wait_ge(s["x_in"], 16)
            for b in range(NB):
                ln_stats(v, own, lambda j: X[:, b * TB + j, :], TB, 0, "lnA_stats")
                v.wait_ge(s["lnA_rstd"], b + 1)
                if b:
                    v.wait_ge(s["zTA_ps"], TB)
                for t in range(TB):
                    normalise(v, zA[:, t, :], X[:, b * TB + t, :], t).then_inc(s["zA_ready"], 1)
                NU = 2 * TB
                for step in range(NU + 4):
                    if step < NU:
                        u = b * NU + step
                        sv = ps[:, 2 * (u % 2):2 * (u % 2) + 2, 0:BW].rearrange("p c (h k) -> p c h k", k=S2)
                        v.wait_ge(s["scores_ready"], u + 1)
                        own.done(v.tensor_reduce(mxA[:, u % 4, :].rearrange("p (c h) -> p c h", c=2), sv, AX, ALU.max))
                        own.settle()
                        if u >= 4:
                            v.wait_ge(s["pt_ps"], u - 3)
                        v.tensor_tensor(Pb[:, u % 4, :].rearrange("p (c h k) -> p c h k", c=2, h=4), sv,
                                        mxA[:, u % 4, :].rearrange("p (c h) -> p c h", c=2).unsqueeze(3)
                                        .broadcast_to([P, 2, 4, S2]), ALU.subtract).then_inc(s["scores_read"], 1)
                    if 1 <= step <= NU:
                        u = b * NU + step - 1
                        v.wait_ge(s["probs_exp"], u + 1)
                        own.done(v.tensor_reduce(smA[:, u % 4, :], Pb[:, u % 4, :].rearrange("p (h k) -> p h k", h=HG), AX, ALU.add))
                        own.settle()
                        v.reciprocal(smA[:, u % 4, :], smA[:, u % 4, :]).then_inc(s["probs_sum"], 1)
                    if step >= 4 and step % 2 == 1:
                        T = b * TB + (step - 5) // 2
                        v.wait_ge(s["oA_ps"], 2 * T + 2)
                        v.wait_ge(s["xbA"], T + 1)
                        v.tensor_tensor(X[:, T, :], X[:, T, :], ps[:, 6 + T % 2, 0:D], ALU.add).then_inc(s["xA_done"], 1)
            stage_end("vector", v)
            if "B" in stages:
                v.memset(b1s[0], 0.0).then_inc(s["b1_zero"], 1)
                for i in range(2):
                    ln_stats(v, own, lambda j: X[:, i * TB + j, :], TB, TB * i, "lnB_stats")
                    v.wait_ge(s["lnB_stats"], i + 1)
                for i in range(2):
                    v.wait_ge(s["lnB_rstd"], i + 1)
                    for t in range(TB):
                        n = i * TB + t
                        normalise(v, zB[:, n, :], X[:, n, :], n).then_inc(s["zB_ready"], 1)
                v.wait_ge(s["b1_in"], 48)
                for i in range(3):
                    x, rest = b1s[i % 2], b1s[(i + 1) % 2]
                    if i == 1:
                        own.done(v.tensor_copy(b1r[32:64, :], x[32:64, :]))
                    part = slice(64 if i else 0, BROWS)
                    v.tensor_copy(b1r[part, :], x[part, :]).then_inc(s["b1r_ready"], 1)
                    v.wait_ge(s["b1r_ready"], i + 1)
                    if i < 2:
                        tt(rest[part, :], x[part, :], b1r[part, :], ALU.subtract)
                        own.settle()
                ARE, AIM, CRE, CIM, LOGDT, DT, AR, TURN, TH, ABS, SIN, COS, SINH = range(13)
                q = lambda i: kp[:, i, :]

                def op(o, x, y, kind):
                    tt(q(o), q(x), q(y), kind)
                    own.settle()

                def turns(o, r, x):
                    ts(r, x, ROUND, -ROUND, ALU.add, ALU.add)
                    own.settle()
                    tt(o, x, r, ALU.subtract)
                    own.settle()

                v.wait_ge(s["kparam_in"], 16 * 6)
                v.wait_ge(s["kp_exp"], 1)
                v.tensor_tensor(q(AR), q(DT), q(ARE), ALU.mult).then_inc(s["kp_par"], 1)
                op(13, DT, AIM, ALU.mult)
                ts(q(13), q(13), 1 / (2 * math.pi), None, ALU.mult)
                own.settle()
                turns(q(TURN), q(14), q(13))
                stt(q(ABS), q(TURN), -1.0, q(TURN), ALU.mult, ALU.max).then_inc(s["kp_par"], 1)
                v.wait_ge(s["kp_exp"], 2)
                ts(q(13), q(TH), -1.0, 1.0, ALU.mult, ALU.add)
                own.settle()
                own.done(v.reciprocal(q(14), q(13)))
                own.settle()
                own.done(stt(q(14), q(TH), 2.0, q(14), ALU.mult, ALU.mult))
                own.settle()
                ts(q(15), q(14), 1.0, None, ALU.add)
                v.wait_ge(s["kp_exp"], 3)
                own.done(stt(q(16), q(SINH), -2.0, q(SINH), ALU.mult, ALU.mult))
                op(17, 14, COS, ALU.mult)
                op(16, 16, 17, ALU.add)
                op(17, 15, SIN, ALU.mult)
                op(13, ARE, ARE, ALU.mult)
                op(18, AIM, AIM, ALU.mult)
                op(13, 13, 18, ALU.add)
                own.done(v.reciprocal(q(13), q(13)))
                op(14, 16, ARE, ALU.mult)
                op(15, 17, AIM, ALU.mult)
                op(18, 17, ARE, ALU.mult)
                op(19, 16, AIM, ALU.mult)
                op(14, 14, 15, ALU.add)
                op(18, 18, 19, ALU.subtract)
                op(14, 14, 13, ALU.mult)
                op(18, 18, 13, ALU.mult)
                op(16, CRE, 14, ALU.mult)
                op(15, CIM, 18, ALU.mult)
                op(17, CRE, 18, ALU.mult)
                op(19, CIM, 14, ALU.mult)
                op(16, 16, 15, ALU.subtract)
                op(17, 17, 19, ALU.add)
                ts(q(16), q(16), 2.0, None, ALU.mult)
                ts(q(17), q(17), 2.0, None, ALU.mult)
                own.settle()

                v.wait_ge(s["lgB_ps"], NT)
                lgp = bank(2, NT * NE).rearrange("p (t e) -> p t e", e=NE)
                desc16 = desc8[:, 0, :].unsqueeze(1).broadcast_to([P, NT, NE])

                def red(o, x, kind):
                    own.done(v.tensor_reduce(o, x, AX, kind))
                    own.settle()

                def tts(o, x, y, kind):
                    tt(o, x, y, kind)
                    own.settle()

                def recip(o, x):
                    own.done(v.reciprocal(o, x))
                    own.settle()

                red(r1[0], lgp, ALU.max)
                v.tensor_tensor(rt[0], lgp, bc(r1[0], NE), ALU.subtract).then_inc(s["lgB_exp0"], 1)
                v.wait_ge(s["lgB_exp"], 1)
                red(r1[1], rt[1], ALU.add)
                recip(r1[2], r1[1])
                tts(rt[2], rt[1], bc(r1[2], NE), ALU.mult)
                for r in range(2):
                    red(r1[3 + r], rt[2], ALU.max)
                    tts(rt[3], rt[2], bc(r1[3 + r], NE), ALU.is_equal)
                    tts(rt[3], rt[3], desc16, ALU.mult)
                    red(r1[5], rt[3], ALU.max)
                    tts(rt[4 + r], rt[3], bc(r1[5], NE), ALU.is_equal)
                    if r == 0:
                        own.done(stt(rt[2], rt[4], -2.0, rt[2], ALU.mult, ALU.add))
                        own.settle()
                v.tensor_tensor(rt[7], rt[4], rt[5], ALU.add).then_inc(s["ohB_ready"], 1)
                tts(r1[6], r1[3], r1[4], ALU.add)
                ts(r1[6], r1[6], 1e-9, None, ALU.add)
                own.settle()
                recip(r1[7], r1[6])
                for k in range(NSEL):
                    tt(cw[:, k, :], r1[3 + k], r1[7], ALU.mult)
                v.wait_ge(s["cntB_ps"], 1)
                tot = bank(5, NT * NE).rearrange("p (t e) -> p t e", e=NE)
                before = earlier_tiles(rt[8], rt[9], tot)
                tts(r8[0], before[:, NT - 1, :], tot[:, NT - 1, :], ALU.add)
                tts(rt[10], before, bank(4, NT * NE).rearrange("p (t e) -> p t e", e=NE), ALU.add)
                tts(rt[10], rt[10], rt[7], ALU.subtract)
                ts(r8[1], r8[0], 1.0 / P, (P - 1.0) / P + FLOOR, ALU.mult, ALU.add)
                own.settle()
                ts(r8[1], r8[1], ROUND, -ROUND, ALU.add, ALU.add)
                own.settle()
                a_, c_, shift = r8[1], r8[2], 1
                while shift < NE:
                    own.done(v.tensor_copy(c_[:, 0:shift], a_[:, 0:shift]))
                    tts(c_[:, shift:NE], a_[:, shift:NE], a_[:, 0:NE - shift], ALU.add)
                    a_, c_, shift = c_, (r8[3] if c_ is r8[2] else r8[2]), 2 * shift
                end = a_
                tts(r8[4], end, r8[1], ALU.subtract)
                ts(r8[4], r8[4], float(P), None, ALU.mult)
                own.settle()
                tts(rt[10], rt[10], r8[4].unsqueeze(1).broadcast_to([P, NT, NE]), ALU.add)
                for k in range(NSEL):
                    tts(rt[11], rt[10], rt[4 + k], ALU.mult)
                    red(pos[:, k, :], rt[11], ALU.add)
                ts(phi, pos, 1.0 / P, FLOOR, ALU.mult, ALU.add)
                own.settle()
                ts(phi, phi, ROUND, -ROUND, ALU.add, ALU.add)
                own.settle()
                own.done(stt(plo, phi, -float(P), pos, ALU.mult, ALU.add))
                own.done(v.tensor_copy(posU[:], pos))
                own.settle()
                for n in range(NSEL * NT):
                    k, T = n // NT, n % NT
                    if n >= 4:
                        v.wait_ge(s["table_ps"], n - 3)
                    ts(lowhot[:, n % 4, :], iota[:], plo[:, k, T:T + 1], None, ALU.is_equal)
                    ts(hihot[:, n % 4, 0, :], iota[:, 0:ST], phi[:, k, T:T + 1], float(T), ALU.is_equal, ALU.mult)
                    v.tensor_scalar(hihot[:, n % 4, 1, :], iota[:, 0:ST], phi[:, k, T:T + 1], pcol[:, 0:1],
                                    ALU.is_equal, ALU.mult).then_inc(s["hot_ready"], 1)
                tts(ends8, end.unsqueeze(1).broadcast_to([P, ST, NE]), bc(iota[:, 0:ST], NE), ALU.is_le)
                red(te, ends8, ALU.add)
                ts(te, te, NE - 1.0, None, ALU.min)
                own.settle()
                own.done(v.tensor_copy(teI[:], te))
                ts(picked[:], te[0:BROWS, :], erow[:, 0:1], None, ALU.is_equal)
                v.wait_ge(s["table_ps"], NSEL * NT)
                own.done(v.tensor_copy(idlo, ps[:, 6, ST:2 * ST]))
                own.settle()
                own.done(stt(idlo, ps[:, 6, 0:ST], float(P), idlo, ALU.mult, ALU.add))
                own.settle()
                v.tensor_copy(idsU[:], idlo).then_inc(s["route_ready"], 1)
                v.wait_ge(s["z_out"], 16 * NBLK)

                def turns4(o, r):
                    ts(r, o, ROUND, -ROUND, ALU.add, ALU.add)
                    own.settle()
                    tt(o, o, r, ALU.subtract)
                    own.settle()
                    return stt(r, o, -1.0, o, ALU.mult, ALU.max)

                def quads(x):
                    return x.rearrange("p (j c k) -> p j c k", j=2, k=R)

                def flat(x):
                    return x.rearrange("p c k -> p (c k)")

                for st in range(ST + 2):
                    if st < ST:
                        u = st
                        v.wait_ge(s["sig_ready"], u + 1)
                        if u >= 2:
                            v.wait_ge(s["gT_ps"], u - 1)
                        v.tensor_tensor(gt[:, u % 2, :], bank(2 * (u % 2)), sig[:, u % 2, :], ALU.mult).then_inc(s["g_ready"], 1)
                    if st >= 2:
                        u = st - 2
                        v.wait_ge(s["yB_ps"], u + 1)
                        if u >= 2:
                            v.wait_ge(s[f"ys{u % 2}"], 16 * (u // 2))
                        v.tensor_tensor(yb[:, u % 2, :], ps[:, 5, 0:D], rows[:, BOF, :], ALU.add)\
                            .then_inc(s["yB_ready"], 1)
                    c, part = st // KPARTS, st % KPARTS
                    if c >= KCH:
                        continue
                    if part < 2:
                        ang = tk[2 * part]
                        tts(quads(ang), chan(TURN, c), ramps[:, part, :].unsqueeze(1).unsqueeze(1).broadcast_to([P, 2, 16, R]), ALU.mult)
                        turns4(ang, tk[2 * part + 1]).then_inc(s["k_trig"], 1)
                    elif part == 4:
                        v.wait_ge(s["k_sin"], 2 * c + 2)
                        v.wait_ge(s["mag_ready"], 2 * c + 2)
                        tts(flat(Pi), flat(Pr), tk[0], ALU.mult)
                        tts(flat(Pr), flat(Pr), tk[1], ALU.mult)
                    elif part == 5:
                        tt(quads(tk[0]), quads(flat(Pi)), chan(17, c), ALU.mult)
                        tt(quads(tk[1]), quads(flat(Pr)), chan(17, c), ALU.mult)
                        own.settle()
                    elif part == 6:
                        tt(quads(flat(Pr)), quads(flat(Pr)), chan(16, c), ALU.mult)
                        tt(quads(flat(Pi)), quads(flat(Pi)), chan(16, c), ALU.mult)
                        own.settle()
                    elif part == 7:
                        tt(flat(Pr), flat(Pr), tk[0], ALU.subtract)
                        v.tensor_tensor(flat(Pi), flat(Pi), tk[1], ALU.add).then_inc(s["k_used"], 1)
                    elif part == 8:
                        own.done(stt(flat(Qi), flat(Qr), -1.0, tk[2], ALU.mult, ALU.mult))
                        own.settle()
                        v.tensor_tensor(flat(Qr), flat(Qr), tk[3], ALU.mult).then_inc(s["k_used"], 1)
                for T in range(NT):
                    v.wait_ge(s[f"gy{T % 2}"], 32 * (T // 2 + 1))
                    own.done(stt(X[:, T, :], yg[:, T % 2, 0, :], cw[:, 0, T:T + 1], X[:, T, :], ALU.mult, ALU.add))
                    own.settle()
                    stt(X[:, T, :], yg[:, T % 2, 1, :], cw[:, 1, T:T + 1], X[:, T, :], ALU.mult, ALU.add).then_inc(s["xB_done"], 1)
                stage_end("vector", v)
            if "C" in stages:
                v.wait_ge(s["wC_in"], 16 * 6)
                v.memset(VW[:], 0.0).then_inc(s["vw_zero"], 1)
                for b in range(NB):
                    ts(maskb[:, b, :].rearrange("p (h k) -> p h k", h=H1),
                       vmask8[:, b, :].unsqueeze(1).broadcast_to([P, H1, S2]), HUGE, -HUGE, ALU.mult, ALU.add)
                ts(tmask, tmask8[:], 1.0 / H1, None, ALU.mult)
                v.wait_ge(s["prepC_sb"], 1)
                for b in range(NB):
                    v.tensor_tensor(kb1[:, b, :].rearrange("p (h k) -> p h k", h=H1),
                                    k1T[:, b * S2:(b + 1) * S2].unsqueeze(1).broadcast_to([P, H1, S2]),
                                    bc(mask32[:], S2), ALU.mult).then_inc(s["prepC_v"], 1)
                v.wait_ge(s["bfilm_in"], 16 * NB)
                for b in range(NB):
                    for io in range(2):
                        v.wait_ge(s["prepC_ps"], 7 + 2 * b + io + 1)
                        ts(VW[0:S2, b, io, :], ps[0:S2, 2 * b + io, :], mgate[0:S2, 0:1], None, ALU.mult)
                        one = VW[BIAS_ROW:BIAS_ROW + 1, b, io, :]
                        ts(one, one, mgate[BIAS_ROW:BIAS_ROW + 1, 0:1], None, ALU.mult)
                        own.settle()
                        ts(one[:, 0:D], one[:, 0:D], 1.0, None, ALU.add)
                        own.settle()
                        if io == 0:
                            r97 = slice(0, BIAS_ROW + 1)
                            sc, sh = VW[r97, b, 0, 0:D], VW[r97, b, 0, D:2 * D]
                            tt(xn[r97, 0, :], sc, rows[r97, BNI, :], ALU.mult)
                            own.settle()
                            tt(sh, sh, xn[r97, 0, :], ALU.add)
                            tt(sc, sc, rows[r97, GNI, :], ALU.mult)
                            own.settle()
                        v.nop().then_inc(s["prepC_v"], 1)
                for b in range(NB):
                    ln_stats(v, own, lambda j: X[:, b * TB + j, :], TB, 0, "lnC_stats")
                    v.wait_ge(s["lnC_rstd"], b + 1)
                    for t in range(TB):
                        normalise(v, U[:, b * TB + t, :], X[:, b * TB + t, :], t).then_inc(s["u_ready"], 1)
                    v.wait_ge(s["u_ready"], (b + 1) * TB)
                    ln_stats(v, own, lambda j: U[:, b * TB + j, :], TB, TB, "lnU_stats")
                    v.wait_ge(s["lnU_rstd"], b + 1)
                    for step in range(TB + 1):
                        if step < TB:
                            n, par = b * TB + step, step % 2
                            S, Rr, E = Sc[:, par, :], Rk[:, par, :], Ex[:, par, :]
                            hv = lambda x: x.rearrange("p (h k) -> p h k", h=H1)
                            v.wait_ge(s["sC_ps"], n + 1)
                            stt(S, bank(2 + n % 2, SW), 1.0 / math.sqrt(DH1), maskb[:, b, :], ALU.mult, ALU.add)\
                                .then_inc(s["sC_read"], 1)
                            v.wait_ge(s["sC_read"], n + 1)
                            for r in range(TOPK // 8):
                                cur = S if r == 0 else Rr
                                for h in range(H1):
                                    own.done(v.max(top[:, par, h, 8 * r:8 * r + 8], hv(cur)[:, h, :]))
                                own.settle()
                                if r == 0:
                                    v.tensor_tensor(hv(E), hv(S), bc(top[:, par, :, 0], S2), ALU.subtract)\
                                        .then_inc(s["exC_in"], 1)
                                for h in range(H1):
                                    own.done(v.match_replace(hv(Rr)[:, h, :], top[:, par, h, 8 * r:8 * r + 8],
                                                             hv(cur)[:, h, :], TAKEN))
                                own.settle()
                            v.wait_ge(s["exC"], n + 1)
                            own.done(stt(E, Rr, TAKEN / 1.5, E, ALU.is_le, ALU.mult))
                            own.settle()
                            own.done(v.tensor_reduce(smC[:, par, 0, :], hv(E), AX, ALU.add))
                            own.settle()
                            own.done(v.reciprocal(smC[:, par, 1, :], smC[:, par, 0, :]))
                            own.settle()
                            ts(smC[:, par, 2, :], smC[:, par, 1, :], tmask[:, n:n + 1], None, ALU.mult)
                            own.settle()
                            tt(hv(E), hv(E), bc(smC[:, par, 2, :], S2), ALU.mult)
                            own.settle()
                            if n >= 2:
                                v.wait_ge(s["AT_ps"], n - 1)
                            v.tensor_reduce(a77[:, par, :], E.rearrange("p (h k) -> p k h", h=H1), AX, ALU.add)\
                                .then_inc(s["attn_ready"], 1)
                        if step >= 1:
                            n = b * TB + step - 1
                            par = n % 2
                            if b == 0:
                                m = step - 1
                                v.wait_ge(s["ks_sb"], m + 1)
                                stt((KSCr, KSCi)[m // 4][:, m % 4, :], (KS0r, KS0i)[m // 4][:, m % 4, :], sgn[:, 0:1],
                                    ps[:, 5, D:2 * D], ALU.mult, ALU.add).then_inc(s["ks_done"], 1)
                            own.done(normalise(v, xn[:, par, :], U[:, n, :], TB + step - 1))
                            own.settle()
                            v.wait_ge(s["film_ps"], n + 1)
                            tt(xn[:, par, :], xn[:, par, :], ps[:, 6 + n % 2, 0:D], ALU.mult)
                            own.settle()
                            v.tensor_tensor(XIN[:, n, :], xn[:, par, :], ps[:, 6 + n % 2, D:2 * D], ALU.add)\
                                .then_inc(s["xin_ready"], 1)
                for re, im, ny in ((KS0r, KS0i, KS0n), (KSCr, KSCi, KSCn)):
                    own.done(v.tensor_copy(ny, re[:, 0, :]))
                    own.settle()
                    own.done(v.tensor_copy(ny[0:1, :], im[0:1, 0, :]))
                    own.settle()
                    own.done(v.memset(im[0:1, 0, :], 0.0))
                stage_end("vector", v)
            if "D" in stages:
                for b in range(NB):
                    for m in range(4):
                        n = b * 4 + m
                        v.wait_ge(s["xf_sb"], n + 1)
                        x0r, x0i = XS[:, 0, :], XS[:, 1, :]
                        k0n, kcn = (KS0n, KSCn) if m == 0 else (KS0r[:, m, :], KSCr[:, m, :])
                        Y, T = (lambda r: YF[:, m, r, :]), (lambda r: tmpD[:, r, :])
                        for r, (kr, ki) in enumerate(((KS0r[:, m, :], KS0i[:, m, :]), (KS0i[:, m, :], k0n),
                                                      (KSCr[:, m, :], KSCi[:, m, :]), (KSCi[:, m, :], kcn))):
                            tt(Y(r), x0r, kr, ALU.mult)
                            tt(T(r), x0i, ki, ALU.mult)
                        own.settle()
                        for r in range(4):
                            tt(Y(r), Y(r), T(r), (ALU.subtract, ALU.add)[r % 2])
                        own.settle()
                        v.wait_ge(s["pr_p"], 4 * (n + 1))
                        tt(Y(2), Y(2), pt_[:, 0, :], ALU.add)
                        tt(Y(3), Y(3), pt_[:, 2, :], ALU.add)
                        own.settle()
                        tt(Y(2), Y(2), pt_[:, 1, :], ALU.subtract)
                        v.tensor_tensor(Y(3), Y(3), pt_[:, 3, :], ALU.add).then_inc(s["yf_ready"], 1)
                    for t in range(TB):
                        n = b * TB + t
                        T = tmpD[:, 4 + n % 2, :]
                        v.wait_ge(s["yd_ps"], n + 1)
                        v.wait_ge(s["xskip"], n + 1)
                        tt(T, XIN[:, n, :], ps[:, 4 + n % 2, 0:D], ALU.add)
                        own.settle()
                        tt(T, T, ps[:, 6 + n % 2, 0:D], ALU.mult)
                        own.settle()
                        v.tensor_tensor(T, T, ps[:, 6 + n % 2, D:2 * D], ALU.add).then_inc(s["xt_ready"], 1)
                        v.wait_ge(s["xt_ready"], n + 1)
                        tt(U[:, n, :], U[:, n, :], T, ALU.add)
                stage_end("vector", v)
            if "E" in stages:
                v.wait_ge(s["b1p_ps"], 1)
                v.tensor_tensor(b1p, ps[:, 7, 0:HID1 // P], b1[:], ALU.add).then_inc(s["b1p_sb"], 1)
                ts(w1[:, 0, :], w1[:, 0, :], gb_ffn[:, 0, 0:1], None, ALU.mult)
                v.tensor_scalar(w1[:, 1, :], w1[:, 1, :], gb_ffn[:, 0, 1:2], None, ALU.mult).then_inc(s["w1s"], 1)
                for i in range(NBLK):
                    ln_stats(v, own, lambda j: U[:, 4 * i + j, :], 4, 0, "lnE_stats")
                    v.wait_ge(s["lnE_rstd"], i + 1)
                    if i:
                        v.wait_ge(s["xTE_ps"], 4 * i)
                    for t in range(4):
                        normalise(v, xnE[:, t, :], U[:, 4 * i + t, :], t).then_inc(s["zE_ready"], 1)
                    for t in range(4):
                        own.done(v.tensor_tensor(U[:, 4 * i + t, :], U[:, 4 * i + t, :], rows[:, B2, :], ALU.add))
                    own.settle()
                    for t in range(4):
                        n = 4 * i + t
                        v.wait_ge(s["oE_ps"], n + 1)
                        v.tensor_tensor(U[:, n, :], U[:, n, :], ps[:, 4 + n % 2, 0:D], ALU.add).then_inc(s["oE_read"], 1)
                        v.wait_ge(s["oE_read"], n + 1)
                        ln_stats(v, own, lambda j: U[:, n, :], 1, 8 + n % 2, "lnO_stats")
                        v.wait_ge(s["lnO_rstd"], n + 1)
                        if n >= 2:
                            v.wait_ge(s["xE_done"], n - 1)
                        normalise(v, oE[:, n % 2, :], U[:, n, :], 8 + n % 2).then_inc(s["oE_ready"], 1)
                stage_end("vector", v)
            if "F" in stages:
                for i in range(NBLK):
                    ln_stats(v, own, lambda j: X[:, 4 * i + j, :], 4, 0, "lnF_stats")
                    v.wait_ge(s["lnF_rstd"], i + 1)
                    if i:
                        v.wait_ge(s["zTF_ps"], 4 * i)
                    for t in range(4):
                        normalise(v, zF[:, t, :], X[:, 4 * i + t, :], t).then_inc(s["zF_ready"], 1)
                    for t in range(4):
                        n = 4 * i + t
                        v.wait_ge(s["yF_ps"], n + 1)
                        tt(yF[:, n, :], ps[:, 2 + n % 2, 0:D], rows[:, BEXP, :], ALU.add)
                        v.tensor_copy(lg[:, n, :], ps[:, 2 + n % 2, D:D + NE]).then_inc(s["yF_sb"], 1)
                v.wait_ge(s["yF_sb"], NT)
                own.done(v.tensor_reduce(r16[:, 0, :], lg, AX, ALU.max))
                own.settle()
                v.tensor_tensor(fs[:, 0], lg, bc(r16[:, 0, :], NE), ALU.subtract).then_inc(s["lgF"], 1)
                tt(oh, lg, bc(r16[:, 0, :], NE), ALU.is_equal)
                own.settle()
                tt(oh, oh, desc8[:, 0, :].unsqueeze(1).broadcast_to([P, NT, NE]), ALU.mult)
                own.settle()
                own.done(v.tensor_reduce(r16[:, 1, :], oh, AX, ALU.max))
                own.settle()
                v.tensor_tensor(oh, oh, bc(r16[:, 1, :], NE), ALU.is_equal).then_inc(s["oh_ready"], 1)
                v.wait_ge(s["lgF_exp"], 1)
                own.done(v.tensor_reduce(r16[:, 2, :], fs[:, 1], AX, ALU.add))
                own.settle()
                own.done(v.reciprocal(r16[:, 3, :], r16[:, 2, :]))
                v.wait_ge(s["cum_ps"], 1)
                before = earlier_tiles(fs[:, 2], fs[:, 3], bank(5, NT * NE).rearrange("p (t e) -> p t e", e=NE))
                tt(fs[:, 4], before, bank(4, NT * NE).rearrange("p (t e) -> p t e", e=NE), ALU.add)
                own.settle()
                own.done(stt(fs[:, 5], fs[:, 4], CAP, oh, ALU.is_le, ALU.mult))
                own.settle()
                own.done(v.tensor_reduce(r16[:, 4, :], fs[:, 5], AX, ALU.add))
                own.settle()
                tt(r16[:, 5, :], r16[:, 4, :], r16[:, 3, :], ALU.mult)
                own.settle()
                for T in range(NT):
                    stt(X[:, T, :], yF[:, T, :], r16[:, 5, T:T + 1], X[:, T, :], ALU.mult, ALU.add).then_inc(s["xF_ready"], 1)




def host_inputs(inp):
    import numpy as np

    A = {k: np.ascontiguousarray(np.asarray(x)) for k, x in inp.items()}
    o = {}
    o["x"] = A["x"]
    p = np.arange(P)
    o["c_ident"] = np.eye(P, dtype=np.float32)
    o["c_tri"] = (p[:, None] <= p[None, :]).astype(np.float32)
    o["c_mask16"] = (p[:, None] // DH0 == np.arange(HG)[None, :]).astype(np.float32)
    o["c_mask32"] = (p[:, None] // DH1 == np.arange(H1)[None, :]).astype(np.float32)
    o["c_sgn"] = (1.0 - 2.0 * (p[:, None] % 2)).astype(np.float32)
    o["c_desc8"] = np.tile(np.arange(NE, 0, -1, dtype=np.float32), (P, 4))
    o["c_ramps"] = np.tile(np.concatenate([R * np.arange(R), np.arange(R)]).astype(np.float32), (P, 1))
    N = L
    t, f = np.arange(N // 2)[:, None].astype(np.int64), np.arange(N // 2)[None, :].astype(np.int64)
    ang = 2 * np.pi * ((t * f) % N) / N
    fwd = np.concatenate([np.cos(ang), -np.sin(ang)], 1)
    fwd[:, N // 2] = 1.0 - 2.0 * (np.arange(N // 2) % 2)
    inv = fwd.T * 2.0 / N
    inv[0] /= 2
    inv[N // 2] /= 2
    o["c_dftf"], o["c_dfti"] = fwd.astype(np.float32), inv.astype(np.float32)
    wkv = A["L0_xattn_Wkv"].reshape(H0, 2, DH0, DC)
    bkv = A["L0_xattn_bkv"].reshape(H0, 2, DH0)
    o["wk0"], o["wv0"] = (wkv[:, i].reshape(D, DC).T for i in range(2))
    def columns(*v):
        return np.concatenate([x.reshape(-1, P) for x in v]).T

    o["bias0"] = columns(A["L0_xattn_bq"], bkv[:, 0].reshape(D), bkv[:, 1].reshape(D))
    o["ctxT"] = A["ctx_768"].reshape(NB * S2, DC).T
    o["wq0"], o["wo0"] = A["L0_xattn_Wq"].T, A["L0_xattn_Wo"].T
    o["wg0"], o["wof"] = A["L0_ffn_Wg"].T, A["L0_ffn_Wo"].T
    o["w1t"] = A["L0_ffn_W1"].transpose(0, 2, 1)
    o["b1e"] = A["L0_ffn_b1"]
    o["c_erow"] = np.where(p[:BROWS] % 32 < NE, p[:BROWS] % 32, -1).astype(np.float32)[:, None]
    o["c_iota"] = np.tile(np.arange(P, dtype=np.float32), (P, 1))
    o["c_pcol"] = np.arange(P, dtype=np.float32)[:, None]
    o["wq1"] = A["L1_xattn_Wq"].T
    for n in ("Wk", "Wv", "W_film_in", "W_film_out", "W1", "W2", "b2", "D_skip", "g_norm_in", "b_norm_in",
              "g_norm_out", "b_norm_out", "log_dt"):
        o["L1_xattn_" + n] = A["L1_xattn_" + n]
    o["b_film"] = np.concatenate([A["L1_xattn_b_film_in"], A["L1_xattn_b_film_out"]])[None]
    o["L0_xattn_bo"], o["L0_ffn_bo"], o["L1_ffn_b_expert"] = A["L0_xattn_bo"], A["L0_ffn_bo"], A["L1_ffn_b_expert"]
    o["gb_ffn"] = columns(A["L1_xattn_g_ffn"], A["L1_xattn_b_ffn"])
    o["b1"] = columns(A["L1_xattn_b1"])
    o["wx"] = np.concatenate([A["L1_ffn_w_expert"], A["L1_ffn_w_gate"]], 1)
    for n, k in (("k_are", "A_re"), ("k_aim", "A_im"), ("k_cre", "C_re"), ("k_cim", "C_im")):
        o[n] = A["L1_xattn_" + k].reshape(2, P, NS).transpose(0, 2, 1).reshape(P, P)
    o["mod_gate"] = A["L1_xattn_mod_gate"].reshape(1, 1)
    o["text_mask"] = A["mask_BxS_bf1"].view(np.uint8).reshape(NT, P).T
    o["vision_mask"] = A["mask_BxS2_bf1"].view(np.uint8)
    return {k: np.ascontiguousarray(x) for k, x in o.items()}


def kernel(**inputs):
    import concourse.bacc as bacc
    from concourse.bass_utils import run_bass_kernel_spmd

    nc = bacc.Bacc("TRN2", target_bir_lowering=False, num_devices=1)
    arrays = host_inputs(inputs)
    d = {k: nc.dram_tensor(f"in_{k}", a.shape, mybir.dt.from_np(a.dtype), kind="ExternalInput").ap()
         for k, a in arrays.items()}
    out = nc.dram_tensor("out", (NB, L, D), F32, kind="ExternalOutput").ap()
    build(nc, d, out)
    r = run_bass_kernel_spmd(nc, [{f"in_{k}": a for k, a in arrays.items()}], core_ids=[0])
    return r.results[0]["out"]
```

```python
import math
from contextlib import ExitStack

import concourse.bass as bass
from concourse import mybir

P = 128
NB, L, D = 2, 1024, 256
NT, TB = NB * L // P, L // P
KD = D // P
BLK = 512
NBLK = NB * L // BLK
S2, DC = 77, 192
CC = DC // 2
H0, DH0 = 16, 16
HG = 8
GW = HG * S2
BW = GW // 2
NCH = 5
NE, HID0 = 8, 512
H1, DH1, TOPK = 4, 32, 32
SW = H1 * S2
NS = 64
R = 32
HID1 = 1024
CAP = 100.0
BIAS_ROW = 96
NSEL = 2
ST = (NSEL * NB * L + NE * (P - 1)) // P
FLOOR = -0.5 + 1.0 / 512
KCH, KPARTS = 4, 9
KOFF = 2
KW = 32
D_ORDER = tuple((b, m) for b in range(NB) for m in range(4))
ARENA = 37144
SCAT = 4
BROWS = 2 * 32 + NE
HUGE = 1.0e30
TAKEN = -3.0e38
ROUND = 1.5 * 2.0 ** 23
EPS = 1e-5

F32 = mybir.dt.float32
BF16 = mybir.dt.bfloat16
I32, U32 = mybir.dt.int32, mybir.dt.uint32
U8 = mybir.dt.uint8
ALU = mybir.AluOpType
ACT = mybir.ActivationFunctionType
AX = mybir.AxisListType.X
ENGINES = ("sync", "scalar", "vector", "gpsimd", "tensor")


class Steps:

    def __init__(self, eng, sem):
        self.eng, self.sem, self.n = eng, sem, 0

    def done(self, ins):
        self.n += 1
        ins.then_inc(self.sem, 1)

    def settle(self):
        self.eng.wait_ge(self.sem, self.n)


def build(nc, d, out, last="F"):
    ctx = ExitStack()
    with ctx:
        def sb(name, shape, dt=F32):
            return ctx.enter_context(nc.sbuf_tensor(name, shape, dt))

        def sem(name):
            return ctx.enter_context(nc.semaphore(name))

        stages = "ABCDEF"[:"ABCDEF".index(last) + 1]
        ps = ctx.enter_context(nc.psum_tensor("ps", [P, 8, BLK], F32))

        X = sb("X", [P, NT, D])
        ident = sb("ident", [P, P])
        ones = sb("ones", [P, P])
        tri = sb("tri", [P, P])
        neghalf, negone = sb("neghalf", [P, 8]), sb("negone", [P, H1])
        mask16, mask32 = sb("mask16", [P, HG]), sb("mask32", [P, H1])
        desc8 = sb("desc8", [P, 4, NE])
        ramps = sb("ramps", [P, 2, R])
        sgn = sb("sgn", [P, 1])
        halfpi = sb("halfpi", [P, 1])
        wq0, wo0 = sb("wq0", [P, KD, D]), sb("wo0", [P, KD, D])
        wk0, wv0 = sb("wk0", [CC, 2, D]), sb("wv0", [CC, 2, D])
        bias0 = sb("bias0", [P, 3, KD])
        ctxT = sb("ctxT", [CC, 2, NB * S2])
        wg0, wof = sb("wg0", [P, KD, NE]), sb("wof", [P, 4, D])
        wq1, wk1, wv1 = sb("wq1", [P, D]), sb("wk1", [CC, 2, P]), sb("wv1", [CC, 2, D])
        b1 = sb("b1", [P, HID1 // P])
        gb_ffn = sb("gb_ffn", [P, 2, KD])
        wx = sb("wx", [P, KD, D + NE])
        rows = sb("rows", [P, 9, D])
        BO0, BOF, GNI, BNI, GNO, BNO, B2, DSKIP, BEXP = range(9)
        mgate = sb("mgate", [P, 1])
        b1p = sb("b1p", [P, HID1 // P])
        tmask8, vmask8 = sb("tmask8", [P, NT], U8), sb("vmask8", [P, NB, S2], U8)
        bstat = sb("bstat", [P, TB + 2, 6])
        mv = sb("mv", [P, 3 * TB, 2])
        rstd = sb("rstd", [P, 3 * TB])
        arena = sb("arena", [P, ARENA])

        class Region:
            def __init__(self, at=0):
                self.at = at

            def take(self, *dims):
                n = math.prod(dims)
                v = arena[:, self.at:self.at + n]
                self.at += n
                assert self.at <= ARENA, self.at
                names = "abcd"[:len(dims)]
                if len(dims) > 1:
                    kw = {c: k for c, k in zip(names, dims)}
                    v = v.rearrange(f"p ({' '.join(names)}) -> p {' '.join(names)}", **kw)
                return v

        ra = Region()
        kblk, vblk = ra.take(2, NB, GW), ra.take(2, NB, GW)
        vwo = ra.take(NB, 2 * NCH, D)
        zA, zTA, qT = ra.take(TB, D), ra.take(KD, L), ra.take(2, L)
        Pb, PT = ra.take(4, GW), ra.take(2, NCH * P)
        kvT = ra.take(2, 2, NB * S2)
        mxA, smA = ra.take(4, HG), ra.take(4, HG)
        w1all = Region(ARENA - KD * NE * 2 * HID0).take(KD, NE, 2 * HID0)
        assert ra.at <= ARENA - KD * NE * 2 * HID0
        rb = Region()
        rb.take(8 * KW * R)
        rkern = Region()
        Pr, Pi, Qr, Qi = (rkern.take(KW, R) for _ in range(4))
        tk = [rkern.take(KW * R) for _ in range(4)]
        assert rkern.at == rb.at
        KT = rb.take(R, NS)
        zB = Region(2 * NB * GW).take(NT, D)
        assert TB * D <= 2 * NB * GW and (2 * NB * GW + NT * D) <= rkern.at
        zTB = rb.take(2, KD, BLK)
        xg, xTg = rb.take(2, D), rb.take(2, KD, P)
        sig, gt, bof = rb.take(2, HID0), rb.take(2, HID0), rb.take(2, D)
        rt = [rb.take(NT, NE) for _ in range(12)]
        r1 = [rb.take(NT) for _ in range(8)]
        r8 = [rb.take(NE) for _ in range(6)]
        pos = rb.take(NSEL, NT)
        phi, plo = rb.take(NSEL, NT), rb.take(NSEL, NT)
        ends8, te = rb.take(ST, NE), rb.take(ST)
        idw = [rb.take(ST) for _ in range(4)]
        hieq = rb.take(2, 4, ST)
        assert rb.at <= ARENA - KD * NE * 2 * HID0
        cw = sb("cw", [P, NSEL + 1, NT])
        idsU, destU = sb("idsU", [P, ST], U32), sb("destU", [P, ST], U32)
        slotid = sb("slotid", [P, ST])
        teI = sb("teI", [P, ST], I32)
        lowhot = wq0[:].rearrange("p k n -> p (k n)").bitcast(BF16).rearrange("p (a b c) -> p a b c", a=2, b=4)
        hihot = wo0[:].rearrange("p k n -> p (k n)").bitcast(BF16)[:, 0:16 * ST]\
            .rearrange("p (a b c d) -> p a b c d", a=2, b=4, c=2)
        b1r = sb("b1r", [BROWS, 2 * HID0], BF16)
        picked = sb("picked", [BROWS, ST], BF16)
        erow = sb("erow", [BROWS, 1])
        onerow = sb("onerow", [1, P], BF16)
        iota, pcol = sb("iota", [P, P]), sb("pcol", [P, 1])
        rk = Region()
        KS0r, KS0i, KSCr, KSCi = (rk.take(4, D) for _ in range(4))
        KS0n, KSCn = rk.take(D), rk.take(D)
        DF = rk.take(4, L)
        keep_k = rk.at
        kp = sb("kp", [P, 20, P])
        b1s = [kp[:, 8 * i:8 * i + 8, :].rearrange("p a b -> p (a b)") for i in range(2)]
        tmpD = kp[:].rearrange("p a b -> p (a b)").rearrange("p (a b) -> p a b", b=D)
        rc = Region(keep_k)
        U, XIN = rc.take(NT, D), rc.take(NT, D)
        AT, VW = rc.take(NT * P), rc.take(NB, 2, 2 * D)
        keep_c = rc.at
        uT = rc.take(2, KD, P)
        wqk = rc.take(KD, NB, SW)
        filmS = Region(rc.at).take(2, 2 * D)
        kb1 = rc.take(NB, SW)
        vT1 = rc.take(KD, NB * S2)
        k1T = rc.take(NB * S2)
        maskrow = rc.take(SW).bitcast(BF16).rearrange("p (b n) -> p b n", b=NB)
        tmask = rc.take(NT)
        Sc, Rk, Ex = rc.take(2, SW), rc.take(2, SW), rc.take(2, SW)
        top, topx = rc.take(2, H1, TOPK), rc.take(2, H1, TOPK)
        smC = rc.take(2, 4, H1)
        a77 = rc.take(2, S2)
        xn = rc.take(2, D)
        KL = rc.take(L // P, D)
        rc.at = max(rc.at, keep_c + 4 * 4 * D + 8 * BLK)
        keep_kl = rc.at
        XS0 = rc.take(4, 2, 2, D)
        wfilm = Region(keep_kl).take(KD, 2, 2 * D)
        yg = [Region(at).take(NSEL, 4, HID0) for at in (0, keep_k + NT * D, keep_kl + 2048, 0)]
        G, GT = Region(keep_kl + 2048 + 4096).take(2, HID0), Region(keep_k + 12 * D).take(2, 4, P)
        rd = Region(keep_c)
        YF0, DI = rd.take(4, 4, D), rd.take(8, BLK)
        assert rd.at <= keep_kl
        YF1 = Region(keep_kl).take(4, 4, D)
        rd = Region(rc.at)
        XS1, pt_ = rd.take(2, 2, 2, D), rd.take(4, D)
        re_ = Region(keep_k + NT * D)
        xnE, xT = re_.take(4, D), re_.take(KD, BLK)
        hT = re_.take(HID1 // P, BLK)
        rw = Region(keep_k - 4 * L)
        w1, w2 = rw.take(KD, HID1), rw.take(HID1 // P, D)
        oE = re_.take(2, D)
        rf = Region(re_.at)
        zF, zTF = rf.take(2, 4, D), rf.take(KD, BLK)
        yF = rf.take(NT, D)
        lg, oh, fs = rf.take(NT, NE), rf.take(NT, NE), rf.take(8, NT, NE)
        r16 = rf.take(6, NT)

        scr_z = nc.dram_tensor("scr_z", [NT * P, D], F32, kind="Internal").ap()
        scr_g = nc.dram_tensor("scr_g", [(NSEL * NT + ST) * P, HID0], F32, kind="Internal").ap()
        scr_k = nc.dram_tensor("scr_k", [L, D], F32, kind="Internal").ap()

        names = """x_in0 x_in1 consts_in wA_in wB_in wC_in wE_in rows_in kparam_in dft_in
            own_v own_p own_a stage_end 
            lnA_stats lnA_rstd zA_ready zTA_ps zTA_sb qT_ps qT_sb kv_ps kv_sb kblk_ready vwo_ps vwo_sb
            scores_ready scores_read probs_exp probs_sum probs_norm pt_ps pt_sb oA_ps xA_done xbA
            lnB_stats lnB_rstd zB_ready zTB_ps zTB_sb lgT_ps lgT_sb lgB_ps lgB_exp0 lgB_exp ohB_ready cntB_ps
            hieq_ready low_ready hi_ready table_ps route_ready w1all_in b1_zero b1_in b1r_ready z_out
            gx0 gx1 xTg_ps xTg_sb h_ps sig_ready g_ready gs0 gs1 sum_ready sumT_ps sumT_sb oB_ps gy0 gy1 xB_done
            kp_exp kp_par kv_arg mag_ready k_trig k_sin k_used k_ps k_sb k_out k_in w2_in wfilm_in ks_ps ks_sb ks_done
            lnC_stats lnC_rstd u_ready uT_ps uT_sb lnU_rstd prepC_ps prepC_sb prepC_v sC_ps sC_read
            top_neg top_full exC ex_sum weighted xn_ready film_sb attn_ready AT_ps AT_sb film_ps xin_ready maskC vw_zero bfilm_in
            dfi_in xf_ps xf_sb pr_p yf0_ready yf1_ready yd_ps xskip xt_ready
            lnE_stats lnE_rstd zE_ready xTE_ps xTE_sb b1p_ps b1p_sb w1s hE_ps hE_sb oE_ps oE_read
            lnO_stats lnO_rstd oE_ready xbE xE_done
            lnF_stats lnF_rstd zF_ready zTF_ps zTF_sb yF_ps yF_sb lgF lgF_exp oh_ready cum_ps 
            xF_ready stored""".split()
        s = {n: sem(n) for n in names}

        def load(eng, dst, src, signal):
            eng.dma_start(dst, src).then_inc(s[signal], 16)

        def prow(name):
            return d[name].rearrange("(o d) -> o d", o=1).broadcast_to([P, D])

        def chunked(name, k):
            return d[name].rearrange("(k p) n -> p k n", k=k)

        block = ctx.enter_context(nc.Block())
        ends = {e: 0 for e in ENGINES}

        def stage_end(name, eng):
            ends[name] += 1
            eng.drain().then_inc(s["stage_end"], 1)
            eng.wait_ge(s["stage_end"], len(ENGINES) * ends[name])

        def ln_stats(v, own, src, n, at, signal, bs=0):
            for j in range(n):
                own.done(v.bn_stats(bstat[:, bs + j, :], src(j)))
            own.settle()
            for j in range(n):
                ins = v.bn_aggr(mv[:, at + j, :], bstat[:, bs + j, :])
            ins.then_inc(s[signal], 1)

        def ln_rstd(p, own, n, at, stats, count, signal):
            p.wait_ge(s[stats], count)
            own.done(p.tensor_scalar(rstd[:, at:at + n], mv[:, at:at + n, 1], EPS, None, ALU.add))
            own.settle()
            p.tensor_tensor(rstd[:, at:at + n], rstd[:, at:at + n], neghalf[:, 0:n], ALU.pow).then_inc(s[signal], 1)

        def normalise(v, dst, src, k):
            return v.tensor_scalar(dst, src, mv[:, k, 0:1], rstd[:, k:k + 1], ALU.subtract, ALU.mult)

        def chan(i, c):
            v = kp[:, i, :].rearrange("p (j c) -> p j c", j=2)[:, :, c * 16:(c + 1) * 16]
            return v.unsqueeze(3).broadcast_to([P, 2, 16, R])

        def bank(i, n=BLK):
            return ps[:, i, 0:n]

        @block.sync
        def _(sp):
            load(sp, wk0[:], chunked("wk0", 2), "wA_in")
            load(sp, wv0[:], chunked("wv0", 2), "wA_in")
            load(sp, bias0[:], d["bias0"].rearrange("p (a k) -> p a k", a=3), "wA_in")
            load(sp, ctxT[:], chunked("ctxT", 2), "wA_in")
            load(sp, X[:, 0:TB, :], d["x"].rearrange("b (t p) n -> p (b t) n", p=P)[:, 0:TB, :], "x_in0")
            load(sp, wq0[:], chunked("wq0", KD), "wA_in")
            load(sp, wo0[:], chunked("wo0", KD), "wA_in")
            for dst, name in ((ident, "c_ident"), (tri, "c_tri"), (mask16, "c_mask16"), (mask32, "c_mask32"),
                              (sgn, "c_sgn"), (iota, "c_iota"), (pcol, "c_pcol")):
                load(sp, dst[:], d[name], "consts_in")
            load(sp, desc8[:], d["c_desc8"].rearrange("p (a b) -> p a b", a=4), "consts_in")
            load(sp, ramps[:], d["c_ramps"].rearrange("p (a b) -> p a b", a=2), "consts_in")
            load(sp, X[:, TB:NT, :], d["x"].rearrange("b (t p) n -> p (b t) n", p=P)[:, TB:NT, :], "x_in1")
            sp.wait_ge(s["b1_zero"], 1)
            for i in range(3):
                load(sp, b1s[0][32 * i:32 * i + NE, :], d["b1e"], "b1_in")
            for i, name in enumerate(("L0_xattn_bo", "L0_ffn_bo", "L1_xattn_g_norm_in", "L1_xattn_b_norm_in",
                                      "L1_xattn_g_norm_out", "L1_xattn_b_norm_out", "L1_xattn_b2",
                                      "L1_xattn_D_skip", "L1_ffn_b_expert")):
                load(sp, rows[:, i, :], prow(name), "rows_in")
            load(sp, wg0[:], chunked("wg0", KD), "wB_in")
            load(sp, wof[:], chunked("wof", 4), "wB_in")
            load(sp, erow[:], d["c_erow"], "wB_in")
            load(sp, slotid[:], d["c_slot"], "wB_in")
            for e in range(NE):
                load(sp, w1all[:, :, e, :], d["w1t"][e].rearrange("(k p) n -> p k n", p=P), "w1all_in")
            load(sp, wq1[:], d["wq1"], "wC_in")
            load(sp, wk1[:], chunked("L1_xattn_Wk", 2), "wC_in")
            load(sp, wv1[:], chunked("L1_xattn_Wv", 2), "wC_in")
            load(sp, mgate[:], d["mod_gate"].broadcast_to([P, 1]), "wC_in")
            load(sp, tmask8[:], d["text_mask"], "wC_in")
            load(sp, vmask8[:].rearrange("p b k -> p (b k)"),
                 d["vision_mask"].rearrange("b k -> (b k)").rearrange("(o n) -> o n", o=1).broadcast_to([P, NB * S2]),
                 "wC_in")
            load(sp, b1[:], d["b1"], "wE_in")
            load(sp, gb_ffn[:], d["gb_ffn"].rearrange("p (a k) -> p a k", a=2), "wE_in")
            load(sp, wx[:], chunked("wx", KD), "wE_in")
            sp.wait_ge(s["b1r_ready"], 3)
            for i, name in enumerate(("k_are", "k_aim", "k_cre", "k_cim")):
                load(sp, kp[:, i, :], d[name], "kparam_in")
            for h in range(2):
                load(sp, kp[h * NS:(h + 1) * NS, 4, :],
                     d["L1_xattn_log_dt"][h * P:(h + 1) * P].rearrange("(o d) -> o d", o=1).broadcast_to([NS, P]),
                     "kparam_in")
            stage_end("sync", sp)
            if "B" in stages:
                for i in range(NBLK):
                    sp.wait_ge(s["zB_ready"], 4 * i + 4)
                    sp.dma_start(scr_z.rearrange("(t p) n -> p t n", p=P)[:, 4 * i:4 * i + 4, :], zB[:, 4 * i:4 * i + 4, :])\
                        .then_inc(s["z_out"], 16)
                stage_end("sync", sp)
            if "C" in stages:
                for i in range(2):
                    sp.wait_ge(s[f"gs{i}"], 16 * ((ST + 1 - i) // 2))

                def load_gated(i):
                    for k in range(NSEL):
                        rowsb = scr_g[(k * NT + 4 * i) * P:(k * NT + 4 * i + 4) * P, :]
                        load(sp, yg[i][:, k, :, :], rowsb.rearrange("(t p) n -> p t n", p=P), f"gy{i % 2}")

                load_gated(0)
                load(sp, wfilm[:, :, 0, :], chunked("L1_xattn_W_film_in", KD), "wfilm_in")
                load(sp, wfilm[:, :, 1, :], chunked("L1_xattn_W_film_out", KD), "wfilm_in")
                sp.wait_ge(s["vw_zero"], 1)
                for b in range(NB):
                    load(sp, VW[BIAS_ROW:BIAS_ROW + 1, b, :, :].rearrange("p a b -> p (a b)"), d["b_film"], "bfilm_in")
                load_gated(1)
                sp.wait_ge(s["k_sb"], 2 * KCH)
                for j in range(4):
                    sp.dma_start(scr_k.rearrange("(a b) n -> a b n", b=R)[:, :, j * NS:(j + 1) * NS],
                                 KT[32 * j:32 * j + 32, :, :]).then_inc(s["k_out"], 16)
                sp.wait_ge(s["gy0"], 32)
                load_gated(2)
                sp.wait_ge(s["gy1"], 32)
                sp.wait_ge(s["sum_ready"], 4)
                load_gated(3)
                sp.wait_ge(s["k_out"], 64)
                load(sp, KL, scr_k.rearrange("(k p) n -> p k n", p=P), "k_in")
                load(sp, DF, d["c_dftf"].rearrange("(k p) n -> p k n", p=P), "dft_in")
                stage_end("sync", sp)
            if "D" in stages:
                load(sp, DI, d["c_dfti"].rearrange("(k p) n -> p k n", p=P), "dfi_in")
                sp.wait_ge(s["xf_ps"], 16)
                load(sp, w1, chunked("L1_xattn_W1", KD), "w2_in")
                load(sp, w2, chunked("L1_xattn_W2", HID1 // P), "w2_in")
            if "F" in stages:
                for t in range(NT):
                    sp.wait_ge(s["xF_ready"], t + 1)
                    sp.dma_start(out.rearrange("b (t p) n -> p (b t) n", p=P)[:, t, :], X[:, t, :]).then_inc(s["stored"], 16)
                sp.wait_ge(s["stored"], 16 * NT)
            else:
                if "E" in stages:
                    sp.wait_ge(s["xE_done"], NT)
                sp.dma_start(out.rearrange("b (t p) n -> p (b t) n", p=P), X[:]).then_inc(s["stored"], 16)
                sp.wait_ge(s["stored"], 16)

        @block.tensor
        def _(pe):
            def mm(o, l, r, first, final):
                return pe.matmul(o, l, r, start=first, stop=final)

            def spectrum(b, m, ri, at):
                x = XIN[:, b * TB:(b + 1) * TB, :].rearrange("p (j k) n -> p j k n", j=2)
                for k in range(4):
                    ins = mm(bank(at), DF[:, k, (4 * ri + m) * P:(4 * ri + m + 1) * P], x[:, :, k, :], k == 0, k == 3)
                ins.then_inc(s["xf_ps"], 1)

            pe.wait_ge(s["wA_in"], 16 * 6)
            for i in range(4):
                w, g = (wk0, wv0)[i // 2], i % 2
                for c in range(2):
                    ins = mm(bank(i, NB * S2), w[:, c, g * P:(g + 1) * P], ctxT[:, c, :], c == 0, c == 1)
                ins.then_inc(s["kv_ps"], 1)
            def values_out():
                pe.wait_ge(s["kblk_ready"], 8)
                for vb in range(NB):
                    for g in range(2):
                        for c in range(NCH):
                            n = (vb * 2 + g) * NCH + c
                            m = min(P, GW - c * P)
                            if n >= 4:
                                pe.wait_ge(s["vwo_sb"], n - 3)
                            mm(ps[0:m, 4 + n % 4, 0:D], vblk[:, g, vb, c * P:c * P + m], wo0[:, g, :], True, True)\
                                .then_inc(s["vwo_ps"], 1)
                pe.wait_ge(s["vwo_sb"], 4 * NCH)

            for b in range(NB):
                if b == 0:
                    pe.wait_ge(s["consts_in"], 16 * 9)
                else:
                    pe.wait_ge(s["xA_done"], TB)
                for t in range(TB):
                    n = b * TB + t
                    pe.wait_ge(s["zA_ready"], n + 1)
                    if n >= 2:
                        pe.wait_ge(s["zTA_sb"], n - 1)
                    for k in range(KD):
                        ins = pe.transpose(ps[:, 6 + n % 2, k * P:(k + 1) * P], zA[:, t, k * P:(k + 1) * P], ident[:])
                    ins.then_inc(s["zTA_ps"], 1)
                pe.wait_ge(s["zTA_sb"], (b + 1) * TB)
                for h in range(2):
                    for g in range(2):
                        n = (b * 2 + h) * 2 + g
                        if n % 4 >= 2:
                            pe.wait_ge(s["qT_sb"], n - 1)
                        for k in range(KD):
                            ins = mm(bank(6 + n % 2), wq0[:, k, g * P:(g + 1) * P], zTA[:, k, h * BLK:(h + 1) * BLK],
                                     k == 0, k == KD - 1)
                        ins.then_inc(s["qT_ps"], 1)
                pe.wait_ge(s["qT_sb"], (b + 1) * 4)
                if b == 0:
                    values_out()
                NU = 2 * TB
                for step in range(NU + 3):
                    if step < NU:
                        u, t, g = b * NU + step, step // 2, step % 2
                        if u >= 2:
                            pe.wait_ge(s["scores_read"], u - 1)
                        for c in range(2):
                            ins = mm(ps[:, 2 * (u % 2) + c, 0:BW], qT[:, g, t * P:(t + 1) * P],
                                     kblk[:, g, b, c * BW:(c + 1) * BW], True, True)
                        ins.then_inc(s["scores_ready"], 1)
                    if 0 <= step - 2 < NU:
                        u = b * NU + step - 2
                        pe.wait_ge(s["probs_norm"], u + 1)
                        if u >= 1:
                            pe.wait_ge(s["pt_sb"], u)
                        for c in range(NCH):
                            m = min(P, GW - c * P)
                            ins = pe.transpose(ps[0:m, 4 + c // 4, (c % 4) * P:(c % 4) * P + P],
                                               Pb[:, u % 4, c * P:c * P + m], ident[:])
                        ins.then_inc(s["pt_ps"], 1)
                    if 0 <= step - 3 < NU:
                        u = b * NU + step - 3
                        g, T = (step - 3) % 2, u // 2
                        pe.wait_ge(s["pt_sb"], u + 1)
                        if g == 0 and T >= 2:
                            pe.wait_ge(s["xA_done"], T - 1)
                        for c in range(NCH):
                            m = min(P, GW - c * P)
                            ins = mm(ps[:, 6 + T % 2, 0:D], PT[0:m, u % 2, c * P:(c + 1) * P], vwo[0:m, b, g * NCH + c, :],
                                     g == 0 and c == 0, g == 1 and c == NCH - 1)
                        ins.then_inc(s["oA_ps"], 1)
            stage_end("tensor", pe)
            if "B" in stages:
                pe.wait_ge(s["wB_in"], 64)
                for i in range(NBLK + 2):
                    if i < NBLK:
                        for n in range(4 * i, 4 * i + 4):
                            pe.wait_ge(s["zB_ready"], n + 1)
                            if n >= 2:
                                pe.wait_ge(s["zTB_sb"], n - 1)
                            for k in range(KD):
                                ins = pe.transpose(ps[:, n % 2, k * P:(k + 1) * P], zB[:, n, k * P:(k + 1) * P], ident[:])
                            ins.then_inc(s["zTB_ps"], 1)
                    if 1 <= i <= NBLK:
                        pe.wait_ge(s["zTB_sb"], 4 * i)
                        if i >= 2:
                            pe.wait_ge(s["lgT_sb"], i - 1)
                        for k in range(KD):
                            ins = mm(ps[0:NE, 3, :], wg0[:, k, :], zTB[:, (i - 1) % 2, k, :], k == 0, k == KD - 1)
                        ins.then_inc(s["lgT_ps"], 1)
                    if i >= 2:
                        pe.wait_ge(s["lgT_sb"], i - 1)
                        for t in range(4):
                            n = 4 * (i - 2) + t
                            ins = pe.transpose(ps[:, 2, n * NE:(n + 1) * NE], sig[0:NE, i % 2, t * P:(t + 1) * P],
                                               ident[0:NE, 0:NE])
                        ins.then_inc(s["lgB_ps"], 1)
                pe.wait_ge(s["ohB_ready"], 1)
                ohf = rt[7].rearrange("p t e -> p (t e)")
                mm(bank(4, NT * NE), tri[:], ohf, True, True)
                mm(bank(5, NT * NE), ones[:], ohf, True, True).then_inc(s["cntB_ps"], 1)
                for i in range(NSEL * NT // 4):
                    pe.wait_ge(s["low_ready"], i + 1)
                    pe.wait_ge(s["hi_ready"], i + 1)
                    for j in range(4):
                        ins = mm(bank(6, 2 * ST), lowhot[:, i % 2, j, :], hihot[:, i % 2, j, :, :].rearrange("p a b -> p (a b)"),
                                 i + j == 0, i == NSEL * NT // 4 - 1 and j == 3)
                    ins.then_inc(s["table_ps"], 1)
                pe.wait_ge(s["route_ready"], 1)
                pe.wait_ge(s["w1all_in"], 16 * NE)
                pe.wait_ge(s["b1r_ready"], 3)

                def turn_x(u):
                    pe.wait_ge(s[f"gx{u % 2}"], 16 * (u // 2 + 1))
                    if u >= 2:
                        pe.wait_ge(s["xTg_sb"], u - 1)
                    for k in range(KD):
                        ins = pe.transpose(ps[:, 5 + u % 2, k * P:(k + 1) * P],
                                           xg[:, u % 2, k * P:(k + 1) * P], ident[:])
                    ins.then_inc(s["xTg_ps"], 1)

                turn_x(0)
                turn_x(1)
                for st in range(ST + 2):
                    if st < ST:
                        u = st
                        e = pe.value_load(teI[0:1, u:u + 1], min_val=0, max_val=NE - 1)
                        pe.wait_ge(s["xTg_sb"], u + 1)
                        if u >= 2:
                            pe.wait_ge(s["g_ready"], u - 1)
                        for half in range(2):
                            cols = slice(half * HID0, (half + 1) * HID0)
                            o = bank(2 * (u % 2) + half)
                            mm(o, picked[:, u:u + 1].broadcast_to([BROWS, P]), b1r[:, cols], True, False)
                            for k in range(KD):
                                ins = mm(o, xTg[:, u % 2, k, :],
                                         w1all[:, k, bass.ds(e, 1), cols].rearrange("p o n -> p (o n)"), False, k == KD - 1)
                        ins.then_inc(s["h_ps"], 1)
                        if u + 2 < ST:
                            turn_x(u + 2)
                    c, h = (st - KOFF) // KPARTS - 1, (st - KOFF) % KPARTS
                    if 0 <= c < KCH and h < 2:
                        pe.wait_ge(s["k_used"], 2 * (c + 1))
                        if 2 * c + h:
                            pe.wait_ge(s["k_sb"], 2 * c + h)
                        half_rows = slice(64 * h, 64 * h + 64)
                        for c16 in range(16):
                            for jj in range(2):
                                j, w = 2 * h + jj, jj * 16 + c16
                                o = ps[32 * j:32 * j + 32, 7, c16 * R:(c16 + 1) * R]
                                mm(o, Pr[half_rows, w, :], Qr[half_rows, w, :], True, False)
                                ins = mm(o, Pi[half_rows, w, :], Qi[half_rows, w, :], False, True)
                        ins.then_inc(s["k_ps"], 1)
                stage_end("tensor", pe)
            if "C" in stages:
                pe.wait_ge(s["wC_in"], 16 * 6)
                for c in range(2):
                    ins = mm(bank(0, NB * S2), wk1[:, c, :], ctxT[:, c, :], c == 0, c == 1)
                ins.then_inc(s["prepC_ps"], 1)
                for g in range(2):
                    for c in range(2):
                        ins = mm(bank(1 + g, NB * S2), wv1[:, c, g * P:(g + 1) * P], ctxT[:, c, :], c == 0, c == 1)
                    ins.then_inc(s["prepC_ps"], 1)
                pe.wait_ge(s["prepC_v"], 2)
                for b in range(NB):
                    for g in range(2):
                        mm(bank(4 + 2 * b + g, SW), wq1[:, g * P:(g + 1) * P], kb1[:, b, :], True, True)\
                            .then_inc(s["prepC_ps"], 1)
                pe.wait_ge(s["prepC_sb"], 7)

                def film_weights():
                    pe.wait_ge(s["wfilm_in"], 32)
                    for b in range(NB):
                        for io in range(2):
                            for g in range(2):
                                ins = mm(ps[0:S2, 2 * b + io, :], vT1[:, g, b * S2:(b + 1) * S2], wfilm[:, g, io, :], g == 0, g == 1)
                            ins.then_inc(s["prepC_ps"], 1)

                for T in range(NT + 1):
                    if T == 4:
                        film_weights()
                    if T < NT:
                        pe.wait_ge(s["sum_ready"], T + 1)
                        if T >= 2:
                            pe.wait_ge(s["sumT_sb"], T - 1)
                        for f in range(4):
                            ins = pe.transpose(ps[:, 4 + T % 2, f * P:(f + 1) * P], G[:, T % 2, f * P:(f + 1) * P], ident[:])
                        ins.then_inc(s["sumT_ps"], 1)
                    if T:
                        n = T - 1
                        pe.wait_ge(s["sumT_sb"], n + 1)
                        if n >= 2:
                            pe.wait_ge(s["xB_done"], n - 1)
                        for f in range(4):
                            ins = mm(ps[:, 6 + n % 2, 0:D], GT[:, n % 2, f, :], wof[:, f, :], f == 0, f == 3)
                        ins.then_inc(s["oB_ps"], 1)

                pe.wait_ge(s["prepC_v"], 6)

                def turn_u(n):
                    pe.wait_ge(s["u_ready"], n + 1)
                    if n >= 2:
                        pe.wait_ge(s["uT_sb"], n - 1)
                    for k in range(KD):
                        ins = pe.transpose(ps[:, n % 2, k * P:(k + 1) * P], U[:, n, k * P:(k + 1) * P], ident[:])
                    ins.then_inc(s["uT_ps"], 1)

                def scores(n):
                    pe.wait_ge(s["uT_sb"], n + 1)
                    if n >= 2:
                        pe.wait_ge(s["sC_read"], n - 1)
                    mm(bank(2 + n % 2, SW), onerow[:], maskrow[0:1, n // TB, :], True, False)
                    for k in range(KD):
                        ins = mm(bank(2 + n % 2, SW), uT[:, n % 2, k, :], wqk[:, k, n // TB, :], False, k == KD - 1)
                    ins.then_inc(s["sC_ps"], 1)

                turn_u(0)
                turn_u(1)
                scores(0)
                for step in range(NT + 1):
                    if step + 2 < NT:
                        turn_u(step + 2)
                    if step + 1 < NT:
                        scores(step + 1)
                    if step >= 1:
                        n = step - 1
                        pe.wait_ge(s["attn_ready"], n + 1)
                        if n:
                            pe.wait_ge(s["AT_sb"], n)
                        pe.transpose(ps[0:S2, 4, 0:P], a77[:, n % 2, :], ident[:]).then_inc(s["AT_ps"], 1)
                    if 1 <= step <= 8:
                        m = step - 1
                        if m == 0:
                            pe.wait_ge(s["k_in"], 16)
                            pe.wait_ge(s["dft_in"], 16)
                        else:
                            pe.wait_ge(s["ks_done"], m)
                        for k in range(4):
                            ins = mm(bank(5), DF[:, k, m * P:(m + 1) * P],
                                     KL.rearrange("p (j k) n -> p j k n", j=2)[:, :, k, :], k == 0, k == 3)
                        ins.then_inc(s["ks_ps"], 1)
                    if step > TB:
                        i = step - TB - 1
                        if i == 0:
                            pe.wait_ge(s["xin_ready"], TB)
                            pe.wait_ge(s["ks_done"], 8)
                        else:
                            pe.wait_ge(s["xf_sb"], i)
                        spectrum(0, i // 2, i % 2, 5)
                    if step >= 1:
                        n = step - 1
                        pe.wait_ge(s["AT_sb"], n + 1)
                        if n >= 2:
                            pe.wait_ge(s["film_sb"], n - 1)
                        mm(bank(6 + n % 2), AT[0:BIAS_ROW + 1, n * P:(n + 1) * P], VW[0:BIAS_ROW + 1, n // TB, 0, :], True, True)\
                            .then_inc(s["film_ps"], 1)
                stage_end("tensor", pe)
            if "D" in stages:
                for i in range(8):
                    if i >= 4:
                        pe.wait_ge(s["xf_sb"], 8 + i - 3)
                    spectrum(1, i // 2, i % 2, i % 4)
                pe.wait_ge(s["dfi_in"], 16)
                for b in range(NB):
                    pe.wait_ge(s[f"yf{b}_ready"], 4)
                    YF = (YF0, YF1)[b]
                    if b:
                        pe.wait_ge(s["wE_in"], 16 * 3)
                        pe.wait_ge(s["w2_in"], 32)
                        for f in range(HID1 // P):
                            for k in range(KD):
                                ins = mm(ps[:, 0, f:f + 1], w1[:, k, f * P:(f + 1) * P], gb_ffn[:, 1, k:k + 1], k == 0, k == 1)
                        ins.then_inc(s["b1p_ps"], 1)
                    for t in range(TB):
                        n, j, k = b * TB + t, t // 4, t % 4
                        if n >= 2:
                            pe.wait_ge(s["xt_ready"], n - 1)
                        for m in range(8):
                            mm(ps[:, 4 + n % 2, 0:D], DI[:, m, k * P:(k + 1) * P], YF[:, m % 4, 2 * j + m // 4, :], m == 0, m == 7)
                        mm(bank(6 + n % 2), AT[0:BIAS_ROW + 1, n * P:(n + 1) * P], VW[0:BIAS_ROW + 1, b, 1, :], True, True)\
                            .then_inc(s["yd_ps"], 1)
            if "E" in stages:
                pe.wait_ge(s["w1s"], 1)

                def turn_E(i):
                    for t in range(4):
                        n = i * 4 + t
                        pe.wait_ge(s["zE_ready"], n + 1)
                        if n >= 2:
                            pe.wait_ge(s["xTE_sb"], n - 1)
                        for k in range(KD):
                            ins = pe.transpose(ps[:, n % 2, k * P:(k + 1) * P], xnE[:, t, k * P:(k + 1) * P], ident[:])
                        ins.then_inc(s["xTE_ps"], 1)

                def expert_F(i, steps=range(5)):
                    for step in steps:
                        if step < 4:
                            n = i * 4 + step
                            pe.wait_ge(s["zF_ready"], n + 1)
                            if n:
                                pe.wait_ge(s["zTF_sb"], n)
                            for k in range(KD):
                                ins = pe.transpose(ps[:, 6, k * P:(k + 1) * P], zF[:, i % 2, step, k * P:(k + 1) * P], ident[:])
                            ins.then_inc(s["zTF_ps"], 1)
                        if step:
                            n, t = i * 4 + step - 1, step - 1
                            pe.wait_ge(s["zTF_sb"], n + 1)
                            if n:
                                pe.wait_ge(s["yF_sb"], n)
                            for k in range(KD):
                                ins = mm(ps[:, 7, 0:D + NE], zTF[:, k, t * P:(t + 1) * P], wx[:, k, :], k == 0, k == KD - 1)
                            ins.then_inc(s["yF_ps"], 1)

                turn_E(0)
                for i in range(NBLK):
                    pe.wait_ge(s["xTE_sb"], 4 * i + 4)
                    for f in range(HID1 // P):
                        n = i * 8 + f
                        if n >= 2:
                            pe.wait_ge(s["hE_sb"], n - 1)
                        for k in range(KD):
                            ins = mm(bank(2 + n % 2), w1[:, k, f * P:(f + 1) * P], xT[:, k, :], k == 0, k == KD - 1)
                        ins.then_inc(s["hE_ps"], 1)
                        if i >= 2 and 1 <= f <= 5 and "F" in stages:
                            expert_F(i - 2, (f - 1,))
                    if i + 1 < NBLK:
                        turn_E(i + 1)
                    pe.wait_ge(s["hE_sb"], 8 * i + 8)
                    for t in range(4):
                        n = i * 4 + t
                        if n >= 2:
                            pe.wait_ge(s["oE_read"], n - 1)
                        for f in range(HID1 // P):
                            ins = mm(ps[:, 4 + n % 2, 0:D], hT[:, f, t * P:(t + 1) * P], w2[:, f, :], f == 0, f == 7)
                        ins.then_inc(s["oE_ps"], 1)
            if "F" in stages:
                expert_F(NBLK - 2)
                expert_F(NBLK - 1)
                pe.wait_ge(s["oh_ready"], 1)
                pe.wait_ge(s["oE_read"], NT)
                ohf = oh.rearrange("p t e -> p (t e)")
                mm(bank(4, NT * NE), tri[:], ohf, True, True)
                mm(bank(5, NT * NE), ones[:], ohf, True, True).then_inc(s["cum_ps"], 1)

        @block.scalar
        def _(a):
            own = Steps(a, s["own_a"])

            def copy(o, i):
                return a.activation(o, i, ACT.Copy)

            for i in range(4):
                a.wait_ge(s["kv_ps"], i + 1)
                if i == 0:
                    a.wait_ge(s["wA_in"], 16 * 6)
                a.activation(kvT[:, i // 2, i % 2, :], bank(i, NB * S2), ACT.Identity,
                             bias=bias0[:, 1 + i // 2, i % 2:i % 2 + 1]).then_inc(s["kv_sb"], 1)
            for b in range(NB):
                for t in range(TB):
                    n = b * TB + t
                    a.wait_ge(s["zTA_ps"], n + 1)
                    copy(zTA[:, :, t * P:(t + 1) * P], ps[:, 6 + n % 2, 0:D].rearrange("p (k c) -> p k c", k=KD))\
                        .then_inc(s["zTA_sb"], 1)
                for h in range(2):
                    for g in range(2):
                        n = (b * 2 + h) * 2 + g
                        a.wait_ge(s["qT_ps"], n + 1)
                        a.activation(qT[:, g, h * BLK:(h + 1) * BLK], bank(6 + n % 2), ACT.Identity,
                                     bias=bias0[:, 0, g:g + 1]).then_inc(s["qT_sb"], 1)
                if b == 0:
                    for vb in range(NB):
                        for g in range(2):
                            for c in range(NCH):
                                n, m = (vb * 2 + g) * NCH + c, min(P, GW - c * P)
                                a.wait_ge(s["vwo_ps"], n + 1)
                                copy(vwo[0:m, vb, g * NCH + c, :], ps[0:m, 4 + n % 4, 0:D]).then_inc(s["vwo_sb"], 1)
                NU = 2 * TB
                for step in range(NU + 2):
                    if step < NU:
                        u = b * NU + step
                        a.wait_ge(s["scores_read"], u + 1)
                        a.activation(Pb[:, u % 4, :], Pb[:, u % 4, :], ACT.Exp, scale=1.0 / math.sqrt(DH0))\
                            .then_inc(s["probs_exp"], 1)
                    if step >= 2:
                        u = b * NU + step - 2
                        a.wait_ge(s["pt_ps"], u + 1)
                        if u >= 2:
                            a.wait_ge(s["oA_ps"], u - 1)
                        last_rows = GW - 4 * P
                        own.done(copy(PT[:, u % 2, 0:4 * P], bank(4)))
                        copy(PT[0:last_rows, u % 2, 4 * P:5 * P], ps[0:last_rows, 5, 0:P]).then_inc(s["pt_sb"], 1)
            stage_end("scalar", a)
            if "B" in stages:
                a.wait_ge(s["kparam_in"], 16 * 6)
                a.activation(kp[:, 5, :], kp[:, 4, :], ACT.Exp).then_inc(s["kp_exp"], 1)
                for i in range(NBLK + 1):
                    if i < NBLK:
                        for t in range(4):
                            n = 4 * i + t
                            a.wait_ge(s["zTB_ps"], n + 1)
                            if i >= 2 and t == 0:
                                a.wait_ge(s["lgT_ps"], i - 1)
                            copy(zTB[:, i % 2, :, t * P:(t + 1) * P], ps[:, n % 2, 0:D].rearrange("p (k c) -> p k c", k=KD))\
                                .then_inc(s["zTB_sb"], 1)
                    if i >= 1:
                        a.wait_ge(s["lgT_ps"], i)
                        if i >= 3:
                            a.wait_ge(s["lgB_ps"], i - 2)
                        copy(sig[0:NE, (i - 1) % 2, :], ps[0:NE, 3, :]).then_inc(s["lgT_sb"], 1)
                a.wait_ge(s["lgB_exp0"], 1)
                a.activation(rt[1], rt[0], ACT.Exp).then_inc(s["lgB_exp"], 1)

                def put_x(u):
                    a.wait_ge(s["xTg_ps"], u + 1)
                    if u >= 2:
                        a.wait_ge(s["h_ps"], u - 1)
                    copy(xTg[:, u % 2, :, :].rearrange("p k c -> p (k c)"), ps[:, 5 + u % 2, 0:D])\
                        .then_inc(s["xTg_sb"], 1)

                two_pi = 2 * math.pi

                def coef_functions():
                    a.wait_ge(s["kp_par"], 1)
                    a.activation(kp[:, 8, :], kp[:, 6, :], ACT.Tanh, scale=0.5).then_inc(s["kp_exp"], 1)
                    a.wait_ge(s["kp_par"], 2)
                    own.done(a.activation(kp[:, 10, :], kp[:, 7, :], ACT.Sin, scale=two_pi))
                    own.done(a.activation(kp[:, 11, :], kp[:, 9, :], ACT.Sin, scale=-two_pi, bias=halfpi[:]))
                    a.activation(kp[:, 12, :], kp[:, 7, :], ACT.Sin, scale=math.pi).then_inc(s["kp_exp"], 1)

                put_x(0)
                put_x(1)
                for st in range(ST + 2):
                    if st < ST:
                        u = st
                        a.wait_ge(s["h_ps"], u + 1)
                        if u >= 2:
                            a.wait_ge(s["g_ready"], u - 1)
                        a.activation(sig[:, u % 2, :], bank(2 * (u % 2) + 1), ACT.Sigmoid).then_inc(s["sig_ready"], 1)
                        if u + 2 < ST:
                            put_x(u + 2)
                    if st == 0:
                        coef_functions()
                    c, part = (st - KOFF) // KPARTS, (st - KOFF) % KPARTS
                    if 1 <= c <= KCH and part < 2:
                        a.wait_ge(s["k_ps"], 2 * (c - 1) + part + 1)
                        rowsk = slice(64 * part, 64 * part + 64)
                        copy(KT[rowsk, :, (c - 1) * 16:c * 16].rearrange("p b c -> p c b"),
                             ps[rowsk, 7, :].rearrange("p (c b) -> p c b", b=R)).then_inc(s["k_sb"], 1)
                    if 0 <= c < KCH and part in (2, 5):
                        i = part // 5
                        a.wait_ge(s["k_trig"], 2 * c + 1 + i)
                        own.done(a.activation(tk[2 * i], tk[2 * i], ACT.Sin, scale=two_pi))
                        a.activation(tk[2 * i + 1], tk[2 * i + 1], ACT.Sin, scale=-two_pi, bias=halfpi[:])\
                            .then_inc(s["k_sin"], 1)
                    if 0 <= c < KCH and part == 3:
                        a.wait_ge(s["kv_arg"], 2 * c + 2)
                        for mag in (Pr, Qr):
                            a.activation(mag, mag, ACT.Exp).then_inc(s["mag_ready"], 1)
                stage_end("scalar", a)
            if "C" in stages:
                a.wait_ge(s["prepC_ps"], 1)
                copy(k1T[:, :], bank(0, NB * S2)).then_inc(s["prepC_sb"], 1)
                for g in range(2):
                    a.wait_ge(s["prepC_ps"], 2 + g)
                    copy(vT1[:, g, :], bank(1 + g, NB * S2)).then_inc(s["prepC_sb"], 1)
                for b in range(NB):
                    for g in range(2):
                        a.wait_ge(s["prepC_ps"], 4 + 2 * b + g)
                        copy(wqk[:, g, b, :], bank(4 + 2 * b + g, SW)).then_inc(s["prepC_sb"], 1)
                for T in range(NT):
                    a.wait_ge(s["sumT_ps"], T + 1)
                    if T >= 2:
                        a.wait_ge(s["oB_ps"], T - 1)
                    copy(GT[:, T % 2, :, :].rearrange("p f c -> p (f c)"), bank(4 + T % 2)).then_inc(s["sumT_sb"], 1)

                def put_uT(n):
                    a.wait_ge(s["uT_ps"], n + 1)
                    if n >= 2:
                        a.wait_ge(s["sC_ps"], n - 1)
                    copy(uT[:, n % 2, :, :].rearrange("p k c -> p (k c)"), ps[:, n % 2, 0:D]).then_inc(s["uT_sb"], 1)

                def put_scores(n):
                    a.wait_ge(s["sC_ps"], n + 1)
                    a.activation(Sc[:, n % 2, :], bank(2 + n % 2, SW), ACT.Copy, scale=1.0 / math.sqrt(DH1))\
                        .then_inc(s["sC_read"], 1)

                put_uT(0)
                put_uT(1)
                put_scores(0)
                for n in range(NT + 1):
                    if n < NT:
                        a.wait_ge(s["sC_read"], n + 1)
                        a.wait_ge(s["top_neg"], n + 1)
                        if n >= 2:
                            a.wait_ge(s["AT_ps"], n - 1)
                        for h in range(H1):
                            a.activation(Ex[:, n % 2, h * S2:(h + 1) * S2], Sc[:, n % 2, h * S2:(h + 1) * S2], ACT.Exp,
                                         bias=smC[:, n % 2, 3, h:h + 1]).then_inc(s["exC"], 1)
                        if n + 1 < NT:
                            if n:
                                a.wait_ge(s["top_full"], n)
                            put_scores(n + 1)
                        if n + 2 < NT:
                            put_uT(n + 2)
                        a.wait_ge(s["top_full"], n + 1)
                        if n >= 2:
                            a.wait_ge(s["ex_sum"], 4 * (n - 1))
                        for h in range(H1):
                            a.activation(topx[:, n % 2, h, :], top[:, n % 2, h, :], ACT.Exp, bias=smC[:, n % 2, 3, h:h + 1],
                                         accum_out=smC[:, n % 2, 0, h:h + 1]).then_inc(s["ex_sum"], 1)
                    if n:
                        T = n - 1
                        a.wait_ge(s["AT_ps"], T + 1)
                        if T == 0:
                            a.wait_ge(s["maskC"], 2)
                        copy(AT[0:S2, T * P:(T + 1) * P], ps[0:S2, 4, 0:P]).then_inc(s["AT_sb"], 1)
                        if T < TB:
                            a.wait_ge(s["ks_ps"], T + 1)
                            copy((KS0r, KS0i)[T // 4][:, T % 4, :], ps[:, 5, 0:D]).then_inc(s["ks_sb"], 1)
                        else:
                            a.wait_ge(s["xf_ps"], T - TB + 1)
                            copy(XS0[:, (T - TB) // 2, (T - TB) % 2, :, :].rearrange("p j n -> p (j n)"), bank(5))\
                                .then_inc(s["xf_sb"], 1)
                        a.wait_ge(s["film_ps"], T + 1)
                        if T >= 2:
                            a.wait_ge(s["xin_ready"], T - 1)
                        copy(filmS[:, T % 2, :], bank(6 + T % 2)).then_inc(s["film_sb"], 1)
                stage_end("scalar", a)
            if "D" in stages:
                for i in range(8):
                    m, ri = i // 2, i % 2
                    a.wait_ge(s["xf_ps"], 8 + i + 1)
                    if m >= 2 and ri == 0:
                        a.wait_ge(s["yf1_ready"], m - 1)
                    copy(XS1[:, m % 2, ri, :, :].rearrange("p j n -> p (j n)"), bank(i % 4)).then_inc(s["xf_sb"], 1)
            if "E" in stages:
                def put_xT(i):
                    for t in range(4):
                        a.wait_ge(s["xTE_ps"], i * 4 + t + 1)
                        if t == 0 and i:
                            a.wait_ge(s["hE_ps"], 8 * i)
                        copy(xT[:, :, t * P:(t + 1) * P], ps[:, t % 2, 0:D].rearrange("p (k c) -> p k c", k=KD))\
                            .then_inc(s["xTE_sb"], 1)

                def put_zTF(i, tiles=range(4)):
                    for t in tiles:
                        a.wait_ge(s["zTF_ps"], i * 4 + t + 1)
                        if t == 0 and i:
                            a.wait_ge(s["yF_ps"], 4 * i)
                        copy(zTF[:, :, t * P:(t + 1) * P], ps[:, 6, 0:D].rearrange("p (k c) -> p k c", k=KD))\
                            .then_inc(s["zTF_sb"], 1)

                put_xT(0)
                for i in range(NBLK):
                    for f in range(HID1 // P):
                        n = i * 8 + f
                        a.wait_ge(s["hE_ps"], n + 1)
                        if n == 0:
                            a.wait_ge(s["b1p_sb"], 1)
                            a.wait_ge(s["xt_ready"], NT)
                        if f == 0 and i:
                            a.wait_ge(s["oE_ps"], 4 * i)
                        a.activation(hT[:, f, :], bank(2 + n % 2), ACT.Gelu, bias=b1p[:, f:f + 1]).then_inc(s["hE_sb"], 1)
                        if i >= 2 and 1 <= f <= 4 and "F" in stages:
                            put_zTF(i - 2, (f - 1,))
                    if i + 1 < NBLK:
                        put_xT(i + 1)
            if "F" in stages:
                put_zTF(NBLK - 2)
                put_zTF(NBLK - 1)
                a.wait_ge(s["lgF"], 1)
                a.activation(fs[:, 1], fs[:, 0], ACT.Exp).then_inc(s["lgF_exp"], 1)

        @block.gpsimd
        def _(p):
            own = Steps(p, s["own_p"])

            def add_oE(n):
                p.wait_ge(s["oE_ready"], n + 1)
                p.wait_ge(s["xbE"], n + 1)
                p.tensor_tensor(X[:, n, :], X[:, n, :], oE[:, n % 2, :], ALU.add).then_inc(s["xE_done"], 1)

            p.memset(b1s[0], 0.0).then_inc(s["b1_zero"], 1)
            own.done(p.memset(neghalf[:], -0.5))
            own.done(p.memset(negone[:], -1.0))
            own.done(p.memset(ones[:], 1.0))
            own.done(p.memset(onerow[:], 1.0))
            own.done(p.memset(halfpi[:], math.pi / 2))
            own.settle()

            def front_A(b):
                ln_rstd(p, own, TB, 0, "lnA_stats", b + 1, "lnA_rstd")

            def bias_A(T):
                p.tensor_tensor(X[:, T, :], X[:, T, :], rows[:, BO0, :], ALU.add).then_inc(s["xbA"], 1)

            front_A(0)
            p.wait_ge(s["rows_in"], 16 * 9)
            for b in range(NB):
                p.wait_ge(s["zA_ready"], (b + 1) * TB)
                for st in range(2 * TB):
                    if b == 0 and st == 8:
                        front_A(1)
                    if b == 1 and st == 8 and "B" in stages:
                        ln_rstd(p, own, TB, 0, "lnB_stats", 1, "lnB_rstd")
                    if st % 2 == 0:
                        bias_A(b * TB + st // 2)
                    u = b * 2 * TB + st
                    p.wait_ge(s["probs_sum"], u + 1)
                    pv = Pb[:, u % 4, :].rearrange("p (h k) -> p h k", h=HG)
                    p.tensor_tensor(pv, pv, smA[:, u % 4, :].unsqueeze(2).broadcast_to([P, HG, S2]), ALU.mult)\
                        .then_inc(s["probs_norm"], 1)
            stage_end("gpsimd", p)
            if "B" in stages:
                ln_rstd(p, own, TB, TB, "lnB_stats", 2, "lnB_rstd")
                for i in range(NSEL * NT // 4):
                    number = iota[:, 4 * i + 1:4 * i + 5].unsqueeze(2).broadcast_to([P, 4, ST])
                    p.wait_ge(s["hieq_ready"], i + 1)
                    if i >= 2:
                        p.wait_ge(s["table_ps"], i - 1)
                    own.done(p.tensor_tensor(hihot[:, i % 2, :, 0, :], hieq[:, i % 2], number, ALU.mult))
                    p.tensor_scalar(hihot[:, i % 2, :, 1, :], hieq[:, i % 2], pcol[:, 0:1], None, ALU.mult)\
                        .then_inc(s["hi_ready"], 1)
                p.wait_ge(s["route_ready"], 1)
                p.wait_ge(s["z_out"], 16 * NBLK)
                for st in range(ST + SCAT):
                    if st < ST:
                        if st >= 2:
                            p.wait_ge(s["xTg_ps"], st - 1)
                        p.indirect_dma_start(xg[:, st % 2, :], None, scr_z,
                                             bass.IndirectOffsetOnAxis(ap=idsU[:, st:st + 1], axis=0))\
                            .then_inc(s[f"gx{st % 2}"], 16)
                    if st >= SCAT:
                        u = st - SCAT
                        p.wait_ge(s["g_ready"], u + 1)
                        p.indirect_dma_start(scr_g, bass.IndirectOffsetOnAxis(ap=destU[:, u:u + 1], axis=0),
                                             gt[:, u % 2, :], None).then_inc(s[f"gs{u % 2}"], 16)
                    if st >= SCAT and st % 2 == 0 and st < SCAT + 2 * NT:
                        T = (st - SCAT) // 2
                        own.settle()
                        own.done(p.tensor_scalar(bof[:, T % 2, :], rows[:, BOF, :], cw[:, NSEL, T:T + 1], None, ALU.mult))
                        own.settle()
                        own.done(p.tensor_tensor(X[:, T, :], X[:, T, :], bof[:, T % 2, :], ALU.add))
                    c, part = (st - KOFF) // KPARTS, (st - KOFF) % KPARTS
                    if 0 <= c < KCH and part == 5:
                        p.wait_ge(s["kp_par"], 1)
                        if c:
                            p.wait_ge(s["k_ps"], 2 * c)
                        for i, dst in enumerate((Pr, Qr)):
                            p.tensor_tensor(dst.rearrange("p (j c) r -> p j c r", j=2), chan(6, c),
                                            ramps[:, i, :].unsqueeze(1).unsqueeze(1).broadcast_to([P, 2, 16, R]), ALU.mult)\
                                .then_inc(s["kv_arg"], 1)
                stage_end("gpsimd", p)
            if "C" in stages:
                p.memset(AT[:, :], 0.0).then_inc(s["maskC"], 1)
                p.wait_ge(s["maskC"], 1)
                p.memset(AT[BIAS_ROW:BIAS_ROW + 1, :], 1.0).then_inc(s["maskC"], 1)
                p.wait_ge(s["maskC"], 2)

                def rstd_u(b):
                    ln_rstd(p, own, TB, 0, "lnC_stats", b + 1, "lnC_rstd")
                    p.wait_ge(s["lnC_rstd"], b + 1)
                    r0, r1_ = rstd[:, 0:TB], rstd[:, TB * (b + 1):TB * (b + 2)]
                    own.done(p.tensor_tensor(r1_, r0, r0, ALU.mult))
                    own.settle()
                    own.done(p.tensor_tensor(r1_, r1_, mv[:, 0:TB, 1], ALU.mult))
                    own.settle()
                    own.done(p.tensor_scalar(r1_, r1_, EPS, None, ALU.add))
                    own.settle()
                    p.tensor_tensor(r1_, r1_, neghalf[:, 0:TB], ALU.pow).then_inc(s["lnU_rstd"], 1)
                    p.wait_ge(s["lnU_rstd"], b + 1)

                rstd_u(0)
                for step in range(1, NT + 2):
                    if step == 3:
                        rstd_u(1)
                    if step <= NT:
                        n = step - 1
                        hE = Ex[:, n % 2, :].rearrange("p (h k) -> p h k", h=H1)
                        q_ = smC[:, n % 2]
                        p.wait_ge(s["ex_sum"], 4 * (n + 1))
                        own.done(p.tensor_tensor(q_[:, 1, :], q_[:, 0, :], negone[:], ALU.pow))
                        own.settle()
                        own.done(p.tensor_scalar(q_[:, 2, :], q_[:, 1, :], tmask[:, n:n + 1], None, ALU.mult))
                        own.settle()
                        p.wait_ge(s["exC"], 4 * (n + 1))
                        p.tensor_tensor(hE, hE, smC[:, n % 2, 2, :].unsqueeze(2).broadcast_to([P, H1, S2]), ALU.mult)\
                            .then_inc(s["weighted"], 1)
                    if step >= 2:
                        n = step - 2
                        p.wait_ge(s["film_sb"], n + 1)
                        p.wait_ge(s["xn_ready"], n + 1)
                        own.done(p.tensor_tensor(xn[:, n % 2, :], xn[:, n % 2, :], filmS[:, n % 2, 0:D], ALU.mult))
                        own.settle()
                        p.tensor_tensor(XIN[:, n, :], xn[:, n % 2, :], filmS[:, n % 2, D:2 * D], ALU.add)\
                            .then_inc(s["xin_ready"], 1)
                    if step <= NT:
                        n = step - 1
                        if n >= 2:
                            p.wait_ge(s["xin_ready"], n - 1)
                        p.wait_ge(s["u_ready"], n + 1)
                        p.tensor_scalar(xn[:, n % 2, :], U[:, n, :], rstd[:, TB + n:TB + n + 1], None, ALU.mult)\
                            .then_inc(s["xn_ready"], 1)
                stage_end("gpsimd", p)
            if "D" in stages:
                for i, (b, m) in enumerate(D_ORDER):
                    if b:
                        p.wait_ge(s["xf_sb"], 8 + 2 * (m + 1))
                    if i:
                        p.wait_ge(s[f"yf{D_ORDER[i - 1][0]}_ready"], D_ORDER[i - 1][1] + 1)
                    x1r, x1i = (XS0[:, m], XS1[:, m % 2])[b][:, 0, 1, :], (XS0[:, m], XS1[:, m % 2])[b][:, 1, 1, :]
                    kn = KS0n if m == 0 else KS0r[:, m, :]
                    p.tensor_tensor(pt_[:, 0, :], x1r, KS0r[:, m, :], ALU.mult).then_inc(s["pr_p"], 1)
                    p.tensor_tensor(pt_[:, 1, :], x1i, KS0i[:, m, :], ALU.mult).then_inc(s["pr_p"], 1)
                    p.tensor_tensor(pt_[:, 2, :], x1r, KS0i[:, m, :], ALU.mult).then_inc(s["pr_p"], 1)
                    p.tensor_tensor(pt_[:, 3, :], x1i, kn, ALU.mult).then_inc(s["pr_p"], 1)
                    if i in (5, 7):
                        p.wait_ge(s["xf_ps"], 16)
                        for T in range((i // 7) * TB, (i // 7 + 1) * TB):
                            p.tensor_tensor(XIN[:, T, :], XIN[:, T, :], rows[:, DSKIP, :], ALU.mult).then_inc(s["xskip"], 1)
            if "E" in stages:
                for T in range(NT):
                    p.tensor_tensor(X[:, T, :], X[:, T, :], rows[:, BNO, :], ALU.add).then_inc(s["xbE"], 1)
                    if T == 0:
                        ln_rstd(p, own, 4, 0, "lnE_stats", 1, "lnE_rstd")
                for i in range(NBLK):
                    if i + 1 < NBLK:
                        ln_rstd(p, own, 4, 0, "lnE_stats", i + 2, "lnE_rstd")
                    for t in range(4):
                        n = i * 4 + t
                        ln_rstd(p, own, 1, 8 + n % 2, "lnO_stats", n + 1, "lnO_rstd")
                        if n:
                            add_oE(n - 1)
                        if t == 1 and i and "F" in stages:
                            ln_rstd(p, own, 4, 4, "lnF_stats", i, "lnF_rstd")
                add_oE(NT - 1)
            if "F" in stages:
                ln_rstd(p, own, 4, 4, "lnF_stats", NBLK, "lnF_rstd")

        @block.vector
        def _(v):
            own = Steps(v, s["own_v"])

            def tt(o, x, y, op):
                own.done(v.tensor_tensor(o, x, y, op))

            def ts(o, x, c1, c2, op0, op1=ALU.bypass):
                own.done(v.tensor_scalar(o, x, c1, c2, op0, op1) if c2 is not None else v.tensor_scalar(o, x, c1, None, op0))

            def stt(o, x, c, y, op0, op1):
                return v.scalar_tensor_tensor(out=o, in0=x, scalar=c, in1=y, op0=op0, op1=op1)

            def bc(x, n):
                return x.unsqueeze(2).broadcast_to([x.shape[0], x.shape[1], n])

            def earlier_tiles(a, b, totals):
                own.done(v.memset(a, 0.0))
                own.settle()
                own.done(v.tensor_copy(a[:, 1:NT, :], totals[:, 0:NT - 1, :]))
                own.settle()
                shift = 1
                while shift < NT:
                    own.done(v.tensor_copy(b[:, 0:shift, :], a[:, 0:shift, :]))
                    tt(b[:, shift:NT, :], a[:, shift:NT, :], a[:, 0:NT - shift, :], ALU.add)
                    own.settle()
                    a, b, shift = b, a, 2 * shift
                return a

            def front_A():
                v.wait_ge(s["x_in0"], 16)
                ln_stats(v, own, lambda j: X[:, j, :], TB, 0, "lnA_stats")
                v.wait_ge(s["lnA_rstd"], 1)
                for t in range(TB):
                    normalise(v, zA[:, t, :], X[:, t, :], t).then_inc(s["zA_ready"], 1)

            def norm_within(step, src, dst, ready, stats, rstds, free):
                if 4 <= step < 8:
                    for j in (2 * step - 8, 2 * step - 7):
                        own.done(v.bn_stats(bstat[:, j, :], src(j)))
                elif step == 8:
                    own.settle()
                    for j in range(TB):
                        ins = v.bn_aggr(mv[:, j, :], bstat[:, j, :])
                    ins.then_inc(s[stats], 1)
                elif step in (10, 11):
                    v.wait_ge(s[rstds[0]], rstds[1])
                    v.wait_ge(s[free[0]], free[1])
                    for j in range(4 * (step - 10), 4 * (step - 10) + 4):
                        normalise(v, dst(j), src(j), j).then_inc(s[ready], 1)

            def split_bias(i):
                v.wait_ge(s["b1_in"], 48)
                x, rest = b1s[i % 2], b1s[(i + 1) % 2]
                if i == 1:
                    own.done(v.tensor_copy(b1r[32:64, :], x[32:64, :]))
                part = slice(64 if i else 0, BROWS)
                v.tensor_copy(b1r[part, :], x[part, :]).then_inc(s["b1r_ready"], 1)
                v.wait_ge(s["b1r_ready"], i + 1)
                if i < 2:
                    tt(rest[part, :], x[part, :], b1r[part, :], ALU.subtract)
                    own.settle()

            def front_B(b):
                ln_stats(v, own, lambda j: X[:, b * TB + j, :], TB, TB * b, "lnB_stats")
                v.wait_ge(s["lnB_rstd"], b + 1)
                for t in range(TB):
                    n = b * TB + t
                    normalise(v, zB[:, n, :], X[:, n, :], n).then_inc(s["zB_ready"], 1)

            front_A()
            v.wait_ge(s["consts_in"], 16 * 9)
            for i in range(2):
                for g in range(2):
                    v.wait_ge(s["kv_sb"], 2 * i + g + 1)
                    for b in range(NB):
                        v.tensor_tensor((kblk, vblk)[i][:, g, b, :].rearrange("p (h k) -> p h k", h=HG),
                                        kvT[:, i, g, b * S2:(b + 1) * S2].unsqueeze(1).broadcast_to([P, HG, S2]),
                                        bc(mask16[:], S2), ALU.mult).then_inc(s["kblk_ready"], 1)

            for b in range(NB):
                NU = 2 * TB
                for step in range(NU + 4):
                    if b == 0:
                        if step == 4:
                            v.wait_ge(s["x_in1"], 16)
                        norm_within(step, lambda j: X[:, TB + j, :], lambda j: zA[:, j, :], "zA_ready",
                                    "lnA_stats", ("lnA_rstd", 2), ("zTA_ps", TB))
                        if 13 <= step < 16:
                            split_bias(step - 13)
                    elif "B" in stages:
                        norm_within(step, lambda j: X[:, j, :], lambda j: zB[:, j, :], "zB_ready",
                                    "lnB_stats", ("lnB_rstd", 1), ("vwo_ps", 4 * NCH))
                    if step < NU:
                        u = b * NU + step
                        sv = ps[:, 2 * (u % 2):2 * (u % 2) + 2, 0:BW].rearrange("p c (h k) -> p c h k", k=S2)
                        v.wait_ge(s["scores_ready"], u + 1)
                        own.done(v.tensor_reduce(mxA[:, u % 4, :].rearrange("p (c h) -> p c h", c=2), sv, AX, ALU.max))
                        own.settle()
                        if u >= 4:
                            v.wait_ge(s["pt_ps"], u - 3)
                        v.tensor_tensor(Pb[:, u % 4, :].rearrange("p (c h k) -> p c h k", c=2, h=4), sv,
                                        mxA[:, u % 4, :].rearrange("p (c h) -> p c h", c=2).unsqueeze(3)
                                        .broadcast_to([P, 2, 4, S2]), ALU.subtract).then_inc(s["scores_read"], 1)
                    if 1 <= step <= NU:
                        u = b * NU + step - 1
                        v.wait_ge(s["probs_exp"], u + 1)
                        own.done(v.tensor_reduce(smA[:, u % 4, :], Pb[:, u % 4, :].rearrange("p (h k) -> p h k", h=HG), AX, ALU.add))
                        own.settle()
                        v.reciprocal(smA[:, u % 4, :], smA[:, u % 4, :]).then_inc(s["probs_sum"], 1)
                    if step >= 4 and step % 2 == 1:
                        T = b * TB + (step - 5) // 2
                        v.wait_ge(s["oA_ps"], 2 * T + 2)
                        v.wait_ge(s["xbA"], T + 1)
                        v.tensor_tensor(X[:, T, :], X[:, T, :], ps[:, 6 + T % 2, 0:D], ALU.add).then_inc(s["xA_done"], 1)
            stage_end("vector", v)
            if "B" in stages:
                front_B(1)

                v.wait_ge(s["lgB_ps"], NBLK)
                lgp = bank(2, NT * NE).rearrange("p (t e) -> p t e", e=NE)
                desc16 = desc8[:, 0, :].unsqueeze(1).broadcast_to([P, NT, NE])

                def red(o, x, kind):
                    own.done(v.tensor_reduce(o, x, AX, kind))
                    own.settle()

                def tts(o, x, y, kind):
                    tt(o, x, y, kind)
                    own.settle()

                def recip(o, x):
                    own.done(v.reciprocal(o, x))
                    own.settle()

                red(r1[0], lgp, ALU.max)
                v.tensor_tensor(rt[0], lgp, bc(r1[0], NE), ALU.subtract).then_inc(s["lgB_exp0"], 1)
                v.wait_ge(s["lgB_exp"], 1)
                red(r1[1], rt[1], ALU.add)
                recip(r1[2], r1[1])
                tts(rt[2], rt[1], bc(r1[2], NE), ALU.mult)
                for r in range(2):
                    red(r1[3 + r], rt[2], ALU.max)
                    tts(rt[3], rt[2], bc(r1[3 + r], NE), ALU.is_equal)
                    tts(rt[3], rt[3], desc16, ALU.mult)
                    red(r1[5], rt[3], ALU.max)
                    tts(rt[4 + r], rt[3], bc(r1[5], NE), ALU.is_equal)
                    if r == 0:
                        own.done(stt(rt[2], rt[4], -2.0, rt[2], ALU.mult, ALU.add))
                        own.settle()
                v.tensor_tensor(rt[7], rt[4], rt[5], ALU.add).then_inc(s["ohB_ready"], 1)
                tts(r1[6], r1[3], r1[4], ALU.add)
                ts(r1[6], r1[6], 1e-9, None, ALU.add)
                own.settle()
                recip(r1[7], r1[6])
                for k in range(NSEL):
                    tt(cw[:, k, :], r1[3 + k], r1[7], ALU.mult)
                own.settle()
                tt(cw[:, NSEL, :], cw[:, 0, :], cw[:, 1, :], ALU.add)
                v.wait_ge(s["cntB_ps"], 1)
                tot = bank(5, NT * NE).rearrange("p (t e) -> p t e", e=NE)
                before = earlier_tiles(rt[8], rt[9], tot)
                tts(r8[0], before[:, NT - 1, :], tot[:, NT - 1, :], ALU.add)
                tts(rt[10], before, bank(4, NT * NE).rearrange("p (t e) -> p t e", e=NE), ALU.add)
                tts(rt[10], rt[10], rt[7], ALU.subtract)
                ts(r8[1], r8[0], 1.0 / P, (P - 1.0) / P + FLOOR, ALU.mult, ALU.add)
                own.settle()
                ts(r8[1], r8[1], ROUND, -ROUND, ALU.add, ALU.add)
                own.settle()
                a_, c_, shift = r8[1], r8[2], 1
                while shift < NE:
                    own.done(v.tensor_copy(c_[:, 0:shift], a_[:, 0:shift]))
                    tts(c_[:, shift:NE], a_[:, shift:NE], a_[:, 0:NE - shift], ALU.add)
                    a_, c_, shift = c_, (r8[3] if c_ is r8[2] else r8[2]), 2 * shift
                end = a_
                tts(r8[4], end, r8[1], ALU.subtract)
                ts(r8[4], r8[4], float(P), None, ALU.mult)
                own.settle()
                tts(rt[10], rt[10], r8[4].unsqueeze(1).broadcast_to([P, NT, NE]), ALU.add)
                for k in range(NSEL):
                    tts(rt[11], rt[10], rt[4 + k], ALU.mult)
                    red(pos[:, k, :], rt[11], ALU.add)
                ts(phi, pos, 1.0 / P, FLOOR, ALU.mult, ALU.add)
                own.settle()
                ts(phi, phi, ROUND, -ROUND, ALU.add, ALU.add)
                own.settle()
                own.done(stt(plo, phi, -float(P), pos, ALU.mult, ALU.add))
                own.settle()
                for i in range(NSEL * NT // 4):
                    if i >= 2:
                        v.wait_ge(s["table_ps"], i - 1)
                    ph = bc(phi.rearrange("p k t -> p (k t)")[:, 4 * i:4 * i + 4], ST)
                    v.tensor_tensor(hieq[:, i % 2], iota[:, 0:ST].unsqueeze(1).broadcast_to([P, 4, ST]), ph, ALU.is_equal)\
                        .then_inc(s["hieq_ready"], 1)
                    pl = plo.rearrange("p k t -> p (k t)")[:, 4 * i:4 * i + 4]
                    v.tensor_tensor(lowhot[:, i % 2, :, :], iota[:].unsqueeze(1).broadcast_to([P, 4, P]), bc(pl, P),
                                    ALU.is_equal).then_inc(s["low_ready"], 1)
                tts(ends8, end.unsqueeze(1).broadcast_to([P, ST, NE]), bc(iota[:, 0:ST], NE), ALU.is_le)
                red(te, ends8, ALU.add)
                ts(te, te, NE - 1.0, None, ALU.min)
                own.settle()
                own.done(v.tensor_copy(teI[:], te))
                ts(picked[:], te[0:BROWS, :], erow[:, 0:1], None, ALU.is_equal)
                v.wait_ge(s["table_ps"], NSEL * NT // 4)
                hi, lo = ps[:, 6, 0:ST], ps[:, 6, ST:2 * ST]
                ts(idw[0], lo, -float(P), None, ALU.add)
                own.settle()
                own.done(stt(idw[1], hi, float(P), idw[0], ALU.mult, ALU.add))
                own.done(stt(idw[2], hi, 0.0, slotid[:], ALU.is_equal, ALU.mult))
                ts(idw[3], hi, NT + 0.5, -float(NT * P), ALU.is_ge, ALU.mult)
                own.settle()
                tt(idw[2], idw[2], idw[1], ALU.add)
                tt(idw[3], idw[3], idw[1], ALU.add)
                own.settle()
                own.done(v.tensor_copy(destU[:], idw[2]))
                ts(idw[3], idw[3], 0.0, None, ALU.max)
                own.settle()
                v.tensor_copy(idsU[:], idw[3]).then_inc(s["route_ready"], 1)
                v.wait_ge(s["z_out"], 16 * NBLK)

                def turns4(o, r):
                    ts(r, o, ROUND, -ROUND, ALU.add, ALU.add)
                    own.settle()
                    tt(o, o, r, ALU.subtract)
                    own.settle()
                    return stt(r, o, -1.0, o, ALU.mult, ALU.max)

                def quads(x):
                    return x.rearrange("p (j c k) -> p j c k", j=2, k=R)

                def flat(x):
                    return x.rearrange("p c k -> p (c k)")

                ARE, AIM, CRE, CIM, LOGDT, DT, AR, TURN, TH, ABS, SIN, COS, SINH = range(13)
                q = lambda i: kp[:, i, :]

                def op(o, x, y, kind):
                    tt(q(o), q(x), q(y), kind)
                    own.settle()

                def turns(o, r, x):
                    ts(r, x, ROUND, -ROUND, ALU.add, ALU.add)
                    own.settle()
                    tt(o, x, r, ALU.subtract)
                    own.settle()

                def coefficients():
                    v.wait_ge(s["kparam_in"], 16 * 6)
                    v.wait_ge(s["kp_exp"], 1)
                    v.tensor_tensor(q(AR), q(DT), q(ARE), ALU.mult).then_inc(s["kp_par"], 1)
                    op(13, DT, AIM, ALU.mult)
                    ts(q(13), q(13), 1 / (2 * math.pi), None, ALU.mult)
                    own.settle()
                    turns(q(TURN), q(14), q(13))
                    stt(q(ABS), q(TURN), -1.0, q(TURN), ALU.mult, ALU.max).then_inc(s["kp_par"], 1)

                def more_coefficients():
                    v.wait_ge(s["kp_exp"], 2)
                    ts(q(13), q(TH), -1.0, 1.0, ALU.mult, ALU.add)
                    own.settle()
                    own.done(v.reciprocal(q(14), q(13)))
                    own.settle()
                    own.done(stt(q(14), q(TH), 2.0, q(14), ALU.mult, ALU.mult))
                    own.settle()
                    ts(q(15), q(14), 1.0, None, ALU.add)
                    v.wait_ge(s["kp_exp"], 3)
                    own.done(stt(q(16), q(SINH), -2.0, q(SINH), ALU.mult, ALU.mult))
                    op(17, 14, COS, ALU.mult)
                    op(16, 16, 17, ALU.add)
                    op(17, 15, SIN, ALU.mult)
                    op(13, ARE, ARE, ALU.mult)
                    op(18, AIM, AIM, ALU.mult)
                    op(13, 13, 18, ALU.add)
                    own.done(v.reciprocal(q(13), q(13)))
                    op(14, 16, ARE, ALU.mult)
                    op(15, 17, AIM, ALU.mult)
                    op(18, 17, ARE, ALU.mult)
                    op(19, 16, AIM, ALU.mult)
                    op(14, 14, 15, ALU.add)
                    op(18, 18, 19, ALU.subtract)
                    op(14, 14, 13, ALU.mult)
                    op(18, 18, 13, ALU.mult)
                    op(16, CRE, 14, ALU.mult)
                    op(15, CIM, 18, ALU.mult)
                    op(17, CRE, 18, ALU.mult)
                    op(19, CIM, 14, ALU.mult)
                    op(16, 16, 15, ALU.subtract)
                    op(17, 17, 19, ALU.add)
                    ts(q(16), q(16), 2.0, None, ALU.mult)
                    ts(q(17), q(17), 2.0, None, ALU.mult)
                    own.settle()


                for st in range(ST + 2):
                    if st < ST:
                        u = st
                        v.wait_ge(s["sig_ready"], u + 1)
                        if u >= 2:
                            v.wait_ge(s[f"gs{u % 2}"], 16 * (u // 2))
                        v.tensor_tensor(gt[:, u % 2, :], bank(2 * (u % 2)), sig[:, u % 2, :], ALU.mult).then_inc(s["g_ready"], 1)
                    c, part = (st - KOFF) // KPARTS, (st - KOFF) % KPARTS
                    if c >= KCH:
                        continue
                    if st == 0:
                        coefficients()
                    elif st == 1:
                        more_coefficients()
                    elif part < 2:
                        ang = tk[2 * part]
                        tts(quads(ang), chan(TURN, c), ramps[:, part, :].unsqueeze(1).unsqueeze(1).broadcast_to([P, 2, 16, R]), ALU.mult)
                        turns4(ang, tk[2 * part + 1]).then_inc(s["k_trig"], 1)
                    elif part == 4:
                        v.wait_ge(s["k_sin"], 2 * c + 1)
                        v.wait_ge(s["mag_ready"], 2 * c + 2)
                        tts(flat(Pi), flat(Pr), tk[0], ALU.mult)
                        tts(flat(Pr), flat(Pr), tk[1], ALU.mult)
                    elif part == 5:
                        tt(quads(tk[0]), quads(flat(Pi)), chan(17, c), ALU.mult)
                        tt(quads(tk[1]), quads(flat(Pr)), chan(17, c), ALU.mult)
                        own.settle()
                    elif part == 6:
                        tt(quads(flat(Pr)), quads(flat(Pr)), chan(16, c), ALU.mult)
                        tt(quads(flat(Pi)), quads(flat(Pi)), chan(16, c), ALU.mult)
                        own.settle()
                    elif part == 7:
                        tt(flat(Pr), flat(Pr), tk[0], ALU.subtract)
                        v.tensor_tensor(flat(Pi), flat(Pi), tk[1], ALU.add).then_inc(s["k_used"], 1)
                    elif part == 8:
                        v.wait_ge(s["k_sin"], 2 * c + 2)
                        own.done(stt(flat(Qi), flat(Qr), -1.0, tk[2], ALU.mult, ALU.mult))
                        own.settle()
                        v.tensor_tensor(flat(Qr), flat(Qr), tk[3], ALU.mult).then_inc(s["k_used"], 1)
                stage_end("vector", v)
            if "C" in stages:
                v.wait_ge(s["wC_in"], 16 * 6)
                v.memset(VW[:], 0.0).then_inc(s["vw_zero"], 1)
                for b in range(NB):
                    ts(maskrow[0:1, b, :].rearrange("p (h k) -> p h k", h=H1),
                       vmask8[0:1, b, :].unsqueeze(1).broadcast_to([1, H1, S2]), HUGE, -HUGE, ALU.mult, ALU.add)
                ts(tmask, tmask8[:], 1.0 / H1, None, ALU.mult)
                v.wait_ge(s["prepC_sb"], 1)
                for b in range(NB):
                    v.tensor_tensor(kb1[:, b, :].rearrange("p (h k) -> p h k", h=H1),
                                    k1T[:, b * S2:(b + 1) * S2].unsqueeze(1).broadcast_to([P, H1, S2]),
                                    bc(mask32[:], S2), ALU.mult).then_inc(s["prepC_v"], 1)

                def sum_gated(T):
                    i, t = T // 4, T % 4
                    v.wait_ge(s[f"gy{i % 2}"], 32 * (i // 2 + 1))
                    if T >= 2:
                        v.wait_ge(s["sumT_ps"], T - 1)
                    ts(G[:, T % 2, :], yg[i][:, 0, t, :], cw[:, 0, T:T + 1], None, ALU.mult)
                    own.settle()
                    stt(G[:, T % 2, :], yg[i][:, 1, t, :], cw[:, 1, T:T + 1], G[:, T % 2, :], ALU.mult, ALU.add)\
                        .then_inc(s["sum_ready"], 1)


                def stats_u(n):
                    v.wait_ge(s["xB_done"], n + 1)
                    own.done(v.bn_stats(bstat[:, n % TB, :], X[:, n, :]))

                def gather_u(b):
                    own.settle()
                    for j in range(TB):
                        ins = v.bn_aggr(mv[:, j, :], bstat[:, j, :])
                    ins.then_inc(s["lnC_stats"], 1)

                def norm_u(b, tiles):
                    v.wait_ge(s["k_out"], 64)
                    v.wait_ge(s["lnC_rstd"], b + 1)
                    for t in tiles:
                        normalise(v, U[:, b * TB + t, :], X[:, b * TB + t, :], t).then_inc(s["u_ready"], 1)

                def film_rows():
                    v.wait_ge(s["bfilm_in"], 16 * NB)
                    row = VW[BIAS_ROW:BIAS_ROW + 1, :, :, :]
                    one = row[:, :, :, 0:D]
                    ts(row, row, mgate[BIAS_ROW:BIAS_ROW + 1, 0:1], None, ALU.mult)
                    own.settle()
                    ts(one, one, 1.0, None, ALU.add)
                    for b in range(NB):
                        for io in range(2):
                            v.wait_ge(s["prepC_ps"], 7 + 2 * b + io + 1)
                            ts(VW[0:S2, b, io, :], ps[0:S2, 2 * b + io, :], mgate[0:S2, 0:1], None, ALU.mult)
                            own.settle()
                            if io == 0:
                                r97 = slice(0, BIAS_ROW + 1)
                                sc, sh = VW[r97, b, 0, 0:D], VW[r97, b, 0, D:2 * D]
                                tt(xn[r97, 0, :], sc, rows[r97, BNI, :], ALU.mult)
                                own.settle()
                                tt(sh, sh, xn[r97, 0, :], ALU.add)
                                tt(sc, sc, rows[r97, GNI, :], ALU.mult)
                                own.settle()
                            v.nop().then_inc(s["prepC_v"], 1)

                for T in range(NT + 2):
                    if T == 4:
                        film_rows()
                    if T < NT:
                        sum_gated(T)
                    if T >= 2:
                        n = T - 2
                        v.wait_ge(s["oB_ps"], n + 1)
                        v.tensor_tensor(X[:, n, :], X[:, n, :], ps[:, 6 + n % 2, 0:D], ALU.add).then_inc(s["xB_done"], 1)
                        if n < TB:
                            stats_u(n)
                        if T == TB + 2:
                            gather_u(0)
                        if TB + 4 <= T < TB + 8:
                            norm_u(0, (2 * (T - TB - 4), 2 * (T - TB - 4) + 1))
                        if n == TB + 2:
                            stats_u(TB)
                            stats_u(TB + 1)
                        if n >= TB + 2:
                            stats_u(n)
                hv = lambda x: x.rearrange("p (h k) -> p h k", h=H1)
                for step in range(NT + 1):
                    if step == 3:
                        gather_u(1)
                        norm_u(1, range(TB))
                    n, par = step, step % 2
                    S, Rr = Sc[:, par, :], Rk[:, par, :]
                    if n < NT:
                        v.wait_ge(s["sC_read"], n + 1)
                        if n >= 2:
                            v.wait_ge(s["ex_sum"], 4 * (n - 1))
                    for r in range(TOPK // 8):
                        if n < NT:
                            cur = S if r == 0 else Rr
                            before = own.n
                            for h in range(H1):
                                if r:
                                    v.wait_ge(own.sem, before - H1 + h + 1)
                                own.done(v.max(top[:, par, h, 8 * r:8 * r + 8], hv(cur)[:, h, :]))
                            for h in range(H1):
                                v.wait_ge(own.sem, before + h + 1)
                                own.done(v.match_replace(hv(Rr)[:, h, :], top[:, par, h, 8 * r:8 * r + 8],
                                                         hv(cur)[:, h, :], TAKEN))
                                if r == 0 and h == H1 - 1:
                                    v.tensor_scalar(smC[:, par, 3, :], top[:, par, :, 0], -1.0, None, ALU.mult)\
                                        .then_inc(s["top_neg"], 1)
                    if n < NT:
                        v.nop().then_inc(s["top_full"], 1)
                    if 2 <= step <= 9:
                        m = step - 2
                        v.wait_ge(s["ks_sb"], m + 1)
                        stt((KSCr, KSCi)[m // 4][:, m % 4, :], (KS0r, KS0i)[m // 4][:, m % 4, :], sgn[:, 0:1],
                            ps[:, 5, D:2 * D], ALU.mult, ALU.add).then_inc(s["ks_done"], 1)
                    if n:
                        E = Ex[:, 1 - par, :]
                        own.settle()
                        v.wait_ge(s["weighted"], n)
                        own.done(stt(E, Rk[:, 1 - par, :], TAKEN / 1.5, E, ALU.is_le, ALU.mult))
                        own.settle()
                        v.tensor_reduce(a77[:, 1 - par, :], E.rearrange("p (h k) -> p k h", h=H1), AX, ALU.add)\
                            .then_inc(s["attn_ready"], 1)
                v.wait_ge(s["ks_done"], 8)
                for re, im, ny in ((KS0r, KS0i, KS0n), (KSCr, KSCi, KSCn)):
                    own.done(v.tensor_copy(ny, re[:, 0, :]))
                    own.settle()
                    own.done(v.tensor_copy(ny[0:1, :], im[0:1, 0, :]))
                    own.settle()
                    own.done(v.memset(im[0:1, 0, :], 0.0))
                stage_end("vector", v)
            if "D" in stages:
                def front_E(i):
                    ln_stats(v, own, lambda j: U[:, 4 * i + j, :], 4, 0, "lnE_stats")
                    v.wait_ge(s["lnE_rstd"], i + 1)
                    if i:
                        v.wait_ge(s["xTE_ps"], 4 * i)
                    for t in range(4):
                        normalise(v, xnE[:, t, :], U[:, 4 * i + t, :], t).then_inc(s["zE_ready"], 1)
                    for t in range(4):
                        own.done(v.tensor_tensor(U[:, 4 * i + t, :], U[:, 4 * i + t, :], rows[:, B2, :], ALU.add))
                    own.settle()

                def products(i):
                    b, m = D_ORDER[i]
                    if b:
                        v.wait_ge(s["xf_sb"], 8 + 2 * (m + 1))
                    xs = (XS0[:, m], XS1[:, m % 2])[b]
                    x0r, x0i = xs[:, 0, 0, :], xs[:, 1, 0, :]
                    k0n, kcn = (KS0n, KSCn) if m == 0 else (KS0r[:, m, :], KSCr[:, m, :])
                    Y, T = (lambda r: (YF0, YF1)[b][:, m, r, :]), (lambda r: tmpD[:, r, :])
                    for r, (kr, ki) in enumerate(((KS0r[:, m, :], KS0i[:, m, :]), (KS0i[:, m, :], k0n),
                                                  (KSCr[:, m, :], KSCi[:, m, :]), (KSCi[:, m, :], kcn))):
                        tt(Y(r), x0r, kr, ALU.mult)
                        tt(T(r), x0i, ki, ALU.mult)
                    own.settle()
                    for r in range(4):
                        tt(Y(r), Y(r), T(r), (ALU.subtract, ALU.add)[r % 2])
                    own.settle()
                    v.wait_ge(s["pr_p"], 4 * (i + 1))
                    tt(Y(2), Y(2), pt_[:, 0, :], ALU.add)
                    tt(Y(3), Y(3), pt_[:, 2, :], ALU.add)
                    own.settle()
                    tt(Y(2), Y(2), pt_[:, 1, :], ALU.subtract)
                    v.tensor_tensor(Y(3), Y(3), pt_[:, 3, :], ALU.add).then_inc(s[f"yf{b}_ready"], 1)

                for i in range(6):
                    products(i)
                for n in range(NT):
                    if n in (1, 3):
                        products(6 + n // 3)
                    if n == TB + 5 and "E" in stages:
                        own.settle()
                        front_E(0)
                    if n == TB + 2:
                        v.wait_ge(s["b1p_ps"], 1)
                        v.tensor_tensor(b1p[:], ps[:, 0, 0:HID1 // P], b1[:], ALU.add).then_inc(s["b1p_sb"], 1)
                        ts(w1[:, 0, :], w1[:, 0, :], gb_ffn[:, 0, 0:1], None, ALU.mult)
                        v.tensor_scalar(w1[:, 1, :], w1[:, 1, :], gb_ffn[:, 0, 1:2], None, ALU.mult).then_inc(s["w1s"], 1)
                    T = tmpD[:, 4 + n % 2, :]
                    v.wait_ge(s["yd_ps"], n + 1)
                    v.wait_ge(s["xskip"], n + 1)
                    tt(T, XIN[:, n, :], ps[:, 4 + n % 2, 0:D], ALU.add)
                    own.settle()
                    tt(T, T, ps[:, 6 + n % 2, 0:D], ALU.mult)
                    own.settle()
                    v.tensor_tensor(T, T, ps[:, 6 + n % 2, D:2 * D], ALU.add).then_inc(s["xt_ready"], 1)
                    v.wait_ge(s["xt_ready"], n + 1)
                    tt(U[:, n, :], U[:, n, :], T, ALU.add)
            if "E" in stages:
                def add_E(n):
                    v.wait_ge(s["oE_ps"], n + 1)
                    v.tensor_tensor(U[:, n, :], U[:, n, :], ps[:, 4 + n % 2, 0:D], ALU.add).then_inc(s["oE_read"], 1)
                    v.wait_ge(s["oE_read"], n + 1)
                    ln_stats(v, own, lambda j: U[:, n, :], 1, 8 + n % 2, "lnO_stats", bs=TB + n % 2)

                def norm_E(n):
                    v.wait_ge(s["lnO_rstd"], n + 1)
                    if n >= 2:
                        v.wait_ge(s["xE_done"], n - 1)
                    own.done(normalise(v, oE[:, n % 2, :], U[:, n, :], 8 + n % 2))
                    own.settle()
                    v.tensor_tensor(oE[:, n % 2, :], oE[:, n % 2, :], rows[:, GNO, :], ALU.mult).then_inc(s["oE_ready"], 1)

                def stats_F(i):
                    v.wait_ge(s["xE_done"], 4 * i + 4)
                    ln_stats(v, own, lambda j: X[:, 4 * i + j, :], 4, 4, "lnF_stats", bs=4)

                def norm_F(i):
                    v.wait_ge(s["lnF_rstd"], i + 1)
                    if i >= 2:
                        v.wait_ge(s["zTF_ps"], 4 * i - 4)
                    for t in range(4):
                        normalise(v, zF[:, i % 2, t, :], X[:, 4 * i + t, :], 4 + t).then_inc(s["zF_ready"], 1)

                def back_F(i, tiles=range(4)):
                    for t in tiles:
                        n = 4 * i + t
                        v.wait_ge(s["yF_ps"], n + 1)
                        tt(yF[:, n, :], ps[:, 7, 0:D], rows[:, BEXP, :], ALU.add)
                        v.tensor_copy(lg[:, n, :], ps[:, 7, D:D + NE]).then_inc(s["yF_sb"], 1)

                own.settle()
                for i in range(NBLK):
                    if i + 1 < NBLK:
                        front_E(i + 1)
                    if i >= 2 and "F" in stages:
                        back_F(i - 2)
                    for t in range(4):
                        n = 4 * i + t
                        add_E(n)
                        if n:
                            norm_E(n - 1)
                        if t == 1 and i and "F" in stages:
                            stats_F(i - 1)
                            norm_F(i - 1)
                if "F" in stages:
                    back_F(NBLK - 2, (0,))
                norm_E(NT - 1)
            if "F" in stages:
                back_F(NBLK - 2, (1,))
                stats_F(NBLK - 1)
                back_F(NBLK - 2, (2,))
                norm_F(NBLK - 1)
                back_F(NBLK - 2, (3,))
                back_F(NBLK - 1)
                v.wait_ge(s["yF_sb"], NT)
                own.done(v.tensor_reduce(r16[:, 0, :], lg, AX, ALU.max))
                own.settle()
                v.tensor_tensor(fs[:, 0], lg, bc(r16[:, 0, :], NE), ALU.subtract).then_inc(s["lgF"], 1)
                tt(oh, lg, bc(r16[:, 0, :], NE), ALU.is_equal)
                own.settle()
                tt(oh, oh, desc8[:, 0, :].unsqueeze(1).broadcast_to([P, NT, NE]), ALU.mult)
                own.settle()
                own.done(v.tensor_reduce(r16[:, 1, :], oh, AX, ALU.max))
                own.settle()
                v.tensor_tensor(oh, oh, bc(r16[:, 1, :], NE), ALU.is_equal).then_inc(s["oh_ready"], 1)
                v.wait_ge(s["lgF_exp"], 1)
                own.done(v.tensor_reduce(r16[:, 2, :], fs[:, 1], AX, ALU.add))
                own.settle()
                own.done(v.reciprocal(r16[:, 3, :], r16[:, 2, :]))
                v.wait_ge(s["cum_ps"], 1)
                before = earlier_tiles(fs[:, 2], fs[:, 3], bank(5, NT * NE).rearrange("p (t e) -> p t e", e=NE))
                tt(fs[:, 4], before, bank(4, NT * NE).rearrange("p (t e) -> p t e", e=NE), ALU.add)
                own.settle()
                own.done(stt(fs[:, 5], fs[:, 4], CAP, oh, ALU.is_le, ALU.mult))
                own.settle()
                own.done(v.tensor_reduce(r16[:, 4, :], fs[:, 5], AX, ALU.add))
                own.settle()
                tt(r16[:, 5, :], r16[:, 4, :], r16[:, 3, :], ALU.mult)
                own.settle()
                for T in range(NT):
                    stt(X[:, T, :], yF[:, T, :], r16[:, 5, T:T + 1], X[:, T, :], ALU.mult, ALU.add).then_inc(s["xF_ready"], 1)




def host_inputs(inp):
    import numpy as np

    A = {k: np.ascontiguousarray(np.asarray(x)) for k, x in inp.items()}
    o = {}
    o["x"] = A["x"]
    p = np.arange(P)
    o["c_ident"] = np.eye(P, dtype=np.float32)
    o["c_tri"] = (p[:, None] <= p[None, :]).astype(np.float32)
    o["c_mask16"] = (p[:, None] // DH0 == np.arange(HG)[None, :]).astype(np.float32)
    o["c_mask32"] = (p[:, None] // DH1 == np.arange(H1)[None, :]).astype(np.float32)
    o["c_sgn"] = (1.0 - 2.0 * (p[:, None] % 2)).astype(np.float32)
    o["c_desc8"] = np.tile(np.arange(NE, 0, -1, dtype=np.float32), (P, 4))
    o["c_ramps"] = np.tile(np.concatenate([R * np.arange(R), np.arange(R)]).astype(np.float32), (P, 1))
    N = L
    t, f = np.arange(N // 2)[:, None].astype(np.int64), np.arange(N // 2)[None, :].astype(np.int64)
    ang = 2 * np.pi * ((t * f) % N) / N
    fwd = np.concatenate([np.cos(ang), -np.sin(ang)], 1)
    fwd[:, N // 2] = 1.0 - 2.0 * (np.arange(N // 2) % 2)
    inv = fwd.T * 2.0 / N
    inv[0] /= 2
    inv[N // 2] /= 2
    o["c_dftf"], o["c_dfti"] = fwd.astype(np.float32), inv.astype(np.float32)
    wkv = A["L0_xattn_Wkv"].reshape(H0, 2, DH0, DC)
    bkv = A["L0_xattn_bkv"].reshape(H0, 2, DH0)
    o["wk0"], o["wv0"] = (wkv[:, i].reshape(D, DC).T for i in range(2))
    def columns(*v):
        return np.concatenate([x.reshape(-1, P) for x in v]).T

    o["bias0"] = columns(A["L0_xattn_bq"], bkv[:, 0].reshape(D), bkv[:, 1].reshape(D))
    o["ctxT"] = A["ctx_768"].reshape(NB * S2, DC).T
    o["wq0"], o["wo0"] = A["L0_xattn_Wq"].T, A["L0_xattn_Wo"].T
    o["wg0"], o["wof"] = A["L0_ffn_Wg"].T, A["L0_ffn_Wo"].T
    o["w1t"] = A["L0_ffn_W1"].transpose(0, 2, 1)
    o["b1e"] = A["L0_ffn_b1"]
    o["c_erow"] = np.where(p[:BROWS] % 32 < NE, p[:BROWS] % 32, -1).astype(np.float32)[:, None]
    o["c_iota"] = np.tile(np.arange(P, dtype=np.float32), (P, 1))
    o["c_pcol"] = np.arange(P, dtype=np.float32)[:, None]
    o["c_slot"] = ((NSEL * NT + 1 + np.arange(ST)[None, :]) * P + p[:, None]).astype(np.float32)
    o["wq1"] = A["L1_xattn_Wq"].T
    for n in ("Wk", "Wv", "W_film_in", "W_film_out", "W1", "W2", "b2", "D_skip", "g_norm_in", "b_norm_in",
              "g_norm_out", "b_norm_out", "log_dt"):
        o["L1_xattn_" + n] = A["L1_xattn_" + n]
    o["b_film"] = np.concatenate([A["L1_xattn_b_film_in"], A["L1_xattn_b_film_out"]])[None]
    o["L0_xattn_bo"], o["L0_ffn_bo"], o["L1_ffn_b_expert"] = A["L0_xattn_bo"], A["L0_ffn_bo"], A["L1_ffn_b_expert"]
    o["gb_ffn"] = columns(A["L1_xattn_g_ffn"], A["L1_xattn_b_ffn"])
    o["b1"] = columns(A["L1_xattn_b1"])
    o["wx"] = np.concatenate([A["L1_ffn_w_expert"], A["L1_ffn_w_gate"]], 1)
    for n, k in (("k_are", "A_re"), ("k_aim", "A_im"), ("k_cre", "C_re"), ("k_cim", "C_im")):
        o[n] = A["L1_xattn_" + k].reshape(2, P, NS).transpose(0, 2, 1).reshape(P, P)
    o["mod_gate"] = A["L1_xattn_mod_gate"].reshape(1, 1)
    o["text_mask"] = A["mask_BxS_bf1"].view(np.uint8).reshape(NT, P).T
    o["vision_mask"] = A["mask_BxS2_bf1"].view(np.uint8)
    return {k: np.ascontiguousarray(x) for k, x in o.items()}


def kernel(**inputs):
    import concourse.bacc as bacc
    from concourse.bass_utils import run_bass_kernel_spmd

    nc = bacc.Bacc("TRN2", target_bir_lowering=False, num_devices=1)
    arrays = host_inputs(inputs)
    d = {k: nc.dram_tensor(f"in_{k}", a.shape, mybir.dt.from_np(a.dtype), kind="ExternalInput").ap()
         for k, a in arrays.items()}
    out = nc.dram_tensor("out", (NB, L, D), F32, kind="ExternalOutput").ap()
    build(nc, d, out)
    r = run_bass_kernel_spmd(nc, [{f"in_{k}": a for k, a in arrays.items()}], core_ids=[0])
    return r.results[0]["out"]
```
